# Optimizing a Trainium2 kernel written in Bass

```python
import numpy as np
import jax
import jax.numpy as jnp

def _softmax(x, axis=-1):
    return jax.nn.softmax(x, axis=axis)

def _gelu(x):
    return jax.nn.gelu(x, approximate=True)

def _silu(x):
    return jax.nn.silu(x)

def _sigmoid(x):
    return jax.nn.sigmoid(x)

def _layernorm(x, axis=-1, eps=1e-05):
    m = jnp.mean(x, axis=axis, keepdims=True)
    v = jnp.var(x, axis=axis, keepdims=True)
    return (x - m) / jnp.sqrt(v + eps)

def _scatter_add(tgt, idx, src, axis=0):
    return tgt.at[idx].add(src)

def _segment_sum(src, seg, n):
    return jax.ops.segment_sum(src, seg, n)
kernel_name = 'mk_gnn_ffn_d2_gnn_r8_3bb911'

def setup_inputs(seed: int=0):
    np.random.seed(seed)
    _w = jnp.asarray

    def _rec_inputs():
        import jax
        import jax.numpy as jnp
        _gk = jax.random.key(seed)
        x = -0.0002117 + 1 * jax.random.normal(jax.random.fold_in(_gk, 1), (12500, 256), jnp.float32)
        _s = jax.random.randint(jax.random.fold_in(_gk, 2), (100000,), 0, 12500, jnp.int32)
        _d = jax.random.randint(jax.random.fold_in(_gk, 3), (100000,), 0, 12500, jnp.int32)
        _loop = jnp.arange(12500, dtype=jnp.int32)
        src = jnp.concatenate([_s, _d, _loop])
        dst = jnp.concatenate([_d, _s, _loop])
        _o = jnp.argsort(dst, stable=True)
        src = src[_o]
        dst = dst[_o]
        edge_weight = jax.random.uniform(jax.random.fold_in(_gk, 13), (212500,), jnp.float32, 0.0, 0.999999)
        return (x, src, dst, edge_weight)
    x, src, dst, edge_weight = _rec_inputs()

    def _L0_gnn_setup():
        import jax, jax.numpy as jnp
        import numpy as np
        IN_C, HID_C, LAT_C = (256, 64, 32)

        def gcn_conv(x, src, dst, ew, W, b):
            N = x.shape[0]
            deg = jax.ops.segment_sum(ew, dst, num_segments=N)
            dis = jnp.where(deg > 0, jax.lax.rsqrt(jnp.maximum(deg, 1e-12)), 0.0)
            norm = dis[src] * ew * dis[dst]
            h = x @ W
            out = jax.ops.segment_sum(norm[:, None] * h[src], dst, num_segments=N)
            return out + b

        def add_self_loops(edge_index, edge_weight, N, dtype):
            loop = jnp.arange(N, dtype=edge_index.dtype)
            src = jnp.concatenate([edge_index[0], loop])
            dst = jnp.concatenate([edge_index[1], loop])
            ew = jnp.concatenate([edge_weight, jnp.ones((N,), dtype=dtype)])
            return (src, dst, ew)
        key = jax.random.key(seed)
        ks = jax.random.split(key, 12)
        N, E = (12500, 156250)
        x = jax.random.normal(ks[0], (N, IN_C), dtype=jnp.float32)
        edge_index = jax.random.randint(ks[1], (2, E), 0, N, dtype=jnp.int64)
        edge_weight = jax.random.uniform(ks[2], (E,), dtype=jnp.float32)
        s = 0.05
        return {'x': x, 'edge_index': edge_index, 'edge_weight': edge_weight, 'W1': jax.random.normal(ks[3], (IN_C, HID_C), jnp.float32) * s, 'b1': jnp.zeros((HID_C,), jnp.float32), 'W2': jax.random.normal(ks[4], (HID_C, LAT_C), jnp.float32) * s, 'b2': jnp.zeros((LAT_C,), jnp.float32), 'Wd1': jax.random.normal(ks[5], (LAT_C, HID_C), jnp.float32) * s, 'bd1': jnp.zeros((HID_C,), jnp.float32), 'Wd2': jax.random.normal(ks[6], (HID_C, IN_C), jnp.float32) * s, 'bd2': jnp.zeros((IN_C,), jnp.float32)}
    _L0_gnn_all = _L0_gnn_setup()
    _L0_gnn_in = {k: v for k, v in _L0_gnn_all.items() if k in ('W1', 'b1', 'W2', 'b2', 'Wd1', 'bd1', 'Wd2', 'bd2')}
    del _L0_gnn_all

    def _L0_ffn_setup():
        import jax, jax.numpy as jnp
        import numpy as np
        B, A = (512, 8)
        IN, OUT = (256, 256)
        SH1, SH2 = (256, 128)
        EH1, EH2 = (128, 64)
        E, TOPK = (4, 2)

        def _shared_mlp(x, W1, b1, W2, b2, W3, b3):
            h = jax.nn.relu(x @ W1 + b1)
            h = jax.nn.relu(h @ W2 + b2)
            return h @ W3 + b3

        def _experts_mlp(x, eW1, eb1, eW2, eb2, eW3, eb3):
            h = jax.nn.relu(jnp.einsum('baf,efh->ebah', x, eW1) + eb1[:, None, None, :])
            h = jax.nn.relu(jnp.einsum('ebah,ehg->ebag', h, eW2) + eb2[:, None, None, :])
            o = jnp.einsum('ebag,ego->ebao', h, eW3) + eb3[:, None, None, :]
            return jnp.moveaxis(o, 0, -1)
        key = jax.random.key(seed)
        ks = jax.random.split(key, 16)
        s = 0.05
        return {'x': jax.random.normal(ks[0], (B, A, IN), jnp.float32), 'sW1': jax.random.normal(ks[1], (IN, SH1), jnp.float32) * s, 'sb1': jnp.zeros((SH1,), jnp.float32), 'sW2': jax.random.normal(ks[2], (SH1, SH2), jnp.float32) * s, 'sb2': jnp.zeros((SH2,), jnp.float32), 'sW3': jax.random.normal(ks[3], (SH2, OUT), jnp.float32) * s, 'sb3': jnp.zeros((OUT,), jnp.float32), 'eW1': jax.random.normal(ks[4], (E, IN, EH1), jnp.float32) * s, 'eb1': jnp.zeros((E, EH1), jnp.float32), 'eW2': jax.random.normal(ks[5], (E, EH1, EH2), jnp.float32) * s, 'eb2': jnp.zeros((E, EH2), jnp.float32), 'eW3': jax.random.normal(ks[6], (E, EH2, OUT), jnp.float32) * s, 'eb3': jnp.zeros((E, OUT), jnp.float32), 'gW': jax.random.normal(ks[7], (IN, E), jnp.float32) * s, 'gb': jnp.zeros((E,), jnp.float32)}
    _L0_ffn_all = _L0_ffn_setup()
    _L0_ffn_in = {k: v for k, v in _L0_ffn_all.items() if k in ('sW1', 'sb1', 'sW2', 'sb2', 'sW3', 'sb3', 'eW1', 'eb1', 'eW2', 'eb2', 'eW3', 'eb3', 'gW', 'gb')}
    del _L0_ffn_all

    def _L1_gnn_setup():
        import jax, jax.numpy as jnp
        import numpy as np
        N, E, IN_DIM, H, D = (6250, 100000, 256, 8, 32)
        ALPHA = 0.2
        key = jax.random.key(seed)
        ks = jax.random.split(key, 6)
        feat = jax.random.normal(ks[0], (N, IN_DIM), dtype=jnp.float32)
        src = jax.random.randint(ks[1], (E,), 0, N, dtype=jnp.int32)
        dst = jax.random.randint(ks[2], (E,), 0, N, dtype=jnp.int32)
        W = jax.random.normal(ks[3], (IN_DIM, H * D), dtype=jnp.float32) * 0.05
        attn_l = jax.random.normal(ks[4], (H, D), dtype=jnp.float32)
        attn_r = jax.random.normal(ks[5], (H, D), dtype=jnp.float32)
        return {'feat': feat, 'src': src, 'dst': dst, 'W': W, 'attn_l': attn_l, 'attn_r': attn_r}
    _L1_gnn_all = _L1_gnn_setup()
    _L1_gnn_in = {k: v for k, v in _L1_gnn_all.items() if k in ('W', 'attn_l', 'attn_r')}
    del _L1_gnn_all

    def _L1_ffn_setup():
        import jax, jax.numpy as jnp
        import numpy as np
        B, S, D = (8, 512, 256)
        H = 4 * D
        CAPACITY = 0.5
        key = jax.random.key(seed)
        ks = jax.random.split(key, 6)
        x = jax.random.normal(ks[0], (B, S, D), dtype=jnp.float32)
        attention_mask = jnp.zeros((B, 1, 1, S), dtype=jnp.float32)
        wr = jax.random.normal(ks[1], (D, 1), dtype=jnp.float32) * 0.02
        br = jnp.zeros((1,), dtype=jnp.float32)
        w1 = jax.random.normal(ks[2], (D, H), dtype=jnp.float32) * 0.02
        b1 = jnp.zeros((H,), dtype=jnp.float32)
        w2 = jax.random.normal(ks[3], (H, D), dtype=jnp.float32) * 0.02
        b2 = jnp.zeros((D,), dtype=jnp.float32)
        return {'x': x, 'attention_mask': attention_mask, 'wr': wr, 'br': br, 'w1': w1, 'b1': b1, 'w2': w2, 'b2': b2}
    _L1_ffn_all = _L1_ffn_setup()
    _L1_ffn_in = {k: v for k, v in _L1_ffn_all.items() if k in ('attention_mask', 'wr', 'br', 'w1', 'b1', 'w2', 'b2')}
    del _L1_ffn_all
    return {'x': x, 'src': src, 'dst': dst, 'edge_weight': edge_weight, 'L0_gnn_W1': _L0_gnn_in['W1'], 'L0_gnn_b1': _L0_gnn_in['b1'], 'L0_gnn_W2': _L0_gnn_in['W2'], 'L0_gnn_b2': _L0_gnn_in['b2'], 'L0_gnn_Wd1': _L0_gnn_in['Wd1'], 'L0_gnn_bd1': _L0_gnn_in['bd1'], 'L0_gnn_Wd2': _L0_gnn_in['Wd2'], 'L0_gnn_bd2': _L0_gnn_in['bd2'], 'L0_ffn_sW1': _L0_ffn_in['sW1'], 'L0_ffn_sb1': _L0_ffn_in['sb1'], 'L0_ffn_sW2': _L0_ffn_in['sW2'], 'L0_ffn_sb2': _L0_ffn_in['sb2'], 'L0_ffn_sW3': _L0_ffn_in['sW3'], 'L0_ffn_sb3': _L0_ffn_in['sb3'], 'L0_ffn_eW1': _L0_ffn_in['eW1'], 'L0_ffn_eb1': _L0_ffn_in['eb1'], 'L0_ffn_eW2': _L0_ffn_in['eW2'], 'L0_ffn_eb2': _L0_ffn_in['eb2'], 'L0_ffn_eW3': _L0_ffn_in['eW3'], 'L0_ffn_eb3': _L0_ffn_in['eb3'], 'L0_ffn_gW': _L0_ffn_in['gW'], 'L0_ffn_gb': _L0_ffn_in['gb'], 'L1_gnn_W': _L1_gnn_in['W'], 'L1_gnn_attn_l': _L1_gnn_in['attn_l'], 'L1_gnn_attn_r': _L1_gnn_in['attn_r'], 'L1_ffn_attention_mask': _L1_ffn_in['attention_mask'], 'L1_ffn_wr': _L1_ffn_in['wr'], 'L1_ffn_br': _L1_ffn_in['br'], 'L1_ffn_w1': _L1_ffn_in['w1'], 'L1_ffn_b1': _L1_ffn_in['b1'], 'L1_ffn_w2': _L1_ffn_in['w2'], 'L1_ffn_b2': _L1_ffn_in['b2']}

def reference(x, src, dst, edge_weight, L0_gnn_W1, L0_gnn_b1, L0_gnn_W2, L0_gnn_b2, L0_gnn_Wd1, L0_gnn_bd1, L0_gnn_Wd2, L0_gnn_bd2, L0_ffn_sW1, L0_ffn_sb1, L0_ffn_sW2, L0_ffn_sb2, L0_ffn_sW3, L0_ffn_sb3, L0_ffn_eW1, L0_ffn_eb1, L0_ffn_eW2, L0_ffn_eb2, L0_ffn_eW3, L0_ffn_eb3, L0_ffn_gW, L0_ffn_gb, L1_gnn_W, L1_gnn_attn_l, L1_gnn_attn_r, L1_ffn_attention_mask, L1_ffn_wr, L1_ffn_br, L1_ffn_w1, L1_ffn_b1, L1_ffn_w2, L1_ffn_b2):
    import jax
    import jax.numpy as jnp

    def _L0_gnn_ref(x, edge_index, edge_weight, W1, b1, W2, b2, Wd1, bd1, Wd2, bd2):
        import jax, jax.numpy as jnp
        import numpy as np
        IN_C, HID_C, LAT_C = (256, 64, 32)

        def gcn_conv(x, src, dst, ew, W, b):
            N = x.shape[0]
            deg = jax.ops.segment_sum(ew, dst, num_segments=N)
            dis = jnp.where(deg > 0, jax.lax.rsqrt(jnp.maximum(deg, 1e-12)), 0.0)
            norm = dis[src] * ew * dis[dst]
            h = x @ W
            out = jax.ops.segment_sum(norm[:, None] * h[src], dst, num_segments=N)
            return out + b

        def add_self_loops(edge_index, edge_weight, N, dtype):
            loop = jnp.arange(N, dtype=edge_index.dtype)
            src = jnp.concatenate([edge_index[0], loop])
            dst = jnp.concatenate([edge_index[1], loop])
            ew = jnp.concatenate([edge_weight, jnp.ones((N,), dtype=dtype)])
            return (src, dst, ew)
        N = x.shape[0]
        src, dst, ew = add_self_loops(edge_index, edge_weight, N, x.dtype)
        h = jax.nn.relu(gcn_conv(x, src, dst, ew, W1, b1))
        z = jax.nn.relu(gcn_conv(h, src, dst, ew, W2, b2))
        d = jax.nn.relu(z @ Wd1 + bd1)
        x_hat = jax.nn.sigmoid(d @ Wd2 + bd2)
        return x_hat

    def _L0_ffn_ref(x, sW1, sb1, sW2, sb2, sW3, sb3, eW1, eb1, eW2, eb2, eW3, eb3, gW, gb):
        import jax, jax.numpy as jnp
        import numpy as np
        B, A = (512, 8)
        IN, OUT = (256, 256)
        SH1, SH2 = (256, 128)
        EH1, EH2 = (128, 64)
        E, TOPK = (4, 2)

        def _shared_mlp(x, W1, b1, W2, b2, W3, b3):
            h = jax.nn.relu(x @ W1 + b1)
            h = jax.nn.relu(h @ W2 + b2)
            return h @ W3 + b3

        def _experts_mlp(x, eW1, eb1, eW2, eb2, eW3, eb3):
            h = jax.nn.relu(jnp.einsum('baf,efh->ebah', x, eW1) + eb1[:, None, None, :])
            h = jax.nn.relu(jnp.einsum('ebah,ehg->ebag', h, eW2) + eb2[:, None, None, :])
            o = jnp.einsum('ebag,ego->ebao', h, eW3) + eb3[:, None, None, :]
            return jnp.moveaxis(o, 0, -1)
        all_out = _experts_mlp(x, eW1, eb1, eW2, eb2, eW3, eb3)
        shared = _shared_mlp(x, sW1, sb1, sW2, sb2, sW3, sb3)
        gates = jax.nn.softmax(x @ gW + gb, axis=-1)
        topv, topi = jax.lax.top_k(gates, TOPK)
        topw = jax.nn.softmax(topv, axis=-1)
        sel = jnp.take_along_axis(all_out, topi[:, :, None, :], axis=-1)
        gated = jnp.sum(sel * topw[:, :, None, :], axis=-1)
        return shared + gated

    def _L1_gnn_ref(feat, src, dst, W, attn_l, attn_r):
        import jax, jax.numpy as jnp
        import numpy as np
        N, E, IN_DIM, H, D = (6250, 100000, 256, 8, 32)
        ALPHA = 0.2
        n = feat.shape[0]
        ft = (feat @ W).reshape(n, H, D)
        a1 = jnp.einsum('nhd,hd->nh', ft, attn_l)
        a2 = jnp.einsum('nhd,hd->nh', ft, attn_r)
        e = jax.nn.leaky_relu(a1[src] + a2[dst], negative_slope=ALPHA)
        m = jax.ops.segment_max(e, dst, num_segments=n)
        ex = jnp.exp(e - m[dst])
        s = jax.ops.segment_sum(ex, dst, num_segments=n)
        alpha = ex / s[dst]
        msg = ft[src] * alpha[:, :, None]
        out = jax.ops.segment_sum(msg, dst, num_segments=n)
        return jax.nn.elu(out.reshape(n, H * D))

    def _L1_ffn_ref(x, attention_mask, wr, br, w1, b1, w2, b2):
        import jax, jax.numpy as jnp
        import numpy as np
        B, S, D = (8, 512, 256)
        H = 4 * D
        CAPACITY = 0.5
        b, s, d = x.shape
        weights = (jnp.einsum('bsd,do->bso', x, wr) + br)[..., 0]
        k = max(1, int(CAPACITY * s))
        kk = k - 1 if k > 1 else 1
        _, idx = jax.lax.top_k(weights, k)
        sel_idx = idx[:, :kk]
        sel = jnp.take_along_axis(x, sel_idx[:, :, None], axis=1)
        h = jax.nn.gelu(jnp.einsum('bkd,dh->bkh', sel, w1) + b1)
        y = jnp.einsum('bkh,hd->bkd', h, w2) + b2
        w_sel = jnp.take_along_axis(weights, sel_idx, axis=1)
        y = y * w_sel[..., None]
        batch_idx = jnp.arange(b)[:, None]
        processed = jnp.zeros_like(x).at[batch_idx, sel_idx].set(y)
        return processed + x
    edge_index = jnp.stack([src, dst])
    x = x + _L0_gnn_ref(_layernorm(x, axis=-1), edge_index, edge_weight, L0_gnn_W1, L0_gnn_b1, L0_gnn_W2, L0_gnn_b2, L0_gnn_Wd1, L0_gnn_bd1, L0_gnn_Wd2, L0_gnn_bd2)
    x = x + _L0_ffn_ref(_layernorm(x, axis=-1)[None], L0_ffn_sW1, L0_ffn_sb1, L0_ffn_sW2, L0_ffn_sb2, L0_ffn_sW3, L0_ffn_sb3, L0_ffn_eW1, L0_ffn_eb1, L0_ffn_eW2, L0_ffn_eb2, L0_ffn_eW3, L0_ffn_eb3, L0_ffn_gW, L0_ffn_gb)[0]
    x = x + _L1_gnn_ref(_layernorm(x, axis=-1), src, dst, L1_gnn_W, L1_gnn_attn_l, L1_gnn_attn_r)
    x = x + _L1_ffn_ref(_layernorm(x, axis=-1)[None], L1_ffn_attention_mask, L1_ffn_wr, L1_ffn_br, L1_ffn_w1, L1_ffn_b1, L1_ffn_w2, L1_ffn_b2)[0]
    return x

_drawn_inputs = setup_inputs


def setup_inputs(seed=0):
    import zlib

    import numpy as np

    out = dict(_drawn_inputs(seed))
    spreads = {'L0_gnn_b1': (0.0, 0.8),
     'L0_gnn_b2': (0.0, 0.8),
     'L0_gnn_bd1': (0.0, 0.704),
     'L0_gnn_bd2': (0.0, 0.293),
     'L0_ffn_sb1': (0.0, 0.35),
     'L0_ffn_sb2': (0.0, 0.1),
     'L0_ffn_sb3': (0.0, 0.1),
     'L0_ffn_eb1': (0.0, 0.8),
     'L0_ffn_eb2': (0.0, 0.425),
     'L0_ffn_eb3': (0.0, 0.1),
     'L0_ffn_gb': (0.0, 0.28),
     'L1_ffn_b1': (0.0, 0.8),
     'L1_ffn_b2': (0.0, 0.8)}
    factors = {'edge_weight': 8.0,
     'L0_gnn_W1': 8.0,
     'L0_gnn_W2': 8.0,
     'L0_gnn_Wd1': 8.0,
     'L0_gnn_Wd2': 4.907,
     'L1_ffn_wr': 4.503,
     'L1_ffn_w1': 5.56,
     'L1_ffn_w2': 5.192}
    for name, (base, spread) in spreads.items():
        noise = np.random.default_rng([zlib.crc32(name.encode()), seed]).standard_normal(out[name].shape)
        drawn = base * np.exp(spread * noise) if base else spread * noise
        out[name] = jnp.asarray(drawn.astype(out[name].dtype))
    for name, factor in factors.items():
        out[name] = (out[name] * factor).astype(out[name].dtype)
    return out
```

```python
import numpy as np
import concourse.bass as bass
from concourse import mybir
from contextlib import ExitStack

F32, BF16, I32 = mybir.dt.float32, mybir.dt.bfloat16, mybir.dt.int32
ALU, ACT, AX = mybir.AluOpType, mybir.ActivationFunctionType, mybir.AxisListType

P = 128
N, D = 12500, 256
E = 212500
TILES = -(-E // P)
TB = -(-TILES // P)
GW = 4
WIN = -(-N // P)
GROUPS = -(-WIN // GW)
W = GROUPS * GW
NP = W * P
SECT = 8
UNROLL = 4 * SECT
BLOCKS = -(-(TILES + WIN - 1) // UNROLL)
STEPS = BLOCKS * UNROLL
QUAD = 4
WBITS = 7
WORD_MAX = (1 << WBITS * QUAD) - 1
assert W <= 1 << WBITS
SB = -(-STEPS // P)
SP = SB * P
assert (STEPS - 1) - (TILES - 1) < W
CH1, CH2 = 64, 32
HEADS, HD = 8, 32
FT = D + HEADS
HID = 4 * D
TOP = N // 2 - 1
CHUNKS = 16
ROUNDS = STEPS // CHUNKS
LEN = ROUNDS * P
HALVES = UNROLL // CHUNKS
assert STEPS % CHUNKS == 0 and CHUNKS * HEADS == P and ROUNDS % HALVES == 0
EPS = 1e-5
FAR = 1 << 20
NEG = -1e38
ds = bass.ds


class Own:

    def __init__(self, eng, sem):
        self.eng, self.sem, self.base, self.k = eng, sem, 0, 0

    def did(self, ins):
        ins.then_inc(self.sem, 1)
        self.k += 1

    def wait(self, back=0):
        self.eng.wait_ge(self.sem, self.base + self.k - back)

    def then(self, ins):
        self.did(ins)
        self.wait()

    def start(self):
        return self.base + self.k

    def turn(self, start, it, per):
        self.base, self.k = start + it * per, 0

    def finish(self, start, times, per):
        assert self.k == per, (self.k, per)
        self.base, self.k = start + times * per, 0


def over_groups(eng, body):
    with eng.Fori(0, GROUPS // 2) as gg:
        for h in range(2):
            body(gg * 2 + h, h)
    body(GROUPS - 1, 0)


class Phase:

    def __init__(self, nc, name):
        self.nc, self.name, self.stack, self.sems = nc, name, ExitStack(), []

    def __enter__(self):
        return self

    def __exit__(self, kind, *a):
        self.stack.__exit__(kind, *a)
        if kind is None:
            self.nc.clear_and_free_semaphores(self.sems)
            self.nc.all_engine_barrier()

    def sb(self, name, shape, dt=F32):
        return self.stack.enter_context(self.nc.sbuf_tensor(f"{self.name}_{name}", shape, dt))

    def ps(self, name, shape, dt=F32):
        return self.stack.enter_context(self.nc.psum_tensor(f"{self.name}_{name}", shape, dt))

    def sem(self, name):
        self.sems.append(self.nc.alloc_semaphore(f"{self.name}_{name}"))
        return self.sems[-1]

    def block(self):
        return self.stack.enter_context(self.nc.Block())


def bcast(ap, dims):
    return ap.to_broadcast(dims)


def constants(nc, K):
    with Phase(nc, "const") as ph:
        made, fixed = ph.sem("made"), ph.sem("fixed")
        tmp = ph.sb("tmp", [P, P])
        block = ph.block()

        @block.gpsimd
        def _(pool):
            pool.memset(K.ident[:, :], 0.0).then_inc(made, 1)
            pool.iota(K.iota[:, :], [[1, P]], base=0, channel_multiplier=0,
                      allow_small_or_imprecise_dtypes=True).then_inc(made, 1)
            pool.iota(K.real[:, :], [[P, W]], base=0, channel_multiplier=1,
                      allow_small_or_imprecise_dtypes=True).then_inc(made, 1)
            pool.wait_ge(made, 3)
            pool.affine_select(out=K.ident[:, :], in_=K.ident[:, :], compare_op=ALU.not_equal, fill=1.0, base=0,
                               pattern=[[-1, P]], channel_multiplier=1).then_inc(made, 1)

        @block.vector
        def _(dve):
            dve.memset(K.ones[:, :], 1.0)
            dve.memset(K.onesb[:, :], 1.0)
            dve.wait_ge(made, 4)
            dve.tensor_copy(K.iotab[:, :], K.iota[:, :])
            dve.tensor_copy(K.identb[:, :], K.ident[:, :])
            dve.tensor_scalar(K.real[:, :], K.real[:, :], float(N), None, ALU.is_lt)


def schedule(nc, K, src, dst, ew):
    with Phase(nc, "sch") as ph:
        dti, sti = ph.sb("dti", [P, TB, P], I32), ph.sb("sti", [P, TB, P], I32)
        et = ph.sb("et", [P, TB, 3 * P])
        stepf = ph.sb("stepf", [P, SP])
        pos = ph.sb("pos", [P, SB])
        lb = ph.sb("lb", [P, TB], I32)
        ct = ph.sb("ct", [P, TB])
        cmp_ = ph.sb("cmp", [P, TB, SP], BF16)
        tcol = ph.sb("tcol", [P, SB], I32)
        nwin = ph.sb("nwin", [P, SB])
        se = ph.sb("se", [P, SB, 3 * P])
        key = ph.sb("key", [P, SB, P])
        val = ph.sb("val", [P, SB, P])
        front = ph.sb("front", [1, P])
        wrow = ph.sb("wrow", [1, SP], I32)
        shifted = ph.sb("shifted", [1, SP // QUAD], I32)
        CH = SP // 4
        rowp = ph.ps("rowp", [1, 4, 512])
        colp = ph.ps("colp", [P, 512])
        tp = [ph.ps(f"tp{i}", [P, 3 * P]) for i in range(3)]
        padded, loaded = ph.sem("padded"), ph.sem("loaded")
        iotas, chain = ph.sem("iotas"), ph.sem("chain")
        et_ready, et_stored = ph.sem("et_ready"), ph.sem("et_stored")
        cmp_done, row_done, col_done = ph.sem("cmp_done"), ph.sem("row_done"), ph.sem("col_done")
        tile_ready, gathered = ph.sem("tile_ready"), ph.sem("gathered")
        rel_ready, tp_done, tp_free, key_ready, stored = (ph.sem(x) for x in
                                                          ("rel_ready", "tp_done", "tp_free", "key_ready", "stored"))
        block = ph.block()
        full = (TB - 1) * P * P
        rest = (E - full) // P
        last = E - full - rest * P
        arrays = [(dst, dti), (src, sti), (ew, et[:, :, 2 * P:3 * P])]

        @block.sync
        def _(sp):
            for a, t in arrays:
                sp.dma_start(t[:, 0:TB - 1, :], a[0:full].rearrange("(b p e) -> p b e", b=TB - 1, p=P)
                             ).then_inc(loaded, 16)
            sp.wait_ge(padded, 1)
            for a, t in arrays:
                sp.dma_start(t[0:rest, TB - 1, :], a[full:full + rest * P].rearrange("(p e) -> p e", e=P)
                             ).then_inc(loaded, 16)
                sp.dma_start(t[rest:rest + 1, TB - 1, 0:last],
                             a[E - last:E].rearrange("(p e) -> p e", p=1)).then_inc(loaded, 16)
            sp.wait_ge(et_ready, 1)
            sp.dma_start(K.etd.rearrange("(b p) f -> p b f", p=P), et[:, :, :]).then_inc(et_stored, 16)
            sp.wait_ge(key_ready, 1)
            sp.dma_start(K.keyd[0:P].rearrange("(p e) -> p e", p=1), front[:, :]).then_inc(stored, 16)
            sp.dma_start(K.keyd[P:P + SP * P].rearrange("(b p e) -> p b e", p=P, e=P), key[:, :, :]
                         ).then_inc(stored, 16)
            sp.wait_ge(stored, 32)

        @block.gpsimd
        def _(pool):
            pool.iota(stepf[:, :], [[1, SP]], base=0, channel_multiplier=0,
                      allow_small_or_imprecise_dtypes=True).then_inc(iotas, 1)
            pool.iota(pos[:, :], [[P, SB]], base=0, channel_multiplier=1,
                      allow_small_or_imprecise_dtypes=True).then_inc(iotas, 1)
            pool.wait_ge(et_stored, 16)
            pool.wait_ge(tile_ready, 1)
            for i in range(SB):
                pool.indirect_dma_start(out=se[:, i, :], out_offset=None, in_=K.etd,
                                        in_offset=bass.IndirectOffsetOnAxis(ap=tcol[:, i:i + 1], axis=0)
                                        ).then_inc(gathered, 16)

        @block.vector
        def _(dve):
            own = Own(dve, chain)
            own.did(dve.memset(dti[:, TB - 1, :], FAR))
            own.did(dve.memset(sti[:, TB - 1, :], 0))
            own.did(dve.memset(front[:, :], -7.0))
            own.then(dve.memset(et[:, TB - 1, 2 * P:3 * P], 0.0))
            dve.sem_inc(padded, 1)
            dve.wait_ge(loaded, 16 * 9)
            own.did(dve.tensor_copy(et[:, :, 0:P], sti[:, :, :]))
            own.did(dve.tensor_copy(et[:, :, P:2 * P], dti[:, :, :]))
            own.then(dve.tensor_scalar(lb[:, :], dti[:, :, P - 1], 7, None, ALU.logical_shift_right))
            dve.sem_inc(et_ready, 1)
            own.then(dve.tensor_copy(ct[:, :], lb[:, :]))
            dve.wait_ge(iotas, 2)
            own.then(dve.tensor_tensor(ct[:, :], ct[:, :], pos[:, 0:TB], ALU.add))
            for b in range(TB):
                dve.tensor_scalar(cmp_[:, b, :], stepf[:, :], ct[:, b:b + 1], None, ALU.is_gt).then_inc(cmp_done, 1)
            dve.wait_ge(col_done, 1)
            dve.tensor_copy(tcol[:, :], colp[:, 0:SB]).then_inc(tile_ready, 1)
            own.then(dve.tensor_tensor(K.wcol[:, :], pos[:, :], colp[:, 0:SB], ALU.subtract))
            own.did(dve.tensor_scalar(nwin[:, :], K.wcol[:, :], float(-P), None, ALU.mult))
            dve.wait_ge(row_done, 1)
            for c in range(4):
                own.did(dve.tensor_tensor(wrow[0:1, c * CH:(c + 1) * CH], stepf[0:1, c * CH:(c + 1) * CH],
                                          rowp[0:1, c, 0:CH], ALU.subtract))
            own.wait()
            quads = wrow[0:1, :].rearrange("a (q i) -> a q i", i=QUAD)
            own.then(dve.tensor_copy(K.wpack[0:1, :], quads[:, :, 0]))
            for i in range(1, QUAD):
                own.then(dve.tensor_scalar(shifted[0:1, :], quads[:, :, i], WBITS * i, None, ALU.logical_shift_left))
                own.then(dve.tensor_tensor(K.wpack[0:1, :], K.wpack[0:1, :], shifted[0:1, :], ALU.bitwise_or))
            quads = wrow[0:1, 0:STEPS].rearrange("a (q i j) -> a q i j", i=QUAD, j=ROUNDS)
            words = lambda t: t[0:1, 0:STEPS // QUAD].rearrange("a (q j) -> a q j", j=ROUNDS)
            own.then(dve.tensor_copy(words(K.wround), quads[:, :, 0, :]))
            for i in range(1, QUAD):
                own.then(dve.tensor_scalar(words(shifted), quads[:, :, i, :], WBITS * i, None, ALU.logical_shift_left))
                own.then(dve.tensor_tensor(words(K.wround), words(K.wround), words(shifted), ALU.bitwise_or))
            dve.wait_ge(gathered, 16 * SB)
            own.then(dve.tensor_scalar(key[:, :, :], se[:, :, P:2 * P], 1.0, None, ALU.add))
            own.then(dve.tensor_tensor(se[:, :, P:2 * P], se[:, :, P:2 * P],
                                       nwin[:, :].unsqueeze(2).to_broadcast([P, SB, P]), ALU.add))
            dve.sem_inc(rel_ready, 1)
            own.then(dve.tensor_scalar(val[:, :, :], se[:, :, P:2 * P], 0.0, None, ALU.is_ge))
            own.then(dve.tensor_tensor(key[:, :, :], key[:, :, :], val[:, :, :], ALU.mult))
            own.then(dve.tensor_scalar(val[:, :, :], se[:, :, P:2 * P], float(P), None, ALU.is_lt))
            dve.tensor_tensor(key[:, :, :], key[:, :, :], val[:, :, :], ALU.mult).then_inc(key_ready, 1)

        @block.tensor
        def _(pe):
            pe.wait_ge(cmp_done, TB)
            for i in range(SB):
                for b in range(TB):
                    last_mm = nc.tensor.matmul(colp[:, i:i + 1], cmp_[:, b, i * P:(i + 1) * P], K.onesb[:, 0:1],
                                               start=(b == 0), stop=(b == TB - 1))
            last_mm.then_inc(col_done, 1)
            for c in range(4):
                for b in range(TB):
                    last_mm = nc.tensor.matmul(rowp[0:1, c, 0:CH], K.onesb[:, 0:1], cmp_[:, b, c * CH:(c + 1) * CH],
                                               start=(b == 0), stop=(b == TB - 1))
            last_mm.then_inc(row_done, 1)
            pe.wait_ge(rel_ready, 1)
            for i in range(SB):
                if i >= 3:
                    pe.wait_ge(tp_free, i - 2)
                for a in range(3):
                    last_mm = nc.tensor.transpose(tp[i % 3][:, a * P:(a + 1) * P], se[:, i, a * P:(a + 1) * P],
                                                  K.ident[:, :])
                last_mm.then_inc(tp_done, 1)

        @block.scalar
        def _(act):
            for i in range(SB):
                act.wait_ge(tp_done, i + 1)
                src_t = tp[i % 3][:, :].rearrange("p (a s) -> p a s", a=3)
                act.activation(K.edges[:, :, i * P:(i + 1) * P], src_t, ACT.Copy).then_inc(tp_free, 1)


def degrees(nc, K):
    U, NB = UNROLL // 2, 2 * BLOCKS
    with Phase(nc, "deg") as ph:
        ew3 = ph.sb("ew3", [P, SP, 3], BF16)
        r = ph.sb("r", [P, SP])
        sel = ph.sb("sel", [P, U, P], BF16)
        parts = ph.sb("parts", [P, SP, 3])
        part = ph.sb("part", [P, SP])
        partT = ph.sb("partT", [P, SB, P])
        woh = ph.sb("woh", [P, SB, W])
        deg = ph.sb("deg", [P, W])
        pos_ = ph.sb("pos", [P, W])
        pd = [ph.ps(f"pd{i}", [P, U * 3]) for i in range(2)]
        pt = [ph.ps(f"pt{i}", [P, P]) for i in range(2)]
        pw = ph.ps("pw", [P, W])
        split, chain = ph.sem("split"), ph.sem("chain")
        sel_free, sel_ready, part_free = (ph.sem(x) for x in ("sel_free", "sel_ready", "part_free"))
        summed, turned, turn_kept, deg_done, rooted = (ph.sem(x) for x in ("summed", "turned", "turn_kept", "deg_done",
                                                                  "rooted"))
        safe = ph.sem("safe")
        block = ph.block()
        HALF = U // 2

        @block.vector
        def _(dve):
            own = Own(dve, chain)
            ewr = K.edges[:, 2, :]
            own.then(dve.tensor_copy(ew3[:, :, 0], ewr))
            own.then(dve.tensor_tensor(r[:, :], ewr, ew3[:, :, 0], ALU.subtract))
            own.then(dve.tensor_copy(ew3[:, :, 1], r[:, :]))
            own.then(dve.tensor_tensor(r[:, :], r[:, :], ew3[:, :, 1], ALU.subtract))
            own.did(dve.memset(parts[:, STEPS:SP, :], 0.0))
            dve.tensor_copy(ew3[:, :, 2], r[:, :]).then_inc(split, 1)
            with dve.Fori(0, NB) as b:
                for k in range(U):
                    if k % HALF == 0:
                        dve.wait_ge(sel_free, b * U + k + HALF)
                    ins = dve.tensor_scalar(sel[:, k, :], K.iotab[:, :], K.edges[:, 1, ds(b * U + k, 1)], None,
                                            ALU.is_equal)
                    if k % HALF == HALF - 1:
                        ins.then_inc(sel_ready, 1)
            for i in range(SB):
                ins = dve.tensor_scalar(woh[:, i, :], K.iotaw[:, :], K.wcol[:, i:i + 1], None, ALU.is_equal)
                own.did(ins)
            dve.wait_ge(part_free, NB + 2)
            own.wait()
            dve.tensor_reduce(part[:, :], parts[:, :, :], AX.X, ALU.add).then_inc(summed, 1)
            dve.wait_ge(deg_done, 1)
            own.then(dve.tensor_scalar(deg[:, :], pw[:, :], 1.0, None, ALU.add))
            own.did(dve.tensor_scalar(pos_[:, :], deg[:, :], 0.0, None, ALU.is_gt))
            dve.tensor_scalar(deg[:, :], deg[:, :], 1e-12, None, ALU.max).then_inc(safe, 1)
            dve.wait_ge(rooted, 1)
            own.then(dve.reciprocal(deg[:, :], deg[:, :]))
            dve.tensor_tensor(K.dis[:, :], deg[:, :], pos_[:, :], ALU.mult)

        @block.tensor
        def _(pe):
            pe.sem_inc(sel_free, U)
            pe.sem_inc(part_free, 2)
            pe.wait_ge(split, 1)
            with pe.Fori(0, NB // 2) as bb:
                for h in range(2):
                    b = bb * 2 + h
                    pe.wait_ge(part_free, b + 1)
                    for k in range(U):
                        if k % HALF == 0:
                            pe.wait_ge(sel_ready, b * 2 + k // HALF + 1)
                        ins = nc.tensor.matmul(pd[h][:, k * 3:k * 3 + 3], sel[:, k, :],
                                               ew3[:, ds(b * U + k, 1), :].rearrange("p a c -> p (a c)"),
                                               start=True, stop=True)
                        if k % HALF == HALF - 1:
                            ins.then_inc(sel_free, HALF)
            pe.wait_ge(summed, 1)
            for i in range(SB):
                if i >= 2:
                    pe.wait_ge(turn_kept, i - 1)
                nc.tensor.transpose(pt[i % 2][:, :], part[:, i * P:(i + 1) * P], K.ident[:, :]).then_inc(turned, 1)
            pe.wait_ge(turn_kept, SB)
            for i in range(SB):
                ins = nc.tensor.matmul(pw[:, :], partT[:, i, :], woh[:, i, :], start=(i == 0), stop=(i == SB - 1))
            ins.then_inc(deg_done, 1)

        @block.scalar
        def _(act):
            with act.Fori(0, NB // 2) as bb:
                for h in range(2):
                    b = bb * 2 + h
                    act.wait_ge(sel_free, b * U + 2 * U)
                    act.activation(parts[:, ds(b * U, U), :],
                                   pd[h][:, :].rearrange("p (s c) -> p s c", c=3), ACT.Copy).then_inc(part_free, 1)
            for i in range(SB):
                act.wait_ge(turned, i + 1)
                act.activation(partT[:, i, :], pt[i % 2][:, :], ACT.Copy).then_inc(turn_kept, 1)
            act.wait_ge(safe, 1)
            act.activation(deg[:, :], deg[:, :], ACT.Sqrt).then_inc(rooted, 1)


def gate(eng, token):
    eng.sem_inc(token, 1)


def stats_of(dve, own, K, st, x, w0, n, token):
    for i in range(n):
        own.did(dve.bn_stats(st[:, i, 0:6], x[:, i, :]))
    own.wait()
    gate(dve, token)
    for i in range(n):
        own.did(dve.bn_aggr(st[:, i, 6:8], st[:, i, 0:6]))
    own.wait()
    own.did(dve.tensor_copy(K.mv[:, ds(w0, n), :], st[:, 0:n, 6:8]))


def rstd_of(nc, K):
    with Phase(nc, f"rstd{nc.next_id()}") as ph:
        eps, eps_ready, rooted, chain = ph.sb("eps", [P, 1]), ph.sem("eps_ready"), ph.sem("rooted"), ph.sem("chain")
        block = ph.block()

        @block.scalar
        def _(act):
            act.wait_ge(eps_ready, 1)
            act.activation(K.rs[:, :], K.mv[:, :, 1], ACT.Sqrt, bias=eps[:, 0:1]).then_inc(rooted, 1)

        @block.vector
        def _(dve):
            own = Own(dve, chain)
            dve.memset(eps[:, :], EPS).then_inc(eps_ready, 1)
            dve.wait_ge(rooted, 1)
            own.then(dve.reciprocal(K.rs[:, :], K.rs[:, :]))
            own.then(dve.tensor_tensor(K.nmr[:, :], K.mv[:, :, 0], K.rs[:, :], ALU.mult))
            dve.tensor_scalar(K.nmr[:, :], K.nmr[:, :], -1.0, None, ALU.mult)


def load_x(nc, K, x):
    PIECE = 16
    pieces = [(w, min(PIECE, N // P - w)) for w in range(0, N // P, PIECE)]
    tail = N - N // P * P
    with Phase(nc, "load") as ph:
        st = ph.sb("st", [P, GW, 8])
        zeroed, chain, passed = ph.sem("zeroed"), ph.sem("chain"), ph.sem("passed")
        loaded = [ph.sem(f"loaded{i}") for i in range(len(pieces) + 1)]
        block = ph.block()

        @block.sync
        def _(sp):
            for (w, n), s in zip(pieces, loaded):
                sp.dma_start(K.x[:, w:w + n, :], x[w * P:(w + n) * P, :].rearrange("(w p) c -> p w c", p=P)
                             ).then_inc(s, 16)
            sp.wait_ge(zeroed, 1)
            sp.dma_start(K.x[0:tail, N // P, :], x[N // P * P:N, :]).then_inc(loaded[-1], 16)

        @block.vector
        def _(dve):
            own = Own(dve, chain)
            own.then(dve.memset(K.x[:, N // P:W, :], 0.0))
            dve.sem_inc(zeroed, 1)
            for (w, n), s in zip(pieces + [(N // P, W - N // P)], loaded):
                dve.wait_ge(s, 16)
                for i in range(0, n, GW):
                    m = min(GW, n - i)
                    stats_of(dve, own, K, st, K.x[:, w + i:w + i + m, :], w + i, m, passed)
                    own.wait()
    rstd_of(nc, K)


def normal(act, K, xn, g, done):
    for i in range(GW):
        w = g * GW + i
        ins = act.activation(xn[:, i, :], K.x[:, ds(w, 1), :].rearrange("p a c -> p (a c)"), ACT.Identity,
                             bias=K.nmr[:, ds(w, 1)], scale=K.rs[:, ds(w, 1)])
    ins.then_inc(done, 1)


def turn_rows(nc, K, xn, pt, done):
    for i in range(GW):
        for k in range(D // P):
            ins = nc.tensor.transpose(pt[:, k, i * P:(i + 1) * P], xn[:, i, k * P:(k + 1) * P], K.ident[:, :])
    ins.then_inc(done, 1)


def first_table(nc, K, w1):
    with Phase(nc, "t1") as ph:
        wt = ph.sb("wt", [P, 2, CH1])
        xn = [ph.sb(f"xn{i}", [P, GW, D]) for i in range(2)]
        xt = [ph.sb(f"xt{i}", [P, 2, GW * P]) for i in range(2)]
        px = [ph.ps(f"px{i}", [P, 2, GW * P]) for i in range(2)]
        pm = [ph.ps(f"pm{i}", [P, GW, CH1]) for i in range(2)]
        loaded, normed, turned, kept, mm_done, scaled, stored = (
            ph.sem(x) for x in ("loaded", "normed", "turned", "kept", "mm_done", "scaled", "stored"))
        block = ph.block()

        @block.scalar
        def _(act):
            act.sem_inc(turned, 2)
            def body(g, h):
                act.wait_ge(turned, g + 1)
                normal(act, K, xn[h], g, normed)
            over_groups(act, body)

        @block.tensor
        def _(pe):
            pe.wait_ge(loaded, 16)
            pe.sem_inc(kept, 2)
            pe.sem_inc(scaled, 2)
            def body(g, h):
                pe.wait_ge(normed, g + 1)
                pe.wait_ge(kept, g + 1)
                turn_rows(nc, K, xn[h], px[h], turned)
                pe.wait_ge(kept, g + 3)
                pe.wait_ge(scaled, g + 1)
                for i in range(GW):
                    for k in range(2):
                        ins = nc.tensor.matmul(pm[h][:, i, :], xt[h][:, k, i * P:(i + 1) * P], wt[:, k, :],
                                               start=(k == 0), stop=(k == 1))
                ins.then_inc(mm_done, 1)
            over_groups(pe, body)

        @block.vector
        def _(dve):
            def body(g, h):
                dve.wait_ge(turned, g + 3)
                dve.tensor_copy(xt[h][:, :, :], px[h][:, :, :]).then_inc(kept, 1)
                dve.wait_ge(mm_done, g + 1)
                for i in range(GW):
                    w = g * GW + i
                    ins = dve.tensor_scalar(K.acc1[:, ds(w, 1), :].rearrange("p a c -> p (a c)"), pm[h][:, i, :],
                                            K.dis[:, ds(w, 1)], None, ALU.mult)
                ins.then_inc(scaled, 1)
            over_groups(dve, body)

        @block.sync
        def _(sp):
            sp.dma_start(wt[:, :, :], w1.rearrange("(k p) c -> p k c", p=P)).then_inc(loaded, 16)
            sp.wait_ge(scaled, GROUPS + 2)
            sp.dma_start(K.t1.rearrange("(w p) c -> p w c", p=P), K.acc1[:, :, :]).then_inc(stored, 16)
            sp.wait_ge(stored, 16)


def take_indices(nc, K, act, idx, slots_used, idx_ready, column):
    with act.Fori(0, BLOCKS) as b:
        for j in range(UNROLL // SECT):
            act.wait_ge(slots_used, b * UNROLL + (j + 1) * SECT)
            act.activation(idx[:, j * SECT:(j + 1) * SECT], column(b, j), ACT.Copy).then_inc(idx_ready, 1)


def gather_rows(pool, table, idx, dest, idx_ready, taken, gathered):
    with pool.Fori(0, BLOCKS) as b:
        for j in range(UNROLL // SECT):
            pool.wait_ge(idx_ready, b * (UNROLL // SECT) + j + 1)
            pool.sem_inc(taken, 1)
            for k in range(j * SECT, (j + 1) * SECT):
                pool.indirect_dma_start(out=dest(k), out_offset=None, in_=table,
                                        in_offset=bass.IndirectOffsetOnAxis(ap=idx[:, k:k + 1], axis=0)
                                        ).then_inc(gathered[k], 16)


def unpack(nc, word):
    return [nc.s_assert_within((word >> (WBITS * i)) & ((1 << WBITS) - 1), 0, W - 1,
                               skip_runtime_bounds_check_because="a step less a tile is a window")
            for i in range(QUAD)]


def quad_windows(eng, K, quad):
    return unpack(eng.bass, eng.value_load(K.wpack[0:1, ds(quad, 1)], min_val=0, max_val=WORD_MAX))


def graph_sum(nc, K, name, table, acc, C):
    RING = 4
    with Phase(nc, name) as ph:
        idx = ph.sb("idx", [P, UNROLL], I32)
        rows = ph.sb("rows", [P, UNROLL, C])
        sel = ph.sb("sel", [P, RING * QUAD, P])
        pm = [ph.ps(f"pm{i}", [P, QUAD, C]) for i in range(RING)]
        gathered = [ph.sem(f"gathered{k}") for k in range(UNROLL)]
        idx_ready, taken, sel_ready, mm_done, added = (
            ph.sem(x) for x in ("idx_ready", "taken", "sel_ready", "mm_done", "added"))
        block = ph.block()

        @block.scalar
        def _(act):
            take_indices(nc, K, act, idx, mm_done, idx_ready,
                         lambda b, j: K.edges[:, 0, ds(b * UNROLL + j * SECT, SECT)])

        @block.gpsimd
        def _(pool):
            gather_rows(pool, table, idx, lambda k: rows[:, k, :], idx_ready, taken, gathered)

        @block.vector
        def _(dve):
            def select(q, first):
                for i in range(QUAD):
                    s = first + i
                    ins = dve.tensor_scalar(sel[:, q * QUAD + i, :], K.iota[:, :], K.edges[:, 1, ds(s, 1)],
                                            K.edges[:, 2, ds(s, 1)], ALU.is_equal, ALU.mult)
                ins.then_inc(sel_ready, 1)

            dve.sem_inc(added, 1)
            select(0, 0)
            with dve.Fori(0, BLOCKS) as b:
                for q in range(UNROLL // QUAD):
                    s = b * UNROLL + q * QUAD
                    ws = quad_windows(dve, K, b * (UNROLL // QUAD) + q)
                    select((q + 1) % RING, s + QUAD)
                    dve.wait_ge(mm_done, UNROLL + s + QUAD)
                    for i in range(QUAD):
                        a = acc[:, ds(ws[i], 1), :].rearrange("p a c -> p (a c)")
                        dve.wait_ge(added, s + i + 1)
                        dve.tensor_tensor(a, a, pm[q % RING][:, i, :], ALU.add).then_inc(added, 1)

        @block.tensor
        def _(pe):
            pe.sem_inc(mm_done, UNROLL)
            with pe.Fori(0, BLOCKS) as b:
                for q in range(UNROLL // QUAD):
                    pe.wait_ge(sel_ready, b * (UNROLL // QUAD) + q + 1)
                    for i in range(QUAD):
                        k = q * QUAD + i
                        pe.wait_ge(gathered[k], b * 16 + 16)
                        ins = nc.tensor.matmul(pm[q % RING][:, i, :], sel[:, (q % RING) * QUAD + i, :],
                                               rows[:, k, :], start=True, stop=True)
                    ins.then_inc(mm_done, QUAD)


def row_bias(sp, tile, bias, sem):
    sp.dma_start(tile, bias.unsqueeze(0).to_broadcast([P, bias.shape[0]])).then_inc(sem, 16)


def scaled_sums(dve, K, u, acc, bias, g):
    for i in range(GW):
        w = g * GW + i
        ins = dve.scalar_tensor_tensor(out=u[:, i, :], in0=acc[:, ds(w, 1), :].rearrange("p a c -> p (a c)"),
                                       scalar=K.dis[:, ds(w, 1)], in1=bias, op0=ALU.mult, op1=ALU.add)
    return ins


def second_table(nc, K, b1, w2):
    with Phase(nc, "t2") as ph:
        wt, bt = ph.sb("wt", [CH1, CH2]), ph.sb("bt", [P, CH1])
        u = [ph.sb(f"u{i}", [P, GW, CH1]) for i in range(2)]
        v = [ph.sb(f"v{i}", [P, GW, CH1]) for i in range(2)]
        ht = [ph.sb(f"ht{i}", [CH1, GW * P]) for i in range(2)]
        pt = [ph.ps(f"pt{i}", [CH1, GW * P]) for i in range(2)]
        pm = [ph.ps(f"pm{i}", [P, GW, CH2]) for i in range(2)]
        loaded, summed, relued, turned, kept, mm_done, scaled, stored, passed = (
            ph.sem(x) for x in ("loaded", "summed", "relued", "turned", "kept", "mm_done", "scaled", "stored",
                                "passed"))
        block = ph.block()

        @block.vector
        def _(dve):
            dve.wait_ge(loaded, 32)
            dve.sem_inc(scaled, 2)
            scaled_sums(dve, K, u[0], K.acc1, bt[:, :], 0).then_inc(summed, 1)

            def body(g, h):
                if not (isinstance(g, int) and g == GROUPS - 1):
                    dve.wait_ge(relued, g + 2)
                    scaled_sums(dve, K, u[1 - h], K.acc1, bt[:, :], g + 1).then_inc(summed, 1)
                dve.wait_ge(mm_done, g + 3)
                for i in range(GW):
                    w = g * GW + i
                    ins = dve.tensor_scalar(K.acc2[:, ds(w, 1), :].rearrange("p a c -> p (a c)"), pm[h][:, i, :],
                                            K.dis[:, ds(w, 1)], None, ALU.mult)
                ins.then_inc(scaled, 1)
            over_groups(dve, body)

        @block.scalar
        def _(act):
            act.sem_inc(turned, 2)
            act.sem_inc(mm_done, 2)
            act.sem_inc(relued, 1)

            def body(g, h):
                act.wait_ge(summed, g + 1)
                act.wait_ge(turned, g + 1)
                act.activation(v[h][:, :, :], u[h][:, :, :], ACT.Relu).then_inc(relued, 1)
                act.wait_ge(turned, g + 3)
                act.wait_ge(mm_done, g + 1)
                act.activation(ht[h][:, :], pt[h][:, :], ACT.Copy).then_inc(kept, 1)
            over_groups(act, body)

        @block.tensor
        def _(pe):
            pe.wait_ge(loaded, 32)

            def body(g, h):
                pe.wait_ge(relued, g + 2)
                gate(pe, passed)
                for i in range(GW):
                    ins = nc.tensor.transpose(pt[h][:, i * P:(i + 1) * P], v[h][:, i, :], K.ident[:, :])
                ins.then_inc(turned, 1)
                pe.wait_ge(kept, g + 1)
                pe.wait_ge(scaled, g + 1)
                for i in range(GW):
                    ins = nc.tensor.matmul(pm[h][:, i, :], ht[h][:, i * P:(i + 1) * P], wt[:, :], start=True, stop=True)
                ins.then_inc(mm_done, 1)
            over_groups(pe, body)

        @block.sync
        def _(sp):
            sp.dma_start(wt[:, :], w2).then_inc(loaded, 16)
            row_bias(sp, bt[:, :], b1, loaded)
            sp.wait_ge(scaled, GROUPS + 2)
            sp.dma_start(K.t2.rearrange("(w p) c -> p w c", p=P), K.acc2[:, :, :]).then_inc(stored, 16)
            sp.wait_ge(stored, 16)


def decode(nc, K, b2, wd1, bd1, wd2, bd2):
    with Phase(nc, "dec") as ph:
        bt = ph.sb("bt", [P, CH2])
        w1t, b1t = ph.sb("w1t", [CH2, CH1]), ph.sb("b1t", [CH1, 1])
        w2t = ph.sb("w2t", [CH1 + 1, D])
        u = [ph.sb(f"u{i}", [P, GW, CH2]) for i in range(2)]
        v = [ph.sb(f"v{i}", [P, GW, CH2]) for i in range(2)]
        zt = ph.sb("zt", [CH2, GW * P])
        dt = ph.sb("dt", [CH1 + 1, GW * P])
        sg = [ph.sb(f"sg{i}", [P, GW, D]) for i in range(2)]
        st = ph.sb("st", [P, GW, 8])
        pt = ph.ps("pt", [CH2, GW * P])
        pd = ph.ps("pd", [CH1, GW * P])
        po = [ph.ps(f"po{i}", [P, GW, D]) for i in range(2)]
        loaded, summed, relued, turned, z_kept, d_done, d_kept, o_done, sig_done, used, ones_set, chain, passed = (
            ph.sem(x) for x in ("loaded", "summed", "relued", "turned", "z_kept", "d_done", "d_kept", "o_done",
                                "sig_done", "used", "ones_set", "chain", "passed"))
        block = ph.block()

        @block.sync
        def _(sp):
            row_bias(sp, bt[:, :], b2, loaded)
            sp.dma_start(w1t[:, :], wd1).then_inc(loaded, 16)
            sp.dma_start(b1t[:, :], bd1.unsqueeze(1)).then_inc(loaded, 16)
            sp.dma_start(w2t[0:CH1, :], wd2).then_inc(loaded, 16)
            sp.dma_start(w2t[CH1:CH1 + 1, :], bd2.unsqueeze(0)).then_inc(loaded, 16)

        @block.vector
        def _(dve):
            own = Own(dve, chain)
            dve.memset(dt[CH1:CH1 + 1, :], 1.0).then_inc(ones_set, 1)
            dve.wait_ge(loaded, 16 * 5)
            scaled_sums(dve, K, u[0], K.acc2, bt[:, :], 0).then_inc(summed, 1)
            start = own.start()

            def body(g, h):
                own.turn(start, g, 2 * GW + 2)
                if not (isinstance(g, int) and g == GROUPS - 1):
                    dve.wait_ge(relued, g + 2)
                    scaled_sums(dve, K, u[1 - h], K.acc2, bt[:, :], g + 1).then_inc(summed, 1)
                dve.wait_ge(sig_done, g + 1)
                xg = K.x[:, ds(g * GW, GW), :]
                ins = dve.tensor_tensor(xg, xg, sg[h][:, :, :], ALU.add)
                own.then(ins)
                dve.sem_inc(used, 1)
                stats_of(dve, own, K, st, xg, g * GW, GW, passed)
            over_groups(dve, body)

        @block.scalar
        def _(act):
            act.sem_inc(used, 2)
            act.sem_inc(relued, 1)
            act.wait_ge(ones_set, 1)
            act.wait_ge(loaded, 16 * 5)

            def body(g, h):
                act.wait_ge(summed, g + 1)
                act.activation(v[h][:, :, :], u[h][:, :, :], ACT.Relu).then_inc(relued, 1)
                act.wait_ge(turned, g + 1)
                act.activation(zt[:, :], pt[:, :], ACT.Copy).then_inc(z_kept, 1)
                act.wait_ge(d_done, g + 1)
                act.activation(dt[0:CH1, :], pd[:, :], ACT.Relu, bias=b1t[:, 0:1]).then_inc(d_kept, 1)
                act.wait_ge(o_done, g + 1)
                act.wait_ge(used, g + 1)
                act.activation(sg[h][:, :, :], po[h][:, :, :], ACT.Sigmoid).then_inc(sig_done, 1)
            over_groups(act, body)

        @block.tensor
        def _(pe):
            pe.wait_ge(loaded, 16 * 5)

            def body(g, h):
                pe.wait_ge(relued, g + 2)
                gate(pe, passed)
                for i in range(GW):
                    ins = nc.tensor.transpose(pt[:, i * P:(i + 1) * P], v[h][:, i, :], K.ident[:, :])
                ins.then_inc(turned, 1)
                pe.wait_ge(z_kept, g + 1)
                nc.tensor.matmul(pd[:, :], w1t[:, :], zt[:, :], start=True, stop=True).then_inc(d_done, 1)
                pe.wait_ge(d_kept, g + 1)
                for i in range(GW):
                    ins = nc.tensor.matmul(po[h][:, i, :], dt[:, i * P:(i + 1) * P], w2t[:, :], start=True, stop=True)
                ins.then_inc(o_done, 1)
            over_groups(pe, body)
    rstd_of(nc, K)


FFN_RING = 9


def mixture(nc, K, a):
    NE, EH1, EH2, SH1, SH2 = 4, 128, 64, 256, 128
    PAIRS = NE * EH2 // P
    with Phase(nc, "moe") as ph:
        sw1, sw2 = ph.sb("sw1", [P, 2, SH1]), ph.sb("sw2", [P, 2, SH2])
        sw3 = ph.sb("sw3", [P, D])
        ew1, ew2 = ph.sb("ew1", [P, NE, 2, EH1]), ph.sb("ew2", [P, NE, EH2])
        ew3 = ph.sb("ew3", [P, PAIRS, D])
        gw, gb = ph.sb("gw", [P, 2, NE]), ph.sb("gb", [P, NE])
        sb1, sb2 = ph.sb("sb1", [P, 2]), ph.sb("sb2", [P, 1])
        eb1 = ph.sb("eb1", [P, NE])
        eb2 = ph.sb("eb2", [1, NE * EH2])
        b3 = ph.sb("b3", [NE + 1, D])
        low = ph.sb("low", [P, NE, NE])
        xn = [ph.sb(f"xn{i}", [P, GW, D]) for i in range(2)]
        xt = [ph.sb(f"xt{i}", [P, 2, GW * P]) for i in range(2)]
        h1 = ph.sb("h1", [P, 2 + NE, GW * P])
        h2 = ph.sb("h2", [P, GW * P])
        e2 = ph.sb("e2", [P, GW, PAIRS * P])
        e2t = ph.sb("e2t", [P, PAIRS, GW * P])
        lg, ex, gt = (ph.sb(x, [P, GW, NE]) for x in ("lg", "ex", "gt"))
        rank, dif = (ph.sb(x, [P, GW, NE]) for x in ("rank", "dif"))
        gtx = ph.sb("gtx", [P, GW, NE, NE])
        eqx = ph.sb("eqx", [P, GW, NE, NE])
        mx, sm = ph.sb("mx", [P, GW]), ph.sb("sm", [P, GW])
        g5 = ph.sb("g5", [P, GW, NE + 1])
        g5t = ph.sb("g5t", [NE + 1, GW * P])
        st = ph.sb("st", [P, GW, 8])
        px = ph.ps("px", [P, 2, GW * P])
        ring = [ph.ps(f"ring{i}", [P, GW * P]) for i in range(2)]
        pe2 = ph.ps("pe2", [P, GW, PAIRS * P])
        po = ph.ps("po", [P, GW, D])
        names = ("loaded normed turned xt_kept lg_kept h1_kept h2_kept ring_done shifted exped gated exped2 weighed "
                 "e2_done e2_ready e2_turned e2t_kept g5t_kept out_done added chain passed").split()
        S = {x: ph.sem(x) for x in names}
        block = ph.block()
        LOADS = 15

        @block.sync
        def _(sp):
            def put(t, src_):
                sp.dma_start(t, src_).then_inc(S["loaded"], 16)
            put(sw1[:, :, :], a["L0_ffn_sW1"].rearrange("(k p) c -> p k c", p=P))
            put(gw[:, :, :], a["L0_ffn_gW"].rearrange("(k p) c -> p k c", p=P))
            put(ew1[:, :, :, :], a["L0_ffn_eW1"].rearrange("e (k p) c -> p e k c", p=P))
            put(sw2[:, :, :], a["L0_ffn_sW2"].rearrange("(k p) c -> p k c", p=P))
            put(sw3[:, :], a["L0_ffn_sW3"])
            put(ew2[:, :, :], a["L0_ffn_eW2"].rearrange("e p c -> p e c"))
            put(ew3[:, :, :], a["L0_ffn_eW3"].rearrange("(q e) h c -> (e h) q c", e=2))
            put(gb[:, :], a["L0_ffn_gb"].unsqueeze(0).to_broadcast([P, NE]))
            put(sb1[:, :], a["L0_ffn_sb1"].rearrange("(k p) -> p k", p=P))
            put(sb2[:, :], a["L0_ffn_sb2"].unsqueeze(1))
            put(eb1[:, :], a["L0_ffn_eb1"].rearrange("e p -> p e"))
            put(eb2[:, :], a["L0_ffn_eb2"].rearrange("(a e) c -> a (e c)", a=1))
            put(b3[0:NE, :], a["L0_ffn_eb3"])
            put(b3[NE:NE + 1, :], a["L0_ffn_sb3"].unsqueeze(0))

        last = lambda g: isinstance(g, int) and g == GROUPS - 1

        @block.tensor
        def _(pe):
            mm = nc.tensor.matmul
            pe.wait_ge(S["loaded"], 16 * (LOADS - 1))
            pe.wait_ge(S["normed"], 1)
            turn_rows(nc, K, xn[0], px, S["turned"])

            for x in ("e2_done", "out_done"):
                pe.sem_inc(S[x], 1)

            def body(g, h):
                at = lambda i: ring[(FFN_RING * h + i) % 2]
                free = lambda i: [("g5t_kept", g + 1), ("lg_kept", g + 1)][i]
                pe.wait_ge(S["xt_kept"], g + 1)
                pe.wait_ge(S["h2_kept"], g + 1)
                for i in range(GW):
                    for k in range(2):
                        ins = mm(at(0)[:, i * NE:(i + 1) * NE], xt[h][:, k, i * P:(i + 1) * P], gw[:, k, :],
                                 start=(k == 0), stop=(k == 1))
                ins.then_inc(S["ring_done"], 1)
                for m in range(2 + NE):
                    if m == 0:
                        pe.wait_ge(S["g5t_kept"], g + 1)
                    elif m == 1:
                        pe.wait_ge(S["lg_kept"], g + 1)
                    else:
                        pe.wait_ge(S["h1_kept"], g * (2 + NE) + m - 1)
                    for k in range(2):
                        wt = sw1[:, k, m * P:(m + 1) * P] if m < 2 else ew1[:, m - 2, k, :]
                        ins = mm(at(1 + m)[:, :], wt, xt[h][:, k, :], start=(k == 0), stop=(k == 1))
                    ins.then_inc(S["ring_done"], 1)
                if not last(g):
                    pe.wait_ge(S["normed"], g + 2)
                    pe.wait_ge(S["e2t_kept"], g + 1)
                    turn_rows(nc, K, xn[1 - h], px, S["turned"])
                pe.wait_ge(S["h1_kept"], g * (2 + NE) + 5)
                for k in range(2):
                    ins = mm(at(7)[:, :], sw2[:, k, :], h1[:, k, :], start=(k == 0), stop=(k == 1))
                ins.then_inc(S["ring_done"], 1)
                pe.wait_ge(S["h1_kept"], (g + 1) * (2 + NE))
                pe.wait_ge(S["e2_ready"], g + 1)
                for i in range(GW):
                    mm(pe2[:, i, :], K.ones[0:1, :], eb2[0:1, :], start=True, stop=False)
                    for e in range(NE):
                        ins = mm(pe2[:, i, e * EH2:(e + 1) * EH2], h1[:, 2 + e, i * P:(i + 1) * P], ew2[:, e, :],
                                 start=False, stop=(e == NE - 1))
                ins.then_inc(S["e2_done"], 1)
                pe.wait_ge(S["weighed"], g + 1)
                for i in range(GW):
                    ins = nc.tensor.transpose(at(8)[0:NE + 1, i * P:(i + 1) * P], g5[:, i, :], K.ident[:, :])
                ins.then_inc(S["ring_done"], 1)
                pe.wait_ge(S["e2_ready"], g + 2)
                if not last(g):
                    pe.wait_ge(S["xt_kept"], g + 2)
                for i in range(GW):
                    for q in range(PAIRS):
                        ins = nc.tensor.transpose(px[:, q, i * P:(i + 1) * P], e2[:, i, q * P:(q + 1) * P],
                                                  K.ident[:, :])
                ins.then_inc(S["e2_turned"], 1)
                pe.wait_ge(S["h2_kept"], g + 2)
                pe.wait_ge(S["added"], g + 1)
                pe.wait_ge(S["g5t_kept"], g + 2)
                pe.wait_ge(S["e2t_kept"], g + 2)
                for i in range(GW):
                    c = slice(i * P, (i + 1) * P)
                    mm(po[:, i, :], h2[:, c], sw3[:, :], start=True, stop=False)
                    mm(po[:, i, :], g5t[:, c], b3[:, :], start=False, stop=False)
                    for q in range(PAIRS):
                        ins = mm(po[:, i, :], e2t[:, q, c], ew3[:, q, :], start=False, stop=(q == PAIRS - 1))
                ins.then_inc(S["out_done"], 1)
            over_groups(pe, body)

        @block.scalar
        def _(act):
            for x in ("h2_kept", "g5t_kept", "e2t_kept"):
                act.sem_inc(S[x], 1)
            act.wait_ge(S["loaded"], 16 * (LOADS - 1))
            normal(act, K, xn[0], 0, S["normed"])

            def body(g, h):
                at = lambda i: ring[(FFN_RING * h + i) % 2]
                if not last(g):
                    act.wait_ge(S["turned"], g + 1)
                    normal(act, K, xn[1 - h], g + 1, S["normed"])
                act.wait_ge(S["ring_done"], g * FFN_RING + 1)
                act.wait_ge(S["shifted"], g + 1)
                act.activation(lg[:, :, :], at(0)[:, 0:GW * NE].rearrange("p (w e) -> p w e", e=NE), ACT.Copy
                               ).then_inc(S["lg_kept"], 1)
                for m in range(2 + NE):
                    act.wait_ge(S["ring_done"], g * FFN_RING + 2 + m)
                    bias = sb1[:, m:m + 1] if m < 2 else eb1[:, m - 2:m - 1]
                    if m == 0:
                        act.wait_ge(S["e2_done"], g + 1)
                    act.activation(h1[:, m, :], at(1 + m)[:, :], ACT.Relu, bias=bias).then_inc(S["h1_kept"], 1)
                act.wait_ge(S["shifted"], g + 2)
                act.activation(ex[:, :, :], gt[:, :, :], ACT.Exp).then_inc(S["exped"], 1)
                act.wait_ge(S["ring_done"], g * FFN_RING + 8)
                act.wait_ge(S["out_done"], g + 1)
                act.activation(h2[:, :], at(7)[:, :], ACT.Relu, bias=sb2[:, 0:1]).then_inc(S["h2_kept"], 1)
                act.wait_ge(S["gated"], g + 1)
                act.activation(ex[:, :, :], dif[:, :, :], ACT.Exp).then_inc(S["exped2"], 1)
                act.wait_ge(S["ring_done"], g * FFN_RING + 9)
                act.activation(g5t[:, :], at(8)[0:NE + 1, :], ACT.Copy).then_inc(S["g5t_kept"], 1)
                act.wait_ge(S["e2_turned"], g + 1)
                act.activation(e2t[:, :, :], px[:, :, :], ACT.Relu).then_inc(S["e2t_kept"], 1)
            over_groups(act, body)

        @block.vector
        def _(dve):
            own = Own(dve, S["chain"])
            tt, X4 = dve.tensor_tensor, [P, GW, NE]
            own.did(dve.memset(low[:, :, :], 0.0))
            own.then(dve.memset(g5[:, :, NE:NE + 1], 1.0))
            for e in range(1, NE):
                own.did(dve.memset(low[:, e, 0:e], 1.0))
            own.wait()
            for x in ("shifted", "added", "e2_ready"):
                dve.sem_inc(S[x], 1)
            start = own.start()
            over = lambda t: t.unsqueeze(2).to_broadcast(X4)
            X5 = [P, GW, NE, NE]

            def columns(g, h):
                dve.wait_ge(S["turned"], g + 1)
                dve.tensor_copy(xt[h][:, :, :], px[:, :, :]).then_inc(S["xt_kept"], 1)

            columns(0, 0)

            def body(g, h):
                own.turn(start, g, 18 + 2 * GW + 1)
                dve.wait_ge(S["lg_kept"], g + 1)
                own.then(tt(gt[:, :, :], lg[:, :, :], gb[:, :].unsqueeze(1).to_broadcast(X4), ALU.add))
                own.then(dve.tensor_reduce(mx[:, :], gt[:, :, :], AX.X, ALU.max))
                own.then(tt(gt[:, :, :], gt[:, :, :], over(mx[:, :]), ALU.subtract))
                dve.sem_inc(S["shifted"], 1)
                dve.wait_ge(S["exped"], g + 1)
                own.then(dve.tensor_reduce(sm[:, :], ex[:, :, :], AX.X, ALU.add))
                own.then(dve.reciprocal(sm[:, :], sm[:, :]))
                own.then(tt(gt[:, :, :], ex[:, :, :], over(sm[:, :]), ALU.mult))
                own.did(dve.tensor_reduce(mx[:, :], gt[:, :, :], AX.X, ALU.max))
                ge, gj = gt[:, :, :].unsqueeze(3).to_broadcast(X5), gt[:, :, :].unsqueeze(2).to_broadcast(X5)
                own.did(tt(gtx[:, :, :, :], gj, ge, ALU.is_gt))
                own.then(tt(eqx[:, :, :, :], gj, ge, ALU.is_equal))
                own.did(tt(dif[:, :, :], gt[:, :, :], over(mx[:, :]), ALU.subtract))
                own.then(tt(eqx[:, :, :, :], eqx[:, :, :, :], low[:, :, :].unsqueeze(1).to_broadcast(X5), ALU.mult))
                dve.sem_inc(S["gated"], 1)
                own.then(tt(gtx[:, :, :, :], gtx[:, :, :, :], eqx[:, :, :, :], ALU.add))
                own.then(dve.tensor_reduce(rank[:, :, :], gtx[:, :, :, :], AX.X, ALU.add))
                dve.wait_ge(S["exped2"], g + 1)
                own.then(dve.scalar_tensor_tensor(out=gt[:, :, :], in0=rank[:, :, :], scalar=1.5, in1=ex[:, :, :],
                                                  op0=ALU.is_lt, op1=ALU.mult))
                own.then(dve.tensor_reduce(sm[:, :], gt[:, :, :], AX.X, ALU.add))
                own.then(dve.reciprocal(sm[:, :], sm[:, :]))
                dve.wait_ge(S["g5t_kept"], g + 1)
                own.then(tt(g5[:, :, 0:NE], gt[:, :, :], over(sm[:, :]), ALU.mult))
                dve.sem_inc(S["weighed"], 1)
                if not last(g):
                    columns(g + 1, 1 - h)
                dve.wait_ge(S["e2_done"], g + 2)
                dve.wait_ge(S["e2t_kept"], g + 1)
                dve.tensor_tensor(e2[:, :, :].rearrange("p w (e c) -> p w e c", c=EH2),
                                  pe2[:, :, :].rearrange("p w (e c) -> p w e c", c=EH2),
                                  g5[:, :, 0:NE].unsqueeze(3).to_broadcast([P, GW, NE, EH2]),
                                  ALU.mult).then_inc(S["e2_ready"], 1)
                dve.wait_ge(S["out_done"], g + 2)
                xg = K.x[:, ds(g * GW, GW), :]
                own.then(dve.tensor_tensor(xg, xg, po[:, :, :], ALU.add))
                dve.sem_inc(S["added"], 1)
                stats_of(dve, own, K, st, xg, g * GW, GW, S["passed"])
            over_groups(dve, body)
    rstd_of(nc, K)


def project(nc, K, w, al, ar):
    with Phase(nc, "proj") as ph:
        WC = D + 2 * HEADS
        wt = ph.sb("wt", [P, 2, WC])
        at = ph.sb("at", [P, 2, D])
        pr = ph.sb("pr", [P, 2, D])
        xn = [ph.sb(f"xn{i}", [P, GW, D]) for i in range(2)]
        xt = [ph.sb(f"xt{i}", [P, 2, GW * P]) for i in range(2)]
        ft = [ph.sb(f"ft{i}", [P, GW, WC]) for i in range(2)]
        px = [ph.ps(f"px{i}", [P, 2, GW * P]) for i in range(2)]
        pf = ph.ps("pf", [P, GW, 512])
        loaded, normed, turned, kept, mm_done, f_kept, chain, w_ready, a2_kept, spilled = (
            ph.sem(x) for x in ("loaded", "normed", "turned", "kept", "mm_done", "f_kept", "chain", "w_ready",
                                "a2_kept", "spilled"))
        stored = [ph.sem(f"stored{i}") for i in range(2)]
        block = ph.block()

        @block.sync
        def _(sp):
            sp.dma_start(wt[:, :, 0:D], w.rearrange("(k p) c -> p k c", p=P)).then_inc(loaded, 16)
            for i, v in enumerate((al, ar)):
                sp.dma_start(at[:, i, :], v.rearrange("(a h) d -> a (h d)", a=1).to_broadcast([P, D])
                             ).then_inc(loaded, 16)
            sp.dma_start(K.xd.rearrange("(w p) c -> p w c", p=P), K.x[:, :, :]).then_inc(spilled, 16)
            for s in stored:
                sp.sem_inc(s, 32)

            def body(g, h):
                sp.wait_ge(f_kept, g + 2)
                rows = slice_rows(g)
                sp.dma_start(K.ftd[rows, :].rearrange("(w p) c -> p w c", p=P), ft[h][:, :, 0:D]).then_inc(stored[h], 16)
                sp.dma_start(K.a1d[rows, :].rearrange("(w p) c -> p w c", p=P), ft[h][:, :, D:D + HEADS]
                             ).then_inc(stored[h], 16)
            over_groups(sp, body)
            sp.wait_ge(stored[0], 32 * (GROUPS // 2 + 2))
            sp.wait_ge(stored[1], 32 * (GROUPS // 2 + 1))
            sp.wait_ge(spilled, 16)

        @block.scalar
        def _(act):
            act.sem_inc(turned, 2)
            act.sem_inc(f_kept, 1)

            def body(g, h):
                act.wait_ge(turned, g + 1)
                normal(act, K, xn[h], g, normed)
                act.wait_ge(mm_done, g + 2)
                act.wait_ge(stored[h], (g // 2) * 32 + 32 if isinstance(g, int) else stored_at(g, h))
                act.wait_ge(a2_kept, g + 1)
                act.activation(ft[h][:, :, :], pf[:, :, 0:WC], ACT.Copy).then_inc(f_kept, 1)
            stored_at = lambda g, h: (g - h) * 16 + 32
            over_groups(act, body)

        @block.tensor
        def _(pe):
            pe.wait_ge(w_ready, 1)
            pe.sem_inc(kept, 2)
            pe.sem_inc(mm_done, 1)

            def body(g, h):
                pe.wait_ge(normed, g + 1)
                pe.wait_ge(kept, g + 1)
                turn_rows(nc, K, xn[h], px[h], turned)
                pe.wait_ge(kept, g + 3)
                pe.wait_ge(f_kept, g + 1)
                for i in range(GW):
                    for k in range(2):
                        ins = nc.tensor.matmul(pf[:, i, 0:WC], xt[h][:, k, i * P:(i + 1) * P], wt[:, k, :],
                                               start=(k == 0), stop=(k == 1))
                ins.then_inc(mm_done, 1)
            over_groups(pe, body)

        @block.vector
        def _(dve):
            own = Own(dve, chain)
            dve.wait_ge(loaded, 48)
            for i in range(2):
                own.then(dve.tensor_tensor(pr[:, :, :], wt[:, :, 0:D], at[:, i, :].unsqueeze(1).to_broadcast([P, 2, D]),
                                           ALU.mult))
                own.then(dve.tensor_reduce(wt[:, :, D + i * HEADS:D + (i + 1) * HEADS],
                                           pr[:, :, :].rearrange("p k (h d) -> p k h d", d=HD), AX.X, ALU.add))
            dve.sem_inc(w_ready, 1)
            dve.sem_inc(a2_kept, 2)

            def body(g, h):
                dve.wait_ge(turned, g + 3)
                dve.wait_ge(mm_done, g + 1)
                dve.tensor_copy(xt[h][:, :, :], px[h][:, :, :]).then_inc(kept, 1)
                dve.wait_ge(f_kept, g + 2)
                dve.tensor_copy(K.a2[:, ds(g * GW, GW), :], ft[h][:, :, D + HEADS:WC]).then_inc(a2_kept, 1)
            over_groups(dve, body)


def slice_rows(g):
    return ds(g * (GW * P), GW * P)


def edge_logits(nc, K):
    NQ = CHUNKS // QUAD
    with Phase(nc, "log") as ph:
        idx = ph.sb("idx", [P, UNROLL], I32)
        lt = ph.sb("lt", [P, HALVES, 2, CHUNKS, HEADS])
        sel = ph.sb("sel", [P, 2 * QUAD, P], BF16)
        sel_t = [ph.sb(f"sel_t{i}", [P, QUAD, P]) for i in range(2)]
        pt = [ph.ps(f"pt{i}", [P, QUAD, P], BF16) for i in range(2)]
        pa = [ph.ps(f"pa{i}", [P, CHUNKS, HEADS]) for i in range(2)]
        px = [ph.ps(f"px{i}", [P, P]) for i in range(2)]
        gathered = [ph.sem(f"gathered{k}") for k in range(UNROLL)]
        stored = [ph.sem(f"stored{i}") for i in range(HALVES)]
        idx_ready, taken, sel_ready, turned, t_kept, a2_done, a2_kept, x_turned, x_kept, slots_used, passed = (
            ph.sem(x) for x in ("idx_ready", "taken", "sel_ready", "turned", "t_kept", "a2_done", "a2_kept",
                                "x_turned", "x_kept", "slots_used", "passed"))
        block = ph.block()
        sources = K.edges[:, 0, 0:STEPS].rearrange("p (c j) -> p c j", c=CHUNKS)

        def rounds(eng, body):
            with eng.Fori(0, BLOCKS) as b:
                for h in range(HALVES):
                    body(b, h, b * HALVES + h)

        @block.gpsimd
        def _(pool):
            gather_rows(pool, K.a1d, idx, lambda k: lt[:, k // CHUNKS, 0, k % CHUNKS, :], idx_ready, taken, gathered)

        @block.sync
        def _(sp):
            sp.sem_inc(slots_used, UNROLL)

            def body(b, h, j):
                sp.wait_ge(a2_kept, j + 3)
                gate(sp, passed)
                sp.wait_ge(x_turned, j + 1)
                sp.dma_start(K.ltd[ds(j, 1), :, :].rearrange("a p c -> (a p) c"),
                             lt[:, h, :, :, :].rearrange("p a c h -> p (a c h)")).then_inc(stored[h], 16)
                sp.wait_ge(stored[h], b * 16 + 16)
                sp.sem_inc(slots_used, CHUNKS)
            rounds(sp, body)

        @block.vector
        def _(dve):
            def body(b, h, j):
                for q in range(NQ):
                    dve.wait_ge(turned, j * NQ + q + 1)
                    for i in range(QUAD):
                        s = j + (q * QUAD + i) * ROUNDS
                        ins = dve.tensor_scalar(sel[:, (q % 2) * QUAD + i, :], K.iotab[:, :],
                                                K.edges[:, 1, ds(s, 1)], None, ALU.is_equal)
                    ins.then_inc(sel_ready, 1)
                dve.wait_ge(x_turned, j + 1)
                dve.tensor_copy(K.xs[:, ds(j * P, P)], px[h][:, :]).then_inc(x_kept, 1)
            rounds(dve, body)

        @block.tensor
        def _(pe):
            pe.sem_inc(turned, 2)
            pe.sem_inc(x_kept, 2)

            def body(b, h, j):
                for q in range(NQ):
                    ws = unpack(nc, pe.value_load(K.wround[0:1, ds(j + q * ROUNDS, 1)], min_val=0, max_val=WORD_MAX))
                    pe.wait_ge(sel_ready, j * NQ + q + 1)
                    gate(pe, passed)
                    for i in range(QUAD):
                        ins = nc.tensor.transpose(pt[q % 2][:, i, :], sel[:, (q % 2) * QUAD + i, :], K.identb[:, :])
                    ins.then_inc(turned, 1)
                    pe.wait_ge(t_kept, j * NQ + q + 1)
                    if q == 0:
                        pe.wait_ge(a2_kept, j + 1)
                    for i in range(QUAD):
                        ins = nc.tensor.matmul(pa[h][:, q * QUAD + i, :], sel_t[q % 2][:, i, :],
                                               K.a2[:, ds(ws[i], 1), :].rearrange("p a c -> p (a c)"),
                                               start=True, stop=True)
                ins.then_inc(a2_done, 1)
                for c in range(CHUNKS):
                    pe.wait_ge(gathered[h * CHUNKS + c], b * 16 + 16)
                pe.wait_ge(x_kept, j + 1)
                gate(pe, passed)
                nc.tensor.transpose(px[h][:, :], lt[:, h, 0, :, :].rearrange("p c h -> p (c h)"),
                                    K.ident[:, :]).then_inc(x_turned, 1)
            rounds(pe, body)

        @block.scalar
        def _(act):
            act.sem_inc(a2_kept, 2)

            def body(b, h, j):
                for j2 in range(2):
                    sect = h * 2 + j2
                    act.wait_ge(slots_used, b * UNROLL + (sect + 1) * SECT)
                    act.activation(idx[:, sect * SECT:(sect + 1) * SECT].unsqueeze(2),
                                   sources[:, j2 * SECT:(j2 + 1) * SECT, ds(j, 1)], ACT.Copy).then_inc(idx_ready, 1)
                for q in range(NQ):
                    act.wait_ge(turned, j * NQ + q + 3)
                    act.activation(sel_t[q % 2][:, :, :], pt[q % 2][:, :, :], ACT.Copy).then_inc(t_kept, 1)
                act.wait_ge(a2_done, j + 1)
                act.activation(lt[:, h, 1, :, :], pa[h][:, :, :], ACT.Copy).then_inc(a2_kept, 1)
            rounds(act, body)


def segment_maxima(nc, K):
    with Phase(nc, "max") as ph:
        ks = ph.sb("ks", [P, LEN + 2])
        fl = ph.sb("fl", [P, LEN + 1], BF16)
        ys = ks[:, 0:LEN]
        col = ph.sb("col", [P, 4])
        row = ph.sb("row", [1, 4, P])
        pr = ph.ps("pr", [1, 2, P])
        pc = ph.ps("pc", [P, 2])
        loaded, chain, cols, rows, carried = (ph.sem(x) for x in ("loaded", "chain", "cols", "rows", "carried"))
        row_ready = ph.sem("row_ready")
        block = ph.block()

        @block.sync
        def _(sp):
            def keys(shift, first, n):
                start = P + shift
                chunks = K.keyd[start:start + CHUNKS * LEN].rearrange("(c e) -> c e", c=CHUNKS)
                return chunks[:, first:first + n].unsqueeze(1).to_broadcast([CHUNKS, HEADS, n])
            sp.dma_start(ks[:, 1:LEN + 1], keys(0, 0, LEN)).then_inc(loaded, 16)
            sp.dma_start(ks[:, 0:1], keys(-1, 0, 1)).then_inc(loaded, 16)
            sp.dma_start(ks[:, LEN + 1:LEN + 2], keys(1, LEN - 1, 1)).then_inc(loaded, 16)

        @block.vector
        def _(dve):
            own = Own(dve, chain)
            scan = dve.tensor_tensor_scan
            heads = lambda r: row[0:1, r, :].rearrange("a (h c) -> a h c", c=CHUNKS)
            parts = lambda t: t.rearrange("a (c h) -> a h c", h=HEADS)
            dve.wait_ge(loaded, 48)
            own.then(dve.tensor_tensor(fl[:, :], ks[:, 1:LEN + 2], ks[:, 0:LEN + 1], ALU.not_equal))
            own.then(dve.tensor_scalar(fl[:, :], fl[:, :], NEG, None, ALU.mult))

            def carry(r, through, edge, backward):
                own.then(dve.tensor_reduce(col[:, 1:2], through, AX.X, ALU.min))
                own.then(dve.tensor_copy(col[:, 0:1], edge))
                dve.sem_inc(cols, 1)
                dve.wait_ge(rows, r + 1)
                own.did(dve.tensor_copy(heads(0), parts(pr[0:1, 0, :])))
                own.did(dve.tensor_copy(heads(1), parts(pr[0:1, 1, :])))
                own.did(dve.memset(row[0:1, 3, :], NEG))
                own.wait()
                stop = CHUNKS - 1 if backward else 0
                own.then(dve.memset(heads(1)[:, :, stop], NEG))
                flip = (lambda t: t[:, ::-1]) if backward else (lambda t: t)
                own.then(scan(flip(row[0:1, 2, :]), flip(row[0:1, 1, :]), flip(row[0:1, 0, :]), NEG, ALU.add, ALU.max))
                if backward:
                    own.then(dve.tensor_copy(parts(row[0:1, 3, :])[:, :, 0:CHUNKS - 1], heads(2)[:, :, 1:CHUNKS]))
                else:
                    own.then(dve.tensor_copy(parts(row[0:1, 3, :])[:, :, 1:CHUNKS], heads(2)[:, :, 0:CHUNKS - 1]))
                dve.sem_inc(row_ready, 1)
                dve.wait_ge(carried, r + 1)
                own.then(dve.tensor_copy(col[:, 2:3], pc[:, 0:1]))

            own.then(scan(ys, fl[:, 0:LEN], K.xs[:, :], NEG, ALU.add, ALU.max))
            carry(0, fl[:, 0:LEN], ys[:, LEN - 1:LEN], False)
            own.then(scan(ys, fl[:, 0:LEN], K.xs[:, :], col[:, 2:3], ALU.add, ALU.max))
            own.then(scan(K.xs[:, ::-1], fl[:, LEN:0:-1], ys[:, ::-1], NEG, ALU.add, ALU.max))
            carry(1, fl[:, 1:LEN + 1], K.xs[:, 0:1], True)
            own.then(scan(K.xs[:, ::-1], fl[:, LEN:0:-1], ys[:, ::-1], col[:, 2:3], ALU.add, ALU.max))

        @block.tensor
        def _(pe):
            for r in range(2):
                pe.wait_ge(cols, r + 1)
                for i in range(2):
                    ins = nc.tensor.matmul(pr[0:1, i, :], col[:, i:i + 1], K.ident[:, :], start=True, stop=True)
                ins.then_inc(rows, 1)
                pe.wait_ge(row_ready, r + 1)
                nc.tensor.matmul(pc[:, 0:1], row[0:1, 3, :], K.ones[0:1, 0:1], start=True, stop=True
                                 ).then_inc(carried, 1)


def edge_weights(nc, K):
    with Phase(nc, "wts") as ph:
        pw = ph.sb("pw", [P, CHUNKS, ROUNDS, HEADS])
        lt = [ph.sb(f"lt{i}", [P, 2, CHUNKS, HEADS]) for i in range(2)]
        t = [ph.sb(f"t{i}", [P, 2, P]) for i in range(2)]
        d = [ph.sb(f"d{i}", [P, CHUNKS, HEADS]) for i in range(2)]
        xc = [ph.sb(f"xc{i}", [P, P]) for i in range(2)]
        pm = [ph.ps(f"pm{i}", [P, CHUNKS, HEADS]) for i in range(2)]
        loaded = [ph.sem(f"loaded{i}") for i in range(2)]
        chain, taken, turned, summed, d_ready, exped, stored, passed = (
            ph.sem(x) for x in ("chain", "taken", "turned", "summed", "d_ready", "exped", "stored", "passed"))
        block = ph.block()

        def rounds(eng, body):
            with eng.Fori(0, ROUNDS // 2 - 1) as b:
                for h in range(2):
                    body(b, h, b * 2 + h)
            for h in range(2):
                body(ROUNDS // 2 - 1, h, ROUNDS - 2 + h)

        @block.sync
        def _(sp):
            sp.sem_inc(summed, 2)

            def body(b, h, j):
                sp.wait_ge(summed, j + 1)
                sp.dma_start(lt[h][:, :, :, :].rearrange("p a c h -> p (a c h)"),
                             K.ltd[ds(j, 1), :, :].rearrange("a p c -> (a p) c")).then_inc(loaded[h], 16)
            rounds(sp, body)
            sp.wait_ge(exped, ROUNDS + 2)
            sp.dma_start(K.pd, pw[:, :, :, :].rearrange("p c j h -> p (c j h)")).then_inc(stored, 16)
            sp.wait_ge(stored, 16)

        @block.tensor
        def _(pe):
            def body(b, h, j):
                pe.wait_ge(taken, j + 1)
                gate(pe, passed)
                pe.wait_ge(summed, j + 1)
                gate(pe, passed)
                nc.tensor.transpose(pm[h][:, :, :].rearrange("p c h -> p (c h)"), xc[h][:, :],
                                    K.ident[:, :]).then_inc(turned, 1)
            rounds(pe, body)

        @block.vector
        def _(dve):
            own = Own(dve, chain)

            def body(b, h, j):
                own.turn(0, j, 3)
                t4 = lambda i: t[h][:, i, :].rearrange("p (c h) -> p c h", c=CHUNKS)
                dve.wait_ge(loaded[h], b * 16 + 16)
                own.did(dve.tensor_tensor(t4(0), lt[h][:, 0, :, :], lt[h][:, 1, :, :], ALU.add))
                dve.wait_ge(turned, j + 1)
                own.then(dve.tensor_tensor(t4(1), pm[h][:, :, :], lt[h][:, 1, :, :],
                                           ALU.add))
                dve.sem_inc(summed, 1)
                own.then(dve.scalar_tensor_tensor(out=t[h][:, :, :], in0=t[h][:, :, :], scalar=0.2, in1=t[h][:, :, :],
                                                  op0=ALU.mult, op1=ALU.max))
                dve.wait_ge(exped, j + 1)
                dve.tensor_tensor(d[h][:, :, :], t4(0), t4(1), ALU.subtract).then_inc(d_ready, 1)
            rounds(dve, body)

        @block.scalar
        def _(act):
            act.sem_inc(exped, 2)
            for h in range(2):
                act.activation(xc[h][:, :], K.xs[:, h * P:(h + 1) * P], ACT.Copy).then_inc(taken, 1)

            def body(b, h, j):
                act.wait_ge(d_ready, j + 1)
                act.activation(pw[:, :, ds(j, 1), :].rearrange("p c a h -> p c (a h)"), d[h][:, :, :], ACT.Exp
                               ).then_inc(exped, 1)
                if not (isinstance(j, int) and j >= ROUNDS - 2):
                    act.activation(xc[h][:, :], K.xs[:, ds((j + 2) * P, P)], ACT.Copy).then_inc(taken, 1)
            rounds(act, body)


def attention_sum(nc, K):
    with Phase(nc, "att") as ph:
        idx = ph.sb("idx", [P, UNROLL], I32)
        rows = ph.sb("rows", [P, UNROLL, FT])
        pb = [ph.sb(f"pb{i}", [P, UNROLL, HEADS]) for i in range(2)]
        sel = ph.sb("sel", [P, 2 * QUAD, P])
        pm = [ph.ps(f"pm{i}", [P, QUAD, 512]) for i in range(2)]
        gathered = [ph.sem(f"gathered{k}") for k in range(UNROLL)]
        p_loaded = [ph.sem(f"p_loaded{i}") for i in range(2)]
        idx_ready, taken, p_put, sel_ready, mm_done, added, scaled, zeroed = (
            ph.sem(x) for x in ("idx_ready", "taken", "p_put", "sel_ready", "mm_done", "added", "scaled", "zeroed"))
        block = ph.block()
        NQ = UNROLL // QUAD
        PAIRS = BLOCKS // 2

        def blocks(eng, body):
            with eng.Fori(0, PAIRS) as bb:
                for h in range(2):
                    body(bb * 2 + h, h, bb)
            if BLOCKS % 2:
                body(BLOCKS - 1, 0, PAIRS)

        @block.sync
        def _(sp):
            def body(b, h, bb):
                sp.wait_ge(mm_done, b * UNROLL + QUAD)
                sp.dma_start(pb[h][:, :, :].rearrange("p s h -> p (s h)"),
                             K.pd[:, ds(b * (UNROLL * HEADS), UNROLL * HEADS)]).then_inc(p_loaded[h], 16)
            blocks(sp, body)

        @block.scalar
        def _(act):
            def body(b, h, bb):
                act.wait_ge(p_loaded[h], bb * 16 + 16)
                for j in range(UNROLL // SECT):
                    c = slice(j * SECT, (j + 1) * SECT)
                    act.wait_ge(mm_done, b * UNROLL + (j + 1) * SECT)
                    act.activation(idx[:, c], K.edges[:, 0, ds(b * UNROLL + j * SECT, SECT)], ACT.Copy
                                   ).then_inc(idx_ready, 1)
                    act.activation(rows[:, c, D:FT], pb[h][:, c, :], ACT.Copy).then_inc(p_put, 1)
            blocks(act, body)

        @block.gpsimd
        def _(pool):
            gather_rows(pool, K.ftd, idx, lambda k: rows[:, k, 0:D], idx_ready, taken, gathered)

        @block.vector
        def _(dve):
            def weigh(b, h, bb, q):
                for i in range(QUAD):
                    ins = dve.tensor_scalar(sel[:, (q % 2) * QUAD + i, :], K.iota[:, :],
                                            K.edges[:, 1, ds(b * UNROLL + q * QUAD + i, 1)], None, ALU.is_equal)
                if q == 0:
                    dve.wait_ge(p_loaded[h], bb * 16 + 16)
                c = slice(q * QUAD, (q + 1) * QUAD)
                for k in range(q * QUAD, (q + 1) * QUAD):
                    dve.wait_ge(gathered[k], b * 16 + 16)
                r = rows[:, c, 0:D].rearrange("p s (h d) -> p s h d", d=HD)
                dve.tensor_tensor(r, r, pb[h][:, c, :].unsqueeze(3).to_broadcast([P, QUAD, HEADS, HD]),
                                  ALU.mult).then_inc(sel_ready, 1)

            def add(b, q, ws):
                s = b * UNROLL + q * QUAD
                dve.wait_ge(mm_done, UNROLL + s + QUAD)
                for i in range(QUAD):
                    a = K.acc[:, ds(ws[i], 1), :].rearrange("p a c -> p (a c)")
                    dve.wait_ge(added, s + i + 1)
                    dve.tensor_tensor(a, a, pm[q % 2][:, i, 0:FT], ALU.add).then_inc(added, 1)

            dve.memset(K.acc[:, :, :], 0.0).then_inc(added, 1)
            weigh(0, 0, 0, 0)

            def body(b, h, bb):
                for q in range(NQ):
                    ws = quad_windows(dve, K, b * NQ + q)
                    if q < NQ - 1:
                        weigh(b, h, bb, q + 1)
                    elif not (isinstance(b, int) and b == BLOCKS - 1):
                        weigh(b + 1, 1 - h, bb + h, 0)
                    add(b, q, ws)
            blocks(dve, body)

        @block.tensor
        def _(pe):
            pe.sem_inc(mm_done, UNROLL)

            def body(b, h, bb):
                for q in range(NQ):
                    pe.wait_ge(sel_ready, b * NQ + q + 1)
                    if q % (SECT // QUAD) == 0:
                        pe.wait_ge(p_put, b * (UNROLL // SECT) + q // (SECT // QUAD) + 1)
                    for i in range(QUAD):
                        ins = nc.tensor.matmul(pm[q % 2][:, i, 0:FT], sel[:, (q % 2) * QUAD + i, :],
                                               rows[:, q * QUAD + i, :], start=True, stop=True)
                    ins.then_inc(mm_done, QUAD)
            blocks(pe, body)


def attended(nc, K):
    with Phase(nc, "elu") as ph:
        xg = [ph.sb(f"xg{i}", [P, GW, D]) for i in range(2)]
        m = ph.sb("m", [P, GW, D])
        e = ph.sb("e", [P, GW, D])
        den = ph.sb("den", [P, GW, HEADS])
        st = ph.sb("st", [P, GW, 8])
        loaded = [ph.sem(f"loaded{i}") for i in range(2)]
        chain, low_ready, exped, used, passed = (ph.sem(x) for x in ("chain", "low_ready", "exped", "used", "passed"))
        block = ph.block()

        @block.sync
        def _(sp):
            sp.sem_inc(used, 2)

            def body(g, h):
                sp.wait_ge(used, g + 1)
                sp.dma_start(xg[h][:, :, :], K.xd[slice_rows(g), :].rearrange("(w p) c -> p w c", p=P)
                             ).then_inc(loaded[h], 16)
            over_groups(sp, body)

        @block.vector
        def _(dve):
            own = Own(dve, chain)

            def body(g, h):
                own.turn(0, g, 5 + 2 * GW + 1)
                a = K.acc[:, ds(g * GW, GW), :]
                o = a[:, :, 0:D]
                heads = o.rearrange("p w (h d) -> p w h d", d=HD)
                own.then(dve.tensor_scalar(den[:, :, :], a[:, :, D:FT], 0.5, None, ALU.max))
                own.then(dve.reciprocal(den[:, :, :], den[:, :, :]))
                own.then(dve.tensor_tensor(heads, heads, den[:, :, :].unsqueeze(3).to_broadcast([P, GW, HEADS, HD]),
                                           ALU.mult))
                dve.tensor_scalar(m[:, :, :], o, 0.0, None, ALU.min).then_inc(low_ready, 1)
                dve.wait_ge(exped, g + 1)
                own.then(dve.scalar_tensor_tensor(out=o, in0=o, scalar=0.0, in1=e[:, :, :], op0=ALU.max, op1=ALU.add))
                dve.wait_ge(loaded[h], (g - h) * 8 + 16)
                own.then(dve.scalar_tensor_tensor(out=o, in0=o, scalar=-1.0, in1=xg[h][:, :, :], op0=ALU.add,
                                                  op1=ALU.add))
                dve.sem_inc(used, 1)
                stats_of(dve, own, K, st, o, g * GW, GW, passed)
            over_groups(dve, body)

        @block.scalar
        def _(act):
            def body(g, h):
                act.wait_ge(low_ready, g + 1)
                act.activation(e[:, :, :], m[:, :, :], ACT.Exp).then_inc(exped, 1)
            over_groups(act, body)
    K.x = K.acc[:, :, 0:D]
    rstd_of(nc, K)


def choose(nc, K, wr, br):
    BITS = 16
    with Phase(nc, "top") as ph:
        xn = [ph.sb(f"xn{i}", [P, GW, D]) for i in range(2)]
        junk = ph.sb("junk", [P, GW, D])
        wrt, brt = ph.sb("wrt", [P, D]), ph.sb("brt", [P, 1])
        dots = ph.sb("dots", [P, GW])
        wv = ph.sb("wv", [P, W])
        kb, sg, half = (ph.sb(x, [P, W], I32) for x in ("kb", "sg", "half"))
        up, low = ph.sb("up", [P, W]), ph.sb("low", [P, W])
        hit, sure, tie, rank, ones = (ph.sb(x, [P, W]) for x in ("hit", "sure", "tie", "rank", "ones"))
        cur, cand, cnt, step, left = (ph.sb(x, [P, 1]) for x in ("cur", "cand", "cnt", "step", "left"))
        lower = ph.sb("lower", [P, P])
        ptot, ptie = ph.ps("ptot", [P, 1]), ph.ps("ptie", [P, 2, W])
        loaded, normed, read, chain, counted, total, lower_ready = (
            ph.sem(x) for x in ("loaded", "normed", "read", "chain", "counted", "total", "lower_ready"))
        block = ph.block()
        COUNTS = 2 * BITS + 2

        @block.sync
        def _(sp):
            sp.dma_start(wrt[:, :], wr.rearrange("c a -> a c").to_broadcast([P, D])).then_inc(loaded, 16)
            sp.dma_start(brt[:, :], br.unsqueeze(0).to_broadcast([P, 1])).then_inc(loaded, 16)

        @block.gpsimd
        def _(pool):
            pool.memset(lower[:, :], 1.0).then_inc(lower_ready, 1)
            pool.wait_ge(lower_ready, 1)
            pool.affine_select(out=lower[:, :], in_=lower[:, :], compare_op=ALU.is_gt, fill=0.0, base=0,
                               pattern=[[1, P]], channel_multiplier=-1).then_inc(lower_ready, 1)

        @block.scalar
        def _(act):
            act.sem_inc(read, 2)

            def body(g, h):
                act.wait_ge(read, g + 1)
                normal(act, K, xn[h], g, normed)
            over_groups(act, body)

        @block.tensor
        def _(pe):
            for r in range(COUNTS):
                pe.wait_ge(counted, r + 1)
                nc.tensor.matmul(ptot[:, :], K.ones[:, :], cnt[:, :], start=True, stop=True).then_inc(total, 1)
            pe.wait_ge(counted, COUNTS + 1)
            pe.wait_ge(lower_ready, 2)
            nc.tensor.matmul(ptie[:, 0, :], lower[:, :], tie[:, :], start=True, stop=True)
            nc.tensor.matmul(ptie[:, 1, :], K.ones[:, :], tie[:, :], start=True, stop=True).then_inc(total, 1)

        @block.vector
        def _(dve):
            own = Own(dve, chain)
            ts, tt = dve.tensor_scalar, dve.tensor_tensor
            dve.wait_ge(loaded, 32)
            start = own.start()

            def body(g, h):
                own.turn(start, g, GW + 1)
                dve.wait_ge(normed, g + 1)
                for i in range(GW):
                    own.did(dve.scalar_tensor_tensor(out=junk[:, i, :], in0=xn[h][:, i, :], scalar=1.0, in1=wrt[:, :],
                                                     op0=ALU.mult, op1=ALU.mult, accum_out=dots[:, i:i + 1]))
                own.wait()
                dve.sem_inc(read, 1)
                own.then(ts(wv[:, ds(g * GW, GW)], dots[:, :], brt[:, 0:1], None, ALU.add))
            over_groups(dve, body)
            own.finish(start + (GROUPS - 1) * (GW + 1), 1, GW + 1)
            bits = wv[:, :].bitcast(I32)
            own.then(ts(sg[:, :], bits, 31, -(1 << 31), ALU.arith_shift_right, ALU.bitwise_or))
            own.then(tt(kb[:, :], bits, sg[:, :], ALU.bitwise_xor))
            own.then(ts(half[:, :], kb[:, :], BITS, None, ALU.logical_shift_right))
            own.then(ts(up[:, :], half[:, :], 1.0, None, ALU.add))
            own.then(ts(half[:, :], kb[:, :], (1 << BITS) - 1, None, ALU.bitwise_and))
            own.then(ts(low[:, :], half[:, :], 1.0, None, ALU.add))
            own.then(tt(up[:, :], up[:, :], K.real[:, :], ALU.mult))
            own.then(ts(up[:, :], up[:, :], -1.0, None, ALU.add))
            own.then(dve.memset(ones[:, :], 1.0))

            def ask(r):
                dve.sem_inc(counted, 1)
                dve.wait_ge(total, r + 1)

            def search(r, of, wanted):
                own.then(dve.memset(cur[:, :], 0.0))
                for b in reversed(range(BITS)):
                    own.then(ts(cand[:, :], cur[:, :], float(1 << b), None, ALU.add))
                    own.then(ts(hit[:, :], of[:, :], cand[:, 0:1], 0.0, ALU.is_ge, ALU.add, accum_out=cnt[:, 0:1]))
                    ask(r)
                    r += 1
                    own.then(ts(step[:, :], ptot[:, :], wanted, float(1 << b), ALU.is_ge, ALU.mult))
                    own.then(tt(cur[:, :], cur[:, :], step[:, :], ALU.add))
                return r

            def left_over(r):
                own.then(dve.tensor_reduce(cnt[:, :], sure[:, :], AX.X, ALU.add))
                ask(r)
                own.then(ts(left[:, :], ptot[:, :], -1.0, float(TOP), ALU.mult, ALU.add))
                return r + 1

            r = search(0, up, float(TOP))
            own.then(ts(sure[:, :], up[:, :], cur[:, 0:1], None, ALU.is_gt))
            r = left_over(r)
            own.then(ts(tie[:, :], up[:, :], cur[:, 0:1], None, ALU.is_equal))
            own.then(tt(low[:, :], low[:, :], tie[:, :], ALU.mult))
            own.then(ts(low[:, :], low[:, :], -1.0, None, ALU.add))
            r = search(r, low, left[:, 0:1])
            own.then(ts(hit[:, :], low[:, :], cur[:, 0:1], None, ALU.is_gt))
            own.then(tt(sure[:, :], sure[:, :], hit[:, :], ALU.add))
            r = left_over(r)
            assert r == COUNTS
            own.then(ts(tie[:, :], low[:, :], cur[:, 0:1], None, ALU.is_equal))
            ask(r)
            own.then(dve.tensor_copy(hit[:, :], ptie[:, 1, :]))
            own.then(dve.tensor_tensor_scan(rank[:, :], ones[:, :], hit[:, :], 0.0, ALU.mult, ALU.add))
            own.then(tt(rank[:, :], rank[:, :], hit[:, :], ALU.subtract))
            own.then(tt(rank[:, :], rank[:, :], ptie[:, 0, :], ALU.add))
            own.then(ts(rank[:, :], rank[:, :], left[:, 0:1], None, ALU.is_lt))
            own.then(tt(tie[:, :], tie[:, :], rank[:, :], ALU.mult))
            own.then(tt(sure[:, :], sure[:, :], tie[:, :], ALU.add))
            dve.tensor_tensor(K.sw[:, :], wv[:, :], sure[:, :], ALU.mult)


def feed_forward(nc, K, w1, b1, w2, b2, out):
    M = HID // P
    RING = 4
    last = lambda g: isinstance(g, int) and g == GROUPS - 1
    with Phase(nc, "ffn") as ph:
        w1t, b1t = ph.sb("w1t", [P, 2, HID]), ph.sb("b1t", [P, M])
        w2t, b2t = ph.sb("w2t", [P, M, D]), ph.sb("b2t", [1, D])
        xn = [ph.sb(f"xn{i}", [P, GW, D]) for i in range(2)]
        xt = [ph.sb(f"xt{i}", [P, 2, GW * P]) for i in range(2)]
        h1 = ph.sb("h1", [P, M, GW * P])
        y = [ph.sb(f"y{i}", [P, GW, D]) for i in range(2)]
        ring = [ph.ps(f"ring{i}", [P, GW * P]) for i in range(RING)]
        px = ph.ps("px", [P, 2, GW * P])
        py = ph.ps("py", [P, GW, D])
        loaded, normed, turned, xt_kept, h_done, h_kept, y_done, y_used, y_ready, chain = (
            ph.sem(x) for x in ("loaded", "normed", "turned", "xt_kept", "h_done", "h_kept", "y_done", "y_used",
                                "y_ready", "chain"))
        stored = [ph.sem(f"stored{i}") for i in range(2)]
        block = ph.block()

        @block.sync
        def _(sp):
            sp.dma_start(w1t[:, :, :], w1.rearrange("(k p) c -> p k c", p=P)).then_inc(loaded, 16)
            sp.dma_start(b1t[:, :], b1.rearrange("(m p) -> p m", p=P)).then_inc(loaded, 16)
            sp.dma_start(w2t[:, :, :], w2.rearrange("(k p) c -> p k c", p=P)).then_inc(loaded, 16)
            sp.dma_start(b2t[:, :], b2.unsqueeze(0)).then_inc(loaded, 16)
            for s in stored:
                sp.sem_inc(s, 16)
            with sp.Fori(0, GROUPS // 2) as gg:
                for h in range(2):
                    g = gg * 2 + h
                    sp.wait_ge(y_ready, g + 1)
                    sp.dma_start(out[slice_rows(g), :].rearrange("(w p) c -> p w c", p=P), y[h][:, :, :]
                                 ).then_inc(stored[h], 16)
            sp.wait_ge(y_ready, GROUPS)
            first = (GROUPS - 1) * GW * P
            whole = (N - first) // P
            sp.dma_start(out[first:first + whole * P, :].rearrange("(w p) c -> p w c", p=P), y[0][:, 0:whole, :]
                         ).then_inc(stored[0], 16)
            rest = N - first - whole * P
            sp.dma_start(out[N - rest:N, :], y[0][0:rest, whole, :]).then_inc(stored[0], 16)
            sp.wait_ge(stored[0], 16 * (GROUPS // 2 + 3))
            sp.wait_ge(stored[1], 16 * (GROUPS // 2 + 1))

        @block.scalar
        def _(act):
            act.sem_inc(h_kept, RING)
            act.wait_ge(loaded, 64)
            normal(act, K, xn[0], 0, normed)

            def body(g, h):
                if not last(g):
                    act.wait_ge(y_used, g + 1)
                    normal(act, K, xn[1 - h], g + 1, normed)
                for m in range(M):
                    act.wait_ge(h_done, g * M + m + 1)
                    act.activation(h1[:, m, :], ring[m % RING][:, :], ACT.Gelu_apprx_tanh, bias=b1t[:, m:m + 1]
                                   ).then_inc(h_kept, 1)
            over_groups(act, body)

        @block.tensor
        def _(pe):
            pe.wait_ge(loaded, 64)
            pe.wait_ge(normed, 1)
            turn_rows(nc, K, xn[0], px, turned)

            def body(g, h):
                pe.wait_ge(xt_kept, g + 1)
                for m in range(M):
                    pe.wait_ge(h_kept, g * M + m + 1)
                    for k in range(2):
                        ins = nc.tensor.matmul(ring[m % RING][:, :], w1t[:, k, m * P:(m + 1) * P], xt[h][:, k, :],
                                               start=(k == 0), stop=(k == 1))
                    ins.then_inc(h_done, 1)
                if not last(g):
                    pe.wait_ge(normed, g + 2)
                    turn_rows(nc, K, xn[1 - h], px, turned)
                pe.wait_ge(y_used, g + 1)
                pe.wait_ge(h_kept, g * M + RING + M)
                for i in range(GW):
                    nc.tensor.matmul(py[:, i, :], K.ones[0:1, :], b2t[:, :], start=True, stop=False)
                    for m in range(M):
                        ins = nc.tensor.matmul(py[:, i, :], h1[:, m, i * P:(i + 1) * P], w2t[:, m, :],
                                               start=False, stop=(m == M - 1))
                ins.then_inc(y_done, 1)
            over_groups(pe, body)

        @block.vector
        def _(dve):
            own = Own(dve, chain)

            def columns(g, h):
                dve.wait_ge(turned, g + 1)
                dve.tensor_copy(xt[h][:, :, :], px[:, :, :]).then_inc(xt_kept, 1)

            dve.sem_inc(y_used, 1)
            columns(0, 0)

            def body(g, h):
                own.turn(0, g, GW)
                if not last(g):
                    columns(g + 1, 1 - h)
                dve.wait_ge(y_done, g + 1)
                dve.wait_ge(stored[h], (g - h) * 8 + 16)
                for i in range(GW):
                    own.did(dve.scalar_tensor_tensor(out=y[h][:, i, :], in0=py[:, i, :],
                                                     scalar=K.sw[:, ds(g * GW + i, 1)], in1=xn[h][:, i, :],
                                                     op0=ALU.mult, op1=ALU.add))
                own.wait()
                dve.sem_inc(y_used, 1)
                dve.tensor_tensor(y[h][:, :, :], y[h][:, :, :], K.x[:, ds(g * GW, GW), :], ALU.add
                                  ).then_inc(y_ready, 1)
            over_groups(dve, body)


class Kept:
    pass


def build(nc, a, out, until=None, dump=None):
    K = Kept()
    with ExitStack() as stack:
        stack.enter_context(nc.allow_non_contiguous_dma(reason="biases over partitions, a few hundred elements"))

        def sb(name, shape, dt=F32):
            return stack.enter_context(nc.sbuf_tensor(name, shape, dt))

        def dram(name, shape, dt=F32):
            return nc.dram_tensor(name, shape, dt, kind="Internal").ap()

        K.etd = dram("edge_tiles", [TB * P, 3 * P])
        K.keyd = dram("keys", [P + SP * P])
        K.t1 = dram("table1", [NP, CH1])
        K.t2 = dram("table2", [NP, CH2])
        K.xd = dram("x_spilled", [NP, D])
        K.ftd = dram("ft_rows", [NP, D])
        K.a1d = dram("a1_rows", [NP, HEADS])
        K.ltd = dram("logits", [ROUNDS, P, 2 * P])
        K.pd = dram("edge_weights", [P, STEPS * HEADS])
        K.ident, K.ones, K.iota = sb("ident", [P, P]), sb("ones", [P, P]), sb("iota", [P, P])
        K.onesb, K.iotab, K.identb = (sb(x, [P, P], BF16) for x in ("onesb", "iotab", "identb"))
        K.real = sb("real", [P, W])
        K.sw = sb("sw", [P, W])
        K.iotaw = K.iota[:, 0:W]
        K.edges = sb("edges", [P, 3, SP])
        K.wpack = sb("wpack", [1, SP // QUAD], I32)
        K.wround = sb("wround", [1, STEPS // QUAD], I32)
        K.wcol = sb("wcol", [P, SB])
        K.dis = sb("dis", [P, W])
        K.a2 = sb("a2", [P, W, HEADS])
        K.mv, K.rs, K.nmr = sb("mv", [P, W, 2]), sb("rs", [P, W]), sb("nmr", [P, W])
        constants(nc, K)
        schedule(nc, K, a["src"], a["dst"], a["edge_weight"])
        degrees(nc, K)
        with nc.sbuf_tensor("x_rows", [P, W, D], F32) as x, ExitStack() as stack2:
            K.x = x
            load_x(nc, K, a["x"])
            K.acc2 = stack2.enter_context(nc.sbuf_tensor("acc2", [P, W, CH2], F32))
            with nc.sbuf_tensor("acc1", [P, W, CH1], F32) as acc1:
                K.acc1 = acc1
                first_table(nc, K, a["L0_gnn_W1"])
                graph_sum(nc, K, "conv1", K.t1, K.acc1, CH1)
                if until == "conv1":
                    return dump(nc, K)
                second_table(nc, K, a["L0_gnn_b1"], a["L0_gnn_W2"])
            graph_sum(nc, K, "conv2", K.t2, K.acc2, CH2)
            if until == "conv2":
                return dump(nc, K)
            decode(nc, K, a["L0_gnn_b2"], a["L0_gnn_Wd1"], a["L0_gnn_bd1"], a["L0_gnn_Wd2"], a["L0_gnn_bd2"])
            if until == "x1":
                return dump(nc, K)
            mixture(nc, K, a)
            if until == "x2":
                return dump(nc, K)
            project(nc, K, a["L1_gnn_W"], a["L1_gnn_attn_l"], a["L1_gnn_attn_r"])
            if until == "proj":
                return dump(nc, K)
        with nc.sbuf_tensor("maxima", [P, LEN], F32) as xs:
            K.xs = xs
            edge_logits(nc, K)
            segment_maxima(nc, K)
            if until == "max":
                return dump(nc, K)
            edge_weights(nc, K)
        with nc.sbuf_tensor("sums", [P, W, FT], F32) as acc:
            K.acc = acc
            attention_sum(nc, K)
            if until == "att":
                return dump(nc, K)
            attended(nc, K)
            if until == "x3":
                return dump(nc, K)
            choose(nc, K, a["L1_ffn_wr"], a["L1_ffn_br"])
            if until == "sw":
                return dump(nc, K)
            feed_forward(nc, K, a["L1_ffn_w1"], a["L1_ffn_b1"], a["L1_ffn_w2"], a["L1_ffn_b2"], out)


def kernel(**inputs):
    import concourse.bacc as bacc
    from concourse.bass_utils import run_bass_kernel_spmd

    nc = bacc.Bacc("TRN2", target_bir_lowering=False, num_devices=1)
    arrays = {name: np.ascontiguousarray(inputs[name]) for name in inputs if name != "L1_ffn_attention_mask"}
    aps = {name: nc.dram_tensor(name, v.shape, mybir.dt.from_np(v.dtype), kind="ExternalInput").ap()
           for name, v in arrays.items()}
    out = nc.dram_tensor("out", (N, D), F32, kind="ExternalOutput").ap()
    build(nc, aps, out)
    return run_bass_kernel_spmd(nc, [arrays], core_ids=[0]).results[0]["out"]
```

```python
import numpy as np
import concourse.bass as bass
from concourse import mybir
from contextlib import ExitStack

F32, BF16, I32 = mybir.dt.float32, mybir.dt.bfloat16, mybir.dt.int32
ALU, ACT, AX = mybir.AluOpType, mybir.ActivationFunctionType, mybir.AxisListType

P = 128
N, D = 12500, 256
E = 212500
TILES = -(-E // P)
TB = -(-TILES // P)
GW = 4
WIN = -(-N // P)
GROUPS = -(-WIN // GW)
W = GROUPS * GW
NP = W * P
SECT = 8
UNROLL = 4 * SECT
BLOCKS = -(-(TILES + WIN - 1) // UNROLL)
STEPS = BLOCKS * UNROLL
QUAD = 4
WBITS = 7
assert W <= 1 << WBITS
SB = -(-STEPS // P)
SP = SB * P
assert (STEPS - 1) - (TILES - 1) < W
CH1, CH2 = 64, 32
HEADS, HD = 8, 32
HID = 4 * D
TOP = N // 2 - 1
RW = HEADS * (HD + 1) + HEADS
EPS = 1e-5
FAR = 1 << 20
NEG = -1e38
ds = bass.ds


class Own:

    def __init__(self, eng, sem):
        self.eng, self.sem, self.base, self.k = eng, sem, 0, 0

    def did(self, ins):
        ins.then_inc(self.sem, 1)
        self.k += 1

    def wait(self, back=0):
        self.eng.wait_ge(self.sem, self.base + self.k - back)

    def then(self, ins):
        self.did(ins)
        self.wait()

    def start(self):
        return self.base + self.k

    def turn(self, start, it, per):
        self.base, self.k = start + it * per, 0

    def finish(self, start, times, per):
        assert self.k == per, (self.k, per)
        self.base, self.k = start + times * per, 0


def over_groups(eng, body):
    with eng.Fori(0, GROUPS // 2) as gg:
        for h in range(2):
            body(gg * 2 + h, h)
    body(GROUPS - 1, 0)


class Phase:

    def __init__(self, nc, name):
        self.nc, self.name, self.stack, self.sems = nc, name, ExitStack(), []

    def __enter__(self):
        return self

    def __exit__(self, kind, *a):
        self.stack.__exit__(kind, *a)
        if kind is None:
            self.nc.clear_and_free_semaphores(self.sems)
            self.nc.all_engine_barrier()

    def sb(self, name, shape, dt=F32):
        return self.stack.enter_context(self.nc.sbuf_tensor(f"{self.name}_{name}", shape, dt))

    def ps(self, name, shape, dt=F32):
        return self.stack.enter_context(self.nc.psum_tensor(f"{self.name}_{name}", shape, dt))

    def sem(self, name):
        self.sems.append(self.nc.alloc_semaphore(f"{self.name}_{name}"))
        return self.sems[-1]

    def block(self):
        return self.stack.enter_context(self.nc.Block())


def bcast(ap, dims):
    return ap.to_broadcast(dims)


def constants(nc, K):
    with Phase(nc, "const") as ph:
        made, fixed = ph.sem("made"), ph.sem("fixed")
        tmp = ph.sb("tmp", [P, P])
        block = ph.block()

        @block.gpsimd
        def _(pool):
            pool.memset(K.ident[:, :], 0.0).then_inc(made, 1)
            pool.iota(K.iota[:, :], [[1, P]], base=0, channel_multiplier=0,
                      allow_small_or_imprecise_dtypes=True).then_inc(made, 1)
            pool.iota(K.real[:, :], [[P, W]], base=0, channel_multiplier=1,
                      allow_small_or_imprecise_dtypes=True).then_inc(made, 1)
            pool.wait_ge(made, 3)
            pool.affine_select(out=K.ident[:, :], in_=K.ident[:, :], compare_op=ALU.not_equal, fill=1.0, base=0,
                               pattern=[[-1, P]], channel_multiplier=1).then_inc(made, 1)

        @block.vector
        def _(dve):
            dve.memset(K.ones[:, :], 1.0)
            dve.memset(K.onesb[:, :], 1.0)
            dve.wait_ge(made, 4)
            dve.tensor_copy(K.iotab[:, :], K.iota[:, :])
            dve.tensor_scalar(K.real[:, :], K.real[:, :], float(N), None, ALU.is_lt)


def schedule(nc, K, src, dst, ew):
    with Phase(nc, "sch") as ph:
        dti, sti = ph.sb("dti", [P, TB, P], I32), ph.sb("sti", [P, TB, P], I32)
        et = ph.sb("et", [P, TB, 3 * P])
        stepf = ph.sb("stepf", [P, SP])
        pos = ph.sb("pos", [P, SB])
        lb = ph.sb("lb", [P, TB], I32)
        ct = ph.sb("ct", [P, TB])
        cmp_ = ph.sb("cmp", [P, TB, SP], BF16)
        tcol = ph.sb("tcol", [P, SB], I32)
        nwin = ph.sb("nwin", [P, SB])
        se = ph.sb("se", [P, SB, 3 * P])
        key = ph.sb("key", [P, SB, P])
        val = ph.sb("val", [P, SB, P])
        front = ph.sb("front", [1, P])
        wrow = ph.sb("wrow", [1, SP], I32)
        shifted = ph.sb("shifted", [1, SP // QUAD], I32)
        CH = SP // 4
        rowp = ph.ps("rowp", [1, 4, 512])
        colp = ph.ps("colp", [P, 512])
        tp = [ph.ps(f"tp{i}", [P, 3 * P]) for i in range(3)]
        padded, loaded = ph.sem("padded"), ph.sem("loaded")
        iotas, chain = ph.sem("iotas"), ph.sem("chain")
        et_ready, et_stored = ph.sem("et_ready"), ph.sem("et_stored")
        cmp_done, row_done, col_done = ph.sem("cmp_done"), ph.sem("row_done"), ph.sem("col_done")
        tile_ready, gathered = ph.sem("tile_ready"), ph.sem("gathered")
        rel_ready, tp_done, tp_free, key_ready, stored = (ph.sem(x) for x in
                                                          ("rel_ready", "tp_done", "tp_free", "key_ready", "stored"))
        block = ph.block()
        full = (TB - 1) * P * P
        rest = (E - full) // P
        last = E - full - rest * P
        arrays = [(dst, dti), (src, sti), (ew, et[:, :, 2 * P:3 * P])]

        @block.sync
        def _(sp):
            for a, t in arrays:
                sp.dma_start(t[:, 0:TB - 1, :], a[0:full].rearrange("(b p e) -> p b e", b=TB - 1, p=P)
                             ).then_inc(loaded, 16)
            sp.wait_ge(padded, 1)
            for a, t in arrays:
                sp.dma_start(t[0:rest, TB - 1, :], a[full:full + rest * P].rearrange("(p e) -> p e", e=P)
                             ).then_inc(loaded, 16)
                sp.dma_start(t[rest:rest + 1, TB - 1, 0:last],
                             a[E - last:E].rearrange("(p e) -> p e", p=1)).then_inc(loaded, 16)
            sp.wait_ge(et_ready, 1)
            sp.dma_start(K.etd.rearrange("(b p) f -> p b f", p=P), et[:, :, :]).then_inc(et_stored, 16)
            sp.wait_ge(key_ready, 1)
            for edge in (K.keyd[0:P], K.keyd[P + SP * P:]):
                sp.dma_start(edge.rearrange("(p e) -> p e", p=1), front[:, :]).then_inc(stored, 16)
            sp.dma_start(K.keyd[P:P + SP * P].rearrange("(b p e) -> p b e", p=P, e=P), key[:, :, :]
                         ).then_inc(stored, 16)
            sp.wait_ge(stored, 48)

        @block.gpsimd
        def _(pool):
            pool.iota(stepf[:, :], [[1, SP]], base=0, channel_multiplier=0,
                      allow_small_or_imprecise_dtypes=True).then_inc(iotas, 1)
            pool.iota(pos[:, :], [[P, SB]], base=0, channel_multiplier=1,
                      allow_small_or_imprecise_dtypes=True).then_inc(iotas, 1)
            pool.wait_ge(et_stored, 16)
            pool.wait_ge(tile_ready, 1)
            for i in range(SB):
                pool.indirect_dma_start(out=se[:, i, :], out_offset=None, in_=K.etd,
                                        in_offset=bass.IndirectOffsetOnAxis(ap=tcol[:, i:i + 1], axis=0)
                                        ).then_inc(gathered, 16)

        @block.vector
        def _(dve):
            own = Own(dve, chain)
            own.did(dve.memset(dti[:, TB - 1, :], FAR))
            own.did(dve.memset(sti[:, TB - 1, :], 0))
            own.did(dve.memset(front[:, :], -7.0))
            own.then(dve.memset(et[:, TB - 1, 2 * P:3 * P], 0.0))
            dve.sem_inc(padded, 1)
            dve.wait_ge(loaded, 16 * 9)
            own.did(dve.tensor_copy(et[:, :, 0:P], sti[:, :, :]))
            own.did(dve.tensor_copy(et[:, :, P:2 * P], dti[:, :, :]))
            own.then(dve.tensor_scalar(lb[:, :], dti[:, :, P - 1], 7, None, ALU.logical_shift_right))
            dve.sem_inc(et_ready, 1)
            own.then(dve.tensor_copy(ct[:, :], lb[:, :]))
            dve.wait_ge(iotas, 2)
            own.then(dve.tensor_tensor(ct[:, :], ct[:, :], pos[:, 0:TB], ALU.add))
            for b in range(TB):
                dve.tensor_scalar(cmp_[:, b, :], stepf[:, :], ct[:, b:b + 1], None, ALU.is_gt).then_inc(cmp_done, 1)
            dve.wait_ge(col_done, 1)
            dve.tensor_copy(tcol[:, :], colp[:, 0:SB]).then_inc(tile_ready, 1)
            own.then(dve.tensor_tensor(K.wcol[:, :], pos[:, :], colp[:, 0:SB], ALU.subtract))
            own.did(dve.tensor_scalar(nwin[:, :], K.wcol[:, :], float(-P), None, ALU.mult))
            dve.wait_ge(row_done, 1)
            for c in range(4):
                own.did(dve.tensor_tensor(wrow[0:1, c * CH:(c + 1) * CH], stepf[0:1, c * CH:(c + 1) * CH],
                                          rowp[0:1, c, 0:CH], ALU.subtract))
            own.wait()
            quads = wrow[0:1, :].rearrange("a (q i) -> a q i", i=QUAD)
            own.then(dve.tensor_copy(K.wpack[0:1, :], quads[:, :, 0]))
            for i in range(1, QUAD):
                own.then(dve.tensor_scalar(shifted[0:1, :], quads[:, :, i], WBITS * i, None, ALU.logical_shift_left))
                own.then(dve.tensor_tensor(K.wpack[0:1, :], K.wpack[0:1, :], shifted[0:1, :], ALU.bitwise_or))
            dve.wait_ge(gathered, 16 * SB)
            own.then(dve.tensor_scalar(key[:, :, :], se[:, :, P:2 * P], 1.0, None, ALU.add))
            own.then(dve.tensor_tensor(se[:, :, P:2 * P], se[:, :, P:2 * P],
                                       nwin[:, :].unsqueeze(2).to_broadcast([P, SB, P]), ALU.add))
            dve.sem_inc(rel_ready, 1)
            own.then(dve.tensor_scalar(val[:, :, :], se[:, :, P:2 * P], 0.0, None, ALU.is_ge))
            own.then(dve.tensor_tensor(key[:, :, :], key[:, :, :], val[:, :, :], ALU.mult))
            own.then(dve.tensor_scalar(val[:, :, :], se[:, :, P:2 * P], float(P), None, ALU.is_lt))
            dve.tensor_tensor(key[:, :, :], key[:, :, :], val[:, :, :], ALU.mult).then_inc(key_ready, 1)

        @block.tensor
        def _(pe):
            pe.wait_ge(cmp_done, TB)
            for i in range(SB):
                for b in range(TB):
                    last_mm = nc.tensor.matmul(colp[:, i:i + 1], cmp_[:, b, i * P:(i + 1) * P], K.onesb[:, 0:1],
                                               start=(b == 0), stop=(b == TB - 1))
            last_mm.then_inc(col_done, 1)
            for c in range(4):
                for b in range(TB):
                    last_mm = nc.tensor.matmul(rowp[0:1, c, 0:CH], K.onesb[:, 0:1], cmp_[:, b, c * CH:(c + 1) * CH],
                                               start=(b == 0), stop=(b == TB - 1))
            last_mm.then_inc(row_done, 1)
            pe.wait_ge(rel_ready, 1)
            for i in range(SB):
                if i >= 3:
                    pe.wait_ge(tp_free, i - 2)
                for a in range(3):
                    last_mm = nc.tensor.transpose(tp[i % 3][:, a * P:(a + 1) * P], se[:, i, a * P:(a + 1) * P],
                                                  K.ident[:, :])
                last_mm.then_inc(tp_done, 1)

        @block.scalar
        def _(act):
            for i in range(SB):
                act.wait_ge(tp_done, i + 1)
                src_t = tp[i % 3][:, :].rearrange("p (a s) -> p a s", a=3)
                act.activation(K.edges[:, :, i * P:(i + 1) * P], src_t[:, 0:2, :], ACT.Copy)
                act.activation(K.ew[:, i * P:(i + 1) * P], src_t[:, 2, :], ACT.Copy).then_inc(tp_free, 1)


def degrees(nc, K):
    U, NB = UNROLL // 2, 2 * BLOCKS
    with Phase(nc, "deg") as ph:
        ew3 = ph.sb("ew3", [P, SP, 3], BF16)
        r = ph.sb("r", [P, SP])
        sel = ph.sb("sel", [P, U, P], BF16)
        parts = ph.sb("parts", [P, SP, 3])
        part = ph.sb("part", [P, SP])
        partT = ph.sb("partT", [P, SB, P])
        woh = ph.sb("woh", [P, SB, W])
        deg = ph.sb("deg", [P, W])
        pos_ = ph.sb("pos", [P, W])
        pd = [ph.ps(f"pd{i}", [P, U * 3]) for i in range(2)]
        pt = [ph.ps(f"pt{i}", [P, P]) for i in range(2)]
        pw = ph.ps("pw", [P, W])
        split, chain = ph.sem("split"), ph.sem("chain")
        sel_free, sel_ready, part_free = (ph.sem(x) for x in ("sel_free", "sel_ready", "part_free"))
        summed, turned, turn_kept, deg_done, rooted = (ph.sem(x) for x in ("summed", "turned", "turn_kept", "deg_done",
                                                                  "rooted"))
        safe = ph.sem("safe")
        block = ph.block()
        HALF = U // 2

        @block.vector
        def _(dve):
            own = Own(dve, chain)
            ewr = K.ew[:, :]
            own.then(dve.tensor_copy(ew3[:, :, 0], ewr))
            own.then(dve.tensor_tensor(r[:, :], ewr, ew3[:, :, 0], ALU.subtract))
            own.then(dve.tensor_copy(ew3[:, :, 1], r[:, :]))
            own.then(dve.tensor_tensor(r[:, :], r[:, :], ew3[:, :, 1], ALU.subtract))
            own.did(dve.memset(parts[:, STEPS:SP, :], 0.0))
            dve.tensor_copy(ew3[:, :, 2], r[:, :]).then_inc(split, 1)
            with dve.Fori(0, NB) as b:
                for k in range(U):
                    if k % HALF == 0:
                        dve.wait_ge(sel_free, b * U + k + HALF)
                    ins = dve.tensor_scalar(sel[:, k, :], K.iotab[:, :], K.edges[:, 1, ds(b * U + k, 1)], None,
                                            ALU.is_equal)
                    if k % HALF == HALF - 1:
                        ins.then_inc(sel_ready, 1)
            for i in range(SB):
                ins = dve.tensor_scalar(woh[:, i, :], K.iotaw[:, :], K.wcol[:, i:i + 1], None, ALU.is_equal)
                own.did(ins)
            dve.wait_ge(part_free, NB + 2)
            own.wait()
            dve.tensor_reduce(part[:, :], parts[:, :, :], AX.X, ALU.add).then_inc(summed, 1)
            dve.wait_ge(deg_done, 1)
            own.then(dve.tensor_scalar(deg[:, :], pw[:, :], 1.0, None, ALU.add))
            own.did(dve.tensor_scalar(pos_[:, :], deg[:, :], 0.0, None, ALU.is_gt))
            dve.tensor_scalar(deg[:, :], deg[:, :], 1e-12, None, ALU.max).then_inc(safe, 1)
            dve.wait_ge(rooted, 1)
            own.then(dve.reciprocal(deg[:, :], deg[:, :]))
            dve.tensor_tensor(K.dis[:, :], deg[:, :], pos_[:, :], ALU.mult)

        @block.tensor
        def _(pe):
            pe.sem_inc(sel_free, U)
            pe.sem_inc(part_free, 2)
            pe.wait_ge(split, 1)
            with pe.Fori(0, NB // 2) as bb:
                for h in range(2):
                    b = bb * 2 + h
                    pe.wait_ge(part_free, b + 1)
                    for k in range(U):
                        if k % HALF == 0:
                            pe.wait_ge(sel_ready, b * 2 + k // HALF + 1)
                        ins = nc.tensor.matmul(pd[h][:, k * 3:k * 3 + 3], sel[:, k, :],
                                               ew3[:, ds(b * U + k, 1), :].rearrange("p a c -> p (a c)"),
                                               start=True, stop=True)
                        if k % HALF == HALF - 1:
                            ins.then_inc(sel_free, HALF)
            pe.wait_ge(summed, 1)
            for i in range(SB):
                if i >= 2:
                    pe.wait_ge(turn_kept, i - 1)
                nc.tensor.transpose(pt[i % 2][:, :], part[:, i * P:(i + 1) * P], K.ident[:, :]).then_inc(turned, 1)
            pe.wait_ge(turn_kept, SB)
            for i in range(SB):
                ins = nc.tensor.matmul(pw[:, :], partT[:, i, :], woh[:, i, :], start=(i == 0), stop=(i == SB - 1))
            ins.then_inc(deg_done, 1)

        @block.scalar
        def _(act):
            with act.Fori(0, NB // 2) as bb:
                for h in range(2):
                    b = bb * 2 + h
                    act.wait_ge(sel_free, b * U + 2 * U)
                    act.activation(parts[:, ds(b * U, U), :],
                                   pd[h][:, :].rearrange("p (s c) -> p s c", c=3), ACT.Copy).then_inc(part_free, 1)
            for i in range(SB):
                act.wait_ge(turned, i + 1)
                act.activation(partT[:, i, :], pt[i % 2][:, :], ACT.Copy).then_inc(turn_kept, 1)
            act.wait_ge(safe, 1)
            act.activation(deg[:, :], deg[:, :], ACT.Sqrt).then_inc(rooted, 1)


def gate(eng, token):
    eng.sem_inc(token, 1)


def stats_of(dve, own, K, st, x, w0, n, token):
    for i in range(n):
        own.did(dve.bn_stats(st[:, i, 0:6], x[:, i, :]))
    own.wait()
    gate(dve, token)
    for i in range(n):
        own.did(dve.bn_aggr(st[:, i, 6:8], st[:, i, 0:6]))
    own.wait()
    own.did(dve.tensor_copy(K.mv[:, ds(w0, n), :], st[:, 0:n, 6:8]))


def rstd_of(nc, K):
    with Phase(nc, f"rstd{nc.next_id()}") as ph:
        eps, eps_ready, rooted, chain = ph.sb("eps", [P, 1]), ph.sem("eps_ready"), ph.sem("rooted"), ph.sem("chain")
        block = ph.block()

        @block.scalar
        def _(act):
            act.wait_ge(eps_ready, 1)
            act.activation(K.rs[:, :], K.mv[:, :, 1], ACT.Sqrt, bias=eps[:, 0:1]).then_inc(rooted, 1)

        @block.vector
        def _(dve):
            own = Own(dve, chain)
            dve.memset(eps[:, :], EPS).then_inc(eps_ready, 1)
            dve.wait_ge(rooted, 1)
            own.then(dve.reciprocal(K.rs[:, :], K.rs[:, :]))
            own.then(dve.tensor_tensor(K.nmr[:, :], K.mv[:, :, 0], K.rs[:, :], ALU.mult))
            dve.tensor_scalar(K.nmr[:, :], K.nmr[:, :], -1.0, None, ALU.mult)


def load_x(nc, K, x):
    PIECE = 16
    pieces = [(w, min(PIECE, N // P - w)) for w in range(0, N // P, PIECE)]
    tail = N - N // P * P
    with Phase(nc, "load") as ph:
        st = ph.sb("st", [P, GW, 8])
        zeroed, chain, passed = ph.sem("zeroed"), ph.sem("chain"), ph.sem("passed")
        loaded = [ph.sem(f"loaded{i}") for i in range(len(pieces) + 1)]
        block = ph.block()

        @block.sync
        def _(sp):
            for (w, n), s in zip(pieces, loaded):
                sp.dma_start(K.x[:, w:w + n, :], x[w * P:(w + n) * P, :].rearrange("(w p) c -> p w c", p=P)
                             ).then_inc(s, 16)
            sp.wait_ge(zeroed, 1)
            sp.dma_start(K.x[0:tail, N // P, :], x[N // P * P:N, :]).then_inc(loaded[-1], 16)

        @block.vector
        def _(dve):
            own = Own(dve, chain)
            own.then(dve.memset(K.x[:, N // P:W, :], 0.0))
            dve.sem_inc(zeroed, 1)
            for (w, n), s in zip(pieces + [(N // P, W - N // P)], loaded):
                dve.wait_ge(s, 16)
                for i in range(0, n, GW):
                    m = min(GW, n - i)
                    stats_of(dve, own, K, st, K.x[:, w + i:w + i + m, :], w + i, m, passed)
                    own.wait()
    rstd_of(nc, K)


def normal(act, K, xn, g, done):
    for i in range(GW):
        w = g * GW + i
        ins = act.activation(xn[:, i, :], K.x[:, ds(w, 1), :].rearrange("p a c -> p (a c)"), ACT.Identity,
                             bias=K.nmr[:, ds(w, 1)], scale=K.rs[:, ds(w, 1)])
    ins.then_inc(done, 1)


def turn_rows(nc, K, xn, pt, done):
    for i in range(GW):
        for k in range(D // P):
            ins = nc.tensor.transpose(pt[:, k, i * P:(i + 1) * P], xn[:, i, k * P:(k + 1) * P], K.ident[:, :])
    ins.then_inc(done, 1)


def first_table(nc, K, w1):
    with Phase(nc, "t1") as ph:
        wt = ph.sb("wt", [P, 2, CH1])
        xn = [ph.sb(f"xn{i}", [P, GW, D]) for i in range(2)]
        xt = [ph.sb(f"xt{i}", [P, 2, GW * P]) for i in range(2)]
        px = [ph.ps(f"px{i}", [P, 2, GW * P]) for i in range(2)]
        pm = [ph.ps(f"pm{i}", [P, GW, CH1]) for i in range(2)]
        loaded, normed, turned, kept, mm_done, scaled, stored = (
            ph.sem(x) for x in ("loaded", "normed", "turned", "kept", "mm_done", "scaled", "stored"))
        block = ph.block()

        @block.scalar
        def _(act):
            act.sem_inc(turned, 2)
            def body(g, h):
                act.wait_ge(turned, g + 1)
                normal(act, K, xn[h], g, normed)
            over_groups(act, body)

        @block.tensor
        def _(pe):
            pe.wait_ge(loaded, 16)
            pe.sem_inc(kept, 2)
            pe.sem_inc(scaled, 2)
            def body(g, h):
                pe.wait_ge(normed, g + 1)
                pe.wait_ge(kept, g + 1)
                turn_rows(nc, K, xn[h], px[h], turned)
                pe.wait_ge(kept, g + 3)
                pe.wait_ge(scaled, g + 1)
                for i in range(GW):
                    for k in range(2):
                        ins = nc.tensor.matmul(pm[h][:, i, :], xt[h][:, k, i * P:(i + 1) * P], wt[:, k, :],
                                               start=(k == 0), stop=(k == 1))
                ins.then_inc(mm_done, 1)
            over_groups(pe, body)

        @block.vector
        def _(dve):
            def body(g, h):
                dve.wait_ge(turned, g + 3)
                dve.tensor_copy(xt[h][:, :, :], px[h][:, :, :]).then_inc(kept, 1)
                dve.wait_ge(mm_done, g + 1)
                for i in range(GW):
                    w = g * GW + i
                    ins = dve.tensor_scalar(K.acc1[:, ds(w, 1), :].rearrange("p a c -> p (a c)"), pm[h][:, i, :],
                                            K.dis[:, ds(w, 1)], None, ALU.mult)
                ins.then_inc(scaled, 1)
            over_groups(dve, body)

        @block.sync
        def _(sp):
            sp.dma_start(wt[:, :, :], w1.rearrange("(k p) c -> p k c", p=P)).then_inc(loaded, 16)
            sp.wait_ge(scaled, GROUPS + 2)
            sp.dma_start(K.t1.rearrange("(w p) c -> p w c", p=P), K.acc1[:, :, :]).then_inc(stored, 16)
            sp.wait_ge(stored, 16)


def take_indices(nc, K, act, idx, slots_used, idx_ready, column):
    with act.Fori(0, BLOCKS) as b:
        for j in range(UNROLL // SECT):
            act.wait_ge(slots_used, b * UNROLL + (j + 1) * SECT)
            act.activation(idx[:, j * SECT:(j + 1) * SECT], column(b, j), ACT.Copy).then_inc(idx_ready, 1)


def gather_rows(pool, table, idx, dest, idx_ready, taken, gathered):
    with pool.Fori(0, BLOCKS) as b:
        for j in range(UNROLL // SECT):
            pool.wait_ge(idx_ready, b * (UNROLL // SECT) + j + 1)
            pool.sem_inc(taken, 1)
            for k in range(j * SECT, (j + 1) * SECT):
                pool.indirect_dma_start(out=dest(k), out_offset=None, in_=table,
                                        in_offset=bass.IndirectOffsetOnAxis(ap=idx[:, k:k + 1], axis=0)
                                        ).then_inc(gathered[k], 16)


def unpack(nc, word):
    return [nc.s_assert_within((word >> (WBITS * i)) & ((1 << WBITS) - 1), 0, W - 1,
                               skip_runtime_bounds_check_because="a step less a tile is a window")
            for i in range(QUAD)]


def quad_windows(eng, K, quad):
    return unpack(eng.bass, eng.value_load(K.wpack[0:1, ds(quad, 1)]))


def graph_sum(nc, K, name, table, acc, C):
    RING = 4
    with Phase(nc, name) as ph:
        idx = ph.sb("idx", [P, UNROLL], I32)
        rows = ph.sb("rows", [P, UNROLL, C])
        sel = ph.sb("sel", [P, RING * QUAD, P])
        pm = [ph.ps(f"pm{i}", [P, QUAD, C]) for i in range(RING)]
        gathered = [ph.sem(f"gathered{k}") for k in range(UNROLL)]
        idx_ready, taken, sel_ready, mm_done, added = (
            ph.sem(x) for x in ("idx_ready", "taken", "sel_ready", "mm_done", "added"))
        block = ph.block()

        @block.scalar
        def _(act):
            take_indices(nc, K, act, idx, mm_done, idx_ready,
                         lambda b, j: K.edges[:, 0, ds(b * UNROLL + j * SECT, SECT)])

        @block.gpsimd
        def _(pool):
            gather_rows(pool, table, idx, lambda k: rows[:, k, :], idx_ready, taken, gathered)

        @block.vector
        def _(dve):
            def select(q, first):
                for i in range(QUAD):
                    s = first + i
                    ins = dve.tensor_scalar(sel[:, q * QUAD + i, :], K.iota[:, :], K.edges[:, 1, ds(s, 1)],
                                            K.ew[:, ds(s, 1)], ALU.is_equal, ALU.mult)
                ins.then_inc(sel_ready, 1)

            dve.sem_inc(added, 1)
            select(0, 0)
            with dve.Fori(0, BLOCKS) as b:
                for q in range(UNROLL // QUAD):
                    s = b * UNROLL + q * QUAD
                    ws = quad_windows(dve, K, b * (UNROLL // QUAD) + q)
                    select((q + 1) % RING, s + QUAD)
                    dve.wait_ge(mm_done, UNROLL + s + QUAD)
                    for i in range(QUAD):
                        a = acc[:, ds(ws[i], 1), :].rearrange("p a c -> p (a c)")
                        dve.wait_ge(added, s + i + 1)
                        dve.tensor_tensor(a, a, pm[q % RING][:, i, :], ALU.add).then_inc(added, 1)

        @block.tensor
        def _(pe):
            pe.sem_inc(mm_done, UNROLL)
            with pe.Fori(0, BLOCKS) as b:
                for q in range(UNROLL // QUAD):
                    pe.wait_ge(sel_ready, b * (UNROLL // QUAD) + q + 1)
                    for i in range(QUAD):
                        k = q * QUAD + i
                        pe.wait_ge(gathered[k], b * 16 + 16)
                        ins = nc.tensor.matmul(pm[q % RING][:, i, :], sel[:, (q % RING) * QUAD + i, :],
                                               rows[:, k, :], start=True, stop=True)
                    ins.then_inc(mm_done, QUAD)


def row_bias(sp, tile, bias, sem):
    sp.dma_start(tile, bias.unsqueeze(0).to_broadcast([P, bias.shape[0]])).then_inc(sem, 16)


def scaled_sums(dve, K, u, acc, bias, g):
    for i in range(GW):
        w = g * GW + i
        ins = dve.scalar_tensor_tensor(out=u[:, i, :], in0=acc[:, ds(w, 1), :].rearrange("p a c -> p (a c)"),
                                       scalar=K.dis[:, ds(w, 1)], in1=bias, op0=ALU.mult, op1=ALU.add)
    return ins


def second_table(nc, K, b1, w2):
    with Phase(nc, "t2") as ph:
        wt, bt = ph.sb("wt", [CH1, CH2]), ph.sb("bt", [P, CH1])
        u = [ph.sb(f"u{i}", [P, GW, CH1]) for i in range(2)]
        v = [ph.sb(f"v{i}", [P, GW, CH1]) for i in range(2)]
        ht = [ph.sb(f"ht{i}", [CH1, GW * P]) for i in range(2)]
        pt = [ph.ps(f"pt{i}", [CH1, GW * P]) for i in range(2)]
        pm = [ph.ps(f"pm{i}", [P, GW, CH2]) for i in range(2)]
        loaded, summed, relued, turned, kept, mm_done, scaled, stored, passed = (
            ph.sem(x) for x in ("loaded", "summed", "relued", "turned", "kept", "mm_done", "scaled", "stored",
                                "passed"))
        block = ph.block()

        @block.vector
        def _(dve):
            dve.wait_ge(loaded, 32)
            dve.sem_inc(scaled, 2)
            scaled_sums(dve, K, u[0], K.acc1, bt[:, :], 0).then_inc(summed, 1)

            def body(g, h):
                if not (isinstance(g, int) and g == GROUPS - 1):
                    dve.wait_ge(relued, g + 2)
                    scaled_sums(dve, K, u[1 - h], K.acc1, bt[:, :], g + 1).then_inc(summed, 1)
                dve.wait_ge(mm_done, g + 3)
                for i in range(GW):
                    w = g * GW + i
                    ins = dve.tensor_scalar(K.acc2[:, ds(w, 1), :].rearrange("p a c -> p (a c)"), pm[h][:, i, :],
                                            K.dis[:, ds(w, 1)], None, ALU.mult)
                ins.then_inc(scaled, 1)
            over_groups(dve, body)

        @block.scalar
        def _(act):
            act.sem_inc(turned, 2)
            act.sem_inc(mm_done, 2)
            act.sem_inc(relued, 1)

            def body(g, h):
                act.wait_ge(summed, g + 1)
                act.wait_ge(turned, g + 1)
                act.activation(v[h][:, :, :], u[h][:, :, :], ACT.Relu).then_inc(relued, 1)
                act.wait_ge(turned, g + 3)
                act.wait_ge(mm_done, g + 1)
                act.activation(ht[h][:, :], pt[h][:, :], ACT.Copy).then_inc(kept, 1)
            over_groups(act, body)

        @block.tensor
        def _(pe):
            pe.wait_ge(loaded, 32)

            def body(g, h):
                pe.wait_ge(relued, g + 2)
                gate(pe, passed)
                for i in range(GW):
                    ins = nc.tensor.transpose(pt[h][:, i * P:(i + 1) * P], v[h][:, i, :], K.ident[:, :])
                ins.then_inc(turned, 1)
                pe.wait_ge(kept, g + 1)
                pe.wait_ge(scaled, g + 1)
                for i in range(GW):
                    ins = nc.tensor.matmul(pm[h][:, i, :], ht[h][:, i * P:(i + 1) * P], wt[:, :], start=True, stop=True)
                ins.then_inc(mm_done, 1)
            over_groups(pe, body)

        @block.sync
        def _(sp):
            sp.dma_start(wt[:, :], w2).then_inc(loaded, 16)
            row_bias(sp, bt[:, :], b1, loaded)
            sp.wait_ge(scaled, GROUPS + 2)
            sp.dma_start(K.t2.rearrange("(w p) c -> p w c", p=P), K.acc2[:, :, :]).then_inc(stored, 16)
            sp.wait_ge(stored, 16)


def decode(nc, K, b2, wd1, bd1, wd2, bd2):
    with Phase(nc, "dec") as ph:
        bt = ph.sb("bt", [P, CH2])
        w1t, b1t = ph.sb("w1t", [CH2, CH1]), ph.sb("b1t", [CH1, 1])
        w2t = ph.sb("w2t", [CH1 + 1, D])
        u = [ph.sb(f"u{i}", [P, GW, CH2]) for i in range(2)]
        v = [ph.sb(f"v{i}", [P, GW, CH2]) for i in range(2)]
        zt = ph.sb("zt", [CH2, GW * P])
        dt = ph.sb("dt", [CH1 + 1, GW * P])
        sg = [ph.sb(f"sg{i}", [P, GW, D]) for i in range(2)]
        st = ph.sb("st", [P, GW, 8])
        pt = ph.ps("pt", [CH2, GW * P])
        pd = ph.ps("pd", [CH1, GW * P])
        po = [ph.ps(f"po{i}", [P, GW, D]) for i in range(2)]
        loaded, summed, relued, turned, z_kept, d_done, d_kept, o_done, sig_done, used, ones_set, chain, passed = (
            ph.sem(x) for x in ("loaded", "summed", "relued", "turned", "z_kept", "d_done", "d_kept", "o_done",
                                "sig_done", "used", "ones_set", "chain", "passed"))
        block = ph.block()

        @block.sync
        def _(sp):
            row_bias(sp, bt[:, :], b2, loaded)
            sp.dma_start(w1t[:, :], wd1).then_inc(loaded, 16)
            sp.dma_start(b1t[:, :], bd1.unsqueeze(1)).then_inc(loaded, 16)
            sp.dma_start(w2t[0:CH1, :], wd2).then_inc(loaded, 16)
            sp.dma_start(w2t[CH1:CH1 + 1, :], bd2.unsqueeze(0)).then_inc(loaded, 16)

        @block.vector
        def _(dve):
            own = Own(dve, chain)
            dve.memset(dt[CH1:CH1 + 1, :], 1.0).then_inc(ones_set, 1)
            dve.wait_ge(loaded, 16 * 5)
            scaled_sums(dve, K, u[0], K.acc2, bt[:, :], 0).then_inc(summed, 1)
            start = own.start()

            def body(g, h):
                own.turn(start, g, 2 * GW + 2)
                if not (isinstance(g, int) and g == GROUPS - 1):
                    dve.wait_ge(relued, g + 2)
                    scaled_sums(dve, K, u[1 - h], K.acc2, bt[:, :], g + 1).then_inc(summed, 1)
                dve.wait_ge(sig_done, g + 1)
                xg = K.x[:, ds(g * GW, GW), :]
                ins = dve.tensor_tensor(xg, xg, sg[h][:, :, :], ALU.add)
                own.then(ins)
                dve.sem_inc(used, 1)
                stats_of(dve, own, K, st, xg, g * GW, GW, passed)
            over_groups(dve, body)

        @block.scalar
        def _(act):
            act.sem_inc(used, 2)
            act.sem_inc(relued, 1)
            act.wait_ge(ones_set, 1)
            act.wait_ge(loaded, 16 * 5)

            def body(g, h):
                act.wait_ge(summed, g + 1)
                act.activation(v[h][:, :, :], u[h][:, :, :], ACT.Relu).then_inc(relued, 1)
                act.wait_ge(turned, g + 1)
                act.activation(zt[:, :], pt[:, :], ACT.Copy).then_inc(z_kept, 1)
                act.wait_ge(d_done, g + 1)
                act.activation(dt[0:CH1, :], pd[:, :], ACT.Relu, bias=b1t[:, 0:1]).then_inc(d_kept, 1)
                act.wait_ge(o_done, g + 1)
                act.wait_ge(used, g + 1)
                act.activation(sg[h][:, :, :], po[h][:, :, :], ACT.Sigmoid).then_inc(sig_done, 1)
            over_groups(act, body)

        @block.tensor
        def _(pe):
            pe.wait_ge(loaded, 16 * 5)

            def body(g, h):
                pe.wait_ge(relued, g + 2)
                gate(pe, passed)
                for i in range(GW):
                    ins = nc.tensor.transpose(pt[:, i * P:(i + 1) * P], v[h][:, i, :], K.ident[:, :])
                ins.then_inc(turned, 1)
                pe.wait_ge(z_kept, g + 1)
                nc.tensor.matmul(pd[:, :], w1t[:, :], zt[:, :], start=True, stop=True).then_inc(d_done, 1)
                pe.wait_ge(d_kept, g + 1)
                for i in range(GW):
                    ins = nc.tensor.matmul(po[h][:, i, :], dt[:, i * P:(i + 1) * P], w2t[:, :], start=True, stop=True)
                ins.then_inc(o_done, 1)
            over_groups(pe, body)
    rstd_of(nc, K)


FFN_RING = 9


def mixture(nc, K, a):
    NE, EH1, EH2, SH1, SH2 = 4, 128, 64, 256, 128
    PAIRS = NE * EH2 // P
    with Phase(nc, "moe") as ph:
        sw1, sw2 = ph.sb("sw1", [P, 2, SH1]), ph.sb("sw2", [P, 2, SH2])
        sw3 = ph.sb("sw3", [P, D])
        ew1, ew2 = ph.sb("ew1", [P, NE, 2, EH1]), ph.sb("ew2", [P, NE, EH2])
        ew3 = ph.sb("ew3", [P, PAIRS, D])
        gw, gb = ph.sb("gw", [P, 2, NE]), ph.sb("gb", [P, NE])
        sb1, sb2 = ph.sb("sb1", [P, 2]), ph.sb("sb2", [P, 1])
        eb1 = ph.sb("eb1", [P, NE])
        eb2 = ph.sb("eb2", [1, NE * EH2])
        b3 = ph.sb("b3", [NE + 1, D])
        low = ph.sb("low", [P, NE, NE])
        xn = [ph.sb(f"xn{i}", [P, GW, D]) for i in range(2)]
        xt = [ph.sb(f"xt{i}", [P, 2, GW * P]) for i in range(2)]
        h1 = ph.sb("h1", [P, 2 + NE, GW * P])
        h2 = ph.sb("h2", [P, GW * P])
        e2 = ph.sb("e2", [P, GW, PAIRS * P])
        e2t = ph.sb("e2t", [P, PAIRS, GW * P])
        lg, ex, gt = (ph.sb(x, [P, GW, NE]) for x in ("lg", "ex", "gt"))
        rank, dif = (ph.sb(x, [P, GW, NE]) for x in ("rank", "dif"))
        gtx = ph.sb("gtx", [P, GW, NE, NE])
        eqx = ph.sb("eqx", [P, GW, NE, NE])
        mx, sm = ph.sb("mx", [P, GW]), ph.sb("sm", [P, GW])
        g5 = ph.sb("g5", [P, GW, NE + 1])
        g5t = ph.sb("g5t", [NE + 1, GW * P])
        st = ph.sb("st", [P, GW, 8])
        px = ph.ps("px", [P, 2, GW * P])
        ring = [ph.ps(f"ring{i}", [P, GW * P]) for i in range(2)]
        pe2 = ph.ps("pe2", [P, GW, PAIRS * P])
        po = ph.ps("po", [P, GW, D])
        names = ("loaded normed turned xt_kept lg_kept h1_kept h2_kept ring_done shifted exped gated exped2 weighed "
                 "e2_done e2_ready e2_turned e2t_kept g5t_kept out_done added chain passed").split()
        S = {x: ph.sem(x) for x in names}
        block = ph.block()
        LOADS = 15

        @block.sync
        def _(sp):
            def put(t, src_):
                sp.dma_start(t, src_).then_inc(S["loaded"], 16)
            put(sw1[:, :, :], a["L0_ffn_sW1"].rearrange("(k p) c -> p k c", p=P))
            put(gw[:, :, :], a["L0_ffn_gW"].rearrange("(k p) c -> p k c", p=P))
            put(ew1[:, :, :, :], a["L0_ffn_eW1"].rearrange("e (k p) c -> p e k c", p=P))
            put(sw2[:, :, :], a["L0_ffn_sW2"].rearrange("(k p) c -> p k c", p=P))
            put(sw3[:, :], a["L0_ffn_sW3"])
            put(ew2[:, :, :], a["L0_ffn_eW2"].rearrange("e p c -> p e c"))
            put(ew3[:, :, :], a["L0_ffn_eW3"].rearrange("(q e) h c -> (e h) q c", e=2))
            put(gb[:, :], a["L0_ffn_gb"].unsqueeze(0).to_broadcast([P, NE]))
            put(sb1[:, :], a["L0_ffn_sb1"].rearrange("(k p) -> p k", p=P))
            put(sb2[:, :], a["L0_ffn_sb2"].unsqueeze(1))
            put(eb1[:, :], a["L0_ffn_eb1"].rearrange("e p -> p e"))
            put(eb2[:, :], a["L0_ffn_eb2"].rearrange("(a e) c -> a (e c)", a=1))
            put(b3[0:NE, :], a["L0_ffn_eb3"])
            put(b3[NE:NE + 1, :], a["L0_ffn_sb3"].unsqueeze(0))

        last = lambda g: isinstance(g, int) and g == GROUPS - 1

        @block.tensor
        def _(pe):
            mm = nc.tensor.matmul
            pe.wait_ge(S["loaded"], 16 * (LOADS - 1))
            pe.wait_ge(S["normed"], 1)
            turn_rows(nc, K, xn[0], px, S["turned"])

            for x in ("e2_done", "out_done"):
                pe.sem_inc(S[x], 1)

            def body(g, h):
                at = lambda i: ring[(FFN_RING * h + i) % 2]
                free = lambda i: [("g5t_kept", g + 1), ("lg_kept", g + 1)][i]
                pe.wait_ge(S["xt_kept"], g + 1)
                pe.wait_ge(S["h2_kept"], g + 1)
                for i in range(GW):
                    for k in range(2):
                        ins = mm(at(0)[:, i * NE:(i + 1) * NE], xt[h][:, k, i * P:(i + 1) * P], gw[:, k, :],
                                 start=(k == 0), stop=(k == 1))
                ins.then_inc(S["ring_done"], 1)
                for m in range(2 + NE):
                    if m == 0:
                        pe.wait_ge(S["g5t_kept"], g + 1)
                    elif m == 1:
                        pe.wait_ge(S["lg_kept"], g + 1)
                    else:
                        pe.wait_ge(S["h1_kept"], g * (2 + NE) + m - 1)
                    for k in range(2):
                        wt = sw1[:, k, m * P:(m + 1) * P] if m < 2 else ew1[:, m - 2, k, :]
                        ins = mm(at(1 + m)[:, :], wt, xt[h][:, k, :], start=(k == 0), stop=(k == 1))
                    ins.then_inc(S["ring_done"], 1)
                if not last(g):
                    pe.wait_ge(S["normed"], g + 2)
                    pe.wait_ge(S["e2t_kept"], g + 1)
                    turn_rows(nc, K, xn[1 - h], px, S["turned"])
                pe.wait_ge(S["h1_kept"], g * (2 + NE) + 5)
                for k in range(2):
                    ins = mm(at(7)[:, :], sw2[:, k, :], h1[:, k, :], start=(k == 0), stop=(k == 1))
                ins.then_inc(S["ring_done"], 1)
                pe.wait_ge(S["h1_kept"], (g + 1) * (2 + NE))
                pe.wait_ge(S["e2_ready"], g + 1)
                for i in range(GW):
                    mm(pe2[:, i, :], K.ones[0:1, :], eb2[0:1, :], start=True, stop=False)
                    for e in range(NE):
                        ins = mm(pe2[:, i, e * EH2:(e + 1) * EH2], h1[:, 2 + e, i * P:(i + 1) * P], ew2[:, e, :],
                                 start=False, stop=(e == NE - 1))
                ins.then_inc(S["e2_done"], 1)
                pe.wait_ge(S["weighed"], g + 1)
                for i in range(GW):
                    ins = nc.tensor.transpose(at(8)[0:NE + 1, i * P:(i + 1) * P], g5[:, i, :], K.ident[:, :])
                ins.then_inc(S["ring_done"], 1)
                pe.wait_ge(S["e2_ready"], g + 2)
                if not last(g):
                    pe.wait_ge(S["xt_kept"], g + 2)
                for i in range(GW):
                    for q in range(PAIRS):
                        ins = nc.tensor.transpose(px[:, q, i * P:(i + 1) * P], e2[:, i, q * P:(q + 1) * P],
                                                  K.ident[:, :])
                ins.then_inc(S["e2_turned"], 1)
                pe.wait_ge(S["h2_kept"], g + 2)
                pe.wait_ge(S["added"], g + 1)
                pe.wait_ge(S["g5t_kept"], g + 2)
                pe.wait_ge(S["e2t_kept"], g + 2)
                for i in range(GW):
                    c = slice(i * P, (i + 1) * P)
                    mm(po[:, i, :], h2[:, c], sw3[:, :], start=True, stop=False)
                    mm(po[:, i, :], g5t[:, c], b3[:, :], start=False, stop=False)
                    for q in range(PAIRS):
                        ins = mm(po[:, i, :], e2t[:, q, c], ew3[:, q, :], start=False, stop=(q == PAIRS - 1))
                ins.then_inc(S["out_done"], 1)
            over_groups(pe, body)

        @block.scalar
        def _(act):
            for x in ("h2_kept", "g5t_kept", "e2t_kept"):
                act.sem_inc(S[x], 1)
            act.wait_ge(S["loaded"], 16 * (LOADS - 1))
            normal(act, K, xn[0], 0, S["normed"])

            def body(g, h):
                at = lambda i: ring[(FFN_RING * h + i) % 2]
                if not last(g):
                    act.wait_ge(S["turned"], g + 1)
                    normal(act, K, xn[1 - h], g + 1, S["normed"])
                act.wait_ge(S["ring_done"], g * FFN_RING + 1)
                act.wait_ge(S["shifted"], g + 1)
                act.activation(lg[:, :, :], at(0)[:, 0:GW * NE].rearrange("p (w e) -> p w e", e=NE), ACT.Copy
                               ).then_inc(S["lg_kept"], 1)
                for m in range(2 + NE):
                    act.wait_ge(S["ring_done"], g * FFN_RING + 2 + m)
                    bias = sb1[:, m:m + 1] if m < 2 else eb1[:, m - 2:m - 1]
                    if m == 0:
                        act.wait_ge(S["e2_done"], g + 1)
                    act.activation(h1[:, m, :], at(1 + m)[:, :], ACT.Relu, bias=bias).then_inc(S["h1_kept"], 1)
                act.wait_ge(S["shifted"], g + 2)
                act.activation(ex[:, :, :], gt[:, :, :], ACT.Exp).then_inc(S["exped"], 1)
                act.wait_ge(S["ring_done"], g * FFN_RING + 8)
                act.wait_ge(S["out_done"], g + 1)
                act.activation(h2[:, :], at(7)[:, :], ACT.Relu, bias=sb2[:, 0:1]).then_inc(S["h2_kept"], 1)
                act.wait_ge(S["gated"], g + 1)
                act.activation(ex[:, :, :], dif[:, :, :], ACT.Exp).then_inc(S["exped2"], 1)
                act.wait_ge(S["ring_done"], g * FFN_RING + 9)
                act.activation(g5t[:, :], at(8)[0:NE + 1, :], ACT.Copy).then_inc(S["g5t_kept"], 1)
                act.wait_ge(S["e2_turned"], g + 1)
                act.activation(e2t[:, :, :], px[:, :, :], ACT.Relu).then_inc(S["e2t_kept"], 1)
            over_groups(act, body)

        @block.vector
        def _(dve):
            own = Own(dve, S["chain"])
            tt, X4 = dve.tensor_tensor, [P, GW, NE]
            own.did(dve.memset(low[:, :, :], 0.0))
            own.then(dve.memset(g5[:, :, NE:NE + 1], 1.0))
            for e in range(1, NE):
                own.did(dve.memset(low[:, e, 0:e], 1.0))
            own.wait()
            for x in ("shifted", "added", "e2_ready"):
                dve.sem_inc(S[x], 1)
            start = own.start()
            over = lambda t: t.unsqueeze(2).to_broadcast(X4)
            X5 = [P, GW, NE, NE]

            def columns(g, h):
                dve.wait_ge(S["turned"], g + 1)
                dve.tensor_copy(xt[h][:, :, :], px[:, :, :]).then_inc(S["xt_kept"], 1)

            columns(0, 0)

            def body(g, h):
                own.turn(start, g, 18 + 2 * GW + 1)
                dve.wait_ge(S["lg_kept"], g + 1)
                own.then(tt(gt[:, :, :], lg[:, :, :], gb[:, :].unsqueeze(1).to_broadcast(X4), ALU.add))
                own.then(dve.tensor_reduce(mx[:, :], gt[:, :, :], AX.X, ALU.max))
                own.then(tt(gt[:, :, :], gt[:, :, :], over(mx[:, :]), ALU.subtract))
                dve.sem_inc(S["shifted"], 1)
                dve.wait_ge(S["exped"], g + 1)
                own.then(dve.tensor_reduce(sm[:, :], ex[:, :, :], AX.X, ALU.add))
                own.then(dve.reciprocal(sm[:, :], sm[:, :]))
                own.then(tt(gt[:, :, :], ex[:, :, :], over(sm[:, :]), ALU.mult))
                own.did(dve.tensor_reduce(mx[:, :], gt[:, :, :], AX.X, ALU.max))
                ge, gj = gt[:, :, :].unsqueeze(3).to_broadcast(X5), gt[:, :, :].unsqueeze(2).to_broadcast(X5)
                own.did(tt(gtx[:, :, :, :], gj, ge, ALU.is_gt))
                own.then(tt(eqx[:, :, :, :], gj, ge, ALU.is_equal))
                own.did(tt(dif[:, :, :], gt[:, :, :], over(mx[:, :]), ALU.subtract))
                own.then(tt(eqx[:, :, :, :], eqx[:, :, :, :], low[:, :, :].unsqueeze(1).to_broadcast(X5), ALU.mult))
                dve.sem_inc(S["gated"], 1)
                own.then(tt(gtx[:, :, :, :], gtx[:, :, :, :], eqx[:, :, :, :], ALU.add))
                own.then(dve.tensor_reduce(rank[:, :, :], gtx[:, :, :, :], AX.X, ALU.add))
                dve.wait_ge(S["exped2"], g + 1)
                own.then(dve.scalar_tensor_tensor(out=gt[:, :, :], in0=rank[:, :, :], scalar=1.5, in1=ex[:, :, :],
                                                  op0=ALU.is_lt, op1=ALU.mult))
                own.then(dve.tensor_reduce(sm[:, :], gt[:, :, :], AX.X, ALU.add))
                own.then(dve.reciprocal(sm[:, :], sm[:, :]))
                dve.wait_ge(S["g5t_kept"], g + 1)
                own.then(tt(g5[:, :, 0:NE], gt[:, :, :], over(sm[:, :]), ALU.mult))
                dve.sem_inc(S["weighed"], 1)
                if not last(g):
                    columns(g + 1, 1 - h)
                dve.wait_ge(S["e2_done"], g + 2)
                dve.wait_ge(S["e2t_kept"], g + 1)
                dve.tensor_tensor(e2[:, :, :].rearrange("p w (e c) -> p w e c", c=EH2),
                                  pe2[:, :, :].rearrange("p w (e c) -> p w e c", c=EH2),
                                  g5[:, :, 0:NE].unsqueeze(3).to_broadcast([P, GW, NE, EH2]),
                                  ALU.mult).then_inc(S["e2_ready"], 1)
                dve.wait_ge(S["out_done"], g + 2)
                xg = K.x[:, ds(g * GW, GW), :]
                own.then(dve.tensor_tensor(xg, xg, po[:, :, :], ALU.add))
                dve.sem_inc(S["added"], 1)
                stats_of(dve, own, K, st, xg, g * GW, GW, S["passed"])
            over_groups(dve, body)
    rstd_of(nc, K)


def project(nc, K, w, al, ar):
    with Phase(nc, "proj") as ph:
        WC, H1 = D + 2 * HEADS, HD + 1
        wt = ph.sb("wt", [P, 2, WC])
        at = ph.sb("at", [P, 2, D])
        pr = ph.sb("pr", [P, 2, D])
        xn = [ph.sb(f"xn{i}", [P, GW, D]) for i in range(2)]
        xt = [ph.sb(f"xt{i}", [P, 2, GW * P]) for i in range(2)]
        ft = [ph.sb(f"ft{i}", [P, GW, RW + HEADS]) for i in range(2)]
        px = [ph.ps(f"px{i}", [P, 2, GW * P]) for i in range(2)]
        pf = ph.ps("pf", [P, GW, 512])
        loaded, normed, turned, kept, mm_done, f_kept, chain, w_ready, a2_kept, spilled = (
            ph.sem(x) for x in ("loaded", "normed", "turned", "kept", "mm_done", "f_kept", "chain", "w_ready",
                                "a2_kept", "spilled"))
        stored = [ph.sem(f"stored{i}") for i in range(2)]
        block = ph.block()

        @block.sync
        def _(sp):
            sp.dma_start(wt[:, :, 0:D], w.rearrange("(k p) c -> p k c", p=P)).then_inc(loaded, 16)
            for i, v in enumerate((al, ar)):
                sp.dma_start(at[:, i, :], v.rearrange("(a h) d -> a (h d)", a=1).to_broadcast([P, D])
                             ).then_inc(loaded, 16)
            sp.dma_start(K.xd.rearrange("(w p) c -> p w c", p=P), K.x[:, :, :]).then_inc(spilled, 16)
            for s in stored:
                sp.sem_inc(s, 16)

            def body(g, h):
                sp.wait_ge(f_kept, g + 2)
                rows = slice_rows(g)
                sp.dma_start(K.ftd[rows, :].rearrange("(w p) c -> p w c", p=P), ft[h][:, :, 0:RW]).then_inc(stored[h], 16)
            over_groups(sp, body)
            sp.wait_ge(stored[0], 16 * (GROUPS // 2 + 2))
            sp.wait_ge(stored[1], 16 * (GROUPS // 2 + 1))
            sp.wait_ge(spilled, 16)

        @block.scalar
        def _(act):
            act.sem_inc(turned, 2)
            act.sem_inc(f_kept, 1)

            def body(g, h):
                act.wait_ge(turned, g + 1)
                normal(act, K, xn[h], g, normed)
                act.wait_ge(mm_done, g + 2)
                act.wait_ge(stored[h], (g - h) * 8 + 16)
                act.wait_ge(a2_kept, g + 1)
                heads = ft[h][:, :, 0:HEADS * H1].rearrange("p w (h d) -> p w h d", d=H1)
                act.activation(heads[:, :, :, 0:HD], pf[:, :, 0:D].rearrange("p w (h d) -> p w h d", d=HD), ACT.Copy)
                act.activation(ft[h][:, :, HEADS * H1:RW + HEADS], pf[:, :, D:WC], ACT.Copy).then_inc(f_kept, 1)
            over_groups(act, body)

        @block.tensor
        def _(pe):
            pe.wait_ge(w_ready, 1)
            pe.sem_inc(kept, 2)
            pe.sem_inc(mm_done, 1)

            def body(g, h):
                pe.wait_ge(normed, g + 1)
                pe.wait_ge(kept, g + 1)
                turn_rows(nc, K, xn[h], px[h], turned)
                pe.wait_ge(kept, g + 3)
                pe.wait_ge(f_kept, g + 1)
                for i in range(GW):
                    for k in range(2):
                        ins = nc.tensor.matmul(pf[:, i, 0:WC], xt[h][:, k, i * P:(i + 1) * P], wt[:, k, :],
                                               start=(k == 0), stop=(k == 1))
                ins.then_inc(mm_done, 1)
            over_groups(pe, body)

        @block.vector
        def _(dve):
            own = Own(dve, chain)
            dve.wait_ge(loaded, 48)
            for i in range(2):
                own.then(dve.tensor_tensor(pr[:, :, :], wt[:, :, 0:D], at[:, i, :].unsqueeze(1).to_broadcast([P, 2, D]),
                                           ALU.mult))
                own.then(dve.tensor_reduce(wt[:, :, D + i * HEADS:D + (i + 1) * HEADS],
                                           pr[:, :, :].rearrange("p k (h d) -> p k h d", d=HD), AX.X, ALU.add))
            dve.sem_inc(w_ready, 1)
            for h in range(2):
                heads = ft[h][:, :, 0:HEADS * H1].rearrange("p w (h d) -> p w h d", d=H1)
                dve.memset(heads[:, :, :, HD], 1.0).then_inc(a2_kept, 1)

            def body(g, h):
                dve.wait_ge(turned, g + 3)
                dve.wait_ge(mm_done, g + 1)
                dve.tensor_copy(xt[h][:, :, :], px[h][:, :, :]).then_inc(kept, 1)
                dve.wait_ge(f_kept, g + 2)
                dve.tensor_copy(K.a2[:, ds(g * GW, GW), :], ft[h][:, :, RW:RW + HEADS]).then_inc(a2_kept, 1)
            over_groups(dve, body)


def slice_rows(g):
    return ds(g * (GW * P), GW * P)


def segment_flags(nc, K):
    with Phase(nc, "flag") as ph:
        ks = ph.sb("ks", [P, SB, P + 2])
        fl = ph.sb("fl", [P, SB, P + 1])
        flb = ph.sb("flb", [P, SB, P + 2], BF16)
        th = ph.sb("th", [P, 2, SB])
        loaded, chain, made, stored = (ph.sem(x) for x in ("loaded", "chain", "made", "stored"))
        block = ph.block()

        @block.sync
        def _(sp):
            def keys(shift):
                return K.keyd[P + shift:P + shift + SP * P].rearrange("(b p e) -> p b e", p=P, e=P)
            sp.dma_start(ks[:, :, 1:P + 1], keys(0)).then_inc(loaded, 16)
            sp.dma_start(ks[:, :, 0:1], keys(-1)[:, :, 0:1]).then_inc(loaded, 16)
            sp.dma_start(ks[:, :, P + 1:P + 2], keys(1)[:, :, P - 1:P]).then_inc(loaded, 16)
            sp.wait_ge(made, 1)
            sp.dma_start(K.fld.rearrange("(b p) e -> p b e", p=P), flb[:, :, :]).then_inc(stored, 16)
            for i in range(2):
                sp.dma_start(K.thd[i, :].rearrange("(b p) -> p b", p=P), th[:, i, :]).then_inc(stored, 16)
            sp.wait_ge(stored, 48)

        @block.vector
        def _(dve):
            own = Own(dve, chain)
            own.did(dve.memset(flb[:, :, :], 0.0))
            dve.wait_ge(loaded, 48)
            own.then(dve.tensor_tensor(fl[:, :, :], ks[:, :, 1:P + 2], ks[:, :, 0:P + 1], ALU.not_equal))
            own.then(dve.tensor_scalar(fl[:, :, :], fl[:, :, :], NEG, None, ALU.mult))
            own.did(dve.tensor_copy(flb[:, :, 0:P + 1], fl[:, :, :]))
            for i in range(2):
                own.did(dve.tensor_reduce(th[:, i, :], fl[:, :, i:i + P], AX.X, ALU.min))
            own.wait()
            dve.sem_inc(made, 1)


def attention(nc, K):
    SEGS, SECTS = P // HEADS, 5
    NB, NQ, SLOTS = STEPS // SEGS, SEGS // QUAD, SECTS * SECT
    PERIOD, RINGQ = 5, 5
    H1 = HD + 1
    SLOT = SEGS + 1
    assert (PERIOD * SEGS) % SLOTS == 0 and NB % PERIOD == 0 and (PERIOD * NQ) % RINGQ == 0
    with Phase(nc, "att") as ph:
        idx = ph.sb("idx", [P, SLOTS], I32)
        rows = ph.sb("rows", [P, SLOTS, RW])
        sel = ph.sb("sel", [P, RINGQ * QUAD, P])
        sel_t = ph.sb("sel_t", [P, QUAD, P])
        a1 = ph.sb("a1", [P, SEGS, HEADS])
        a2 = ph.sb("a2", [P, P])
        fl = ph.sb("fl", [P, P + 2], BF16)
        mx, my = ph.sb("mx", [P, P]), ph.sb("my", [P, P])
        th = ph.sb("th", [1, 2, HEADS, SLOT])
        rv = ph.sb("rv", [1, 2, HEADS * SLOT + 1])
        ro = ph.sb("ro", [1, 2, HEADS * SLOT + 1])
        rc = ph.sb("rc", [1, 2, SEGS, HEADS])
        cc = ph.sb("cc", [P, 2])
        uv = ph.sb("uv", [P, 2, P + HEADS])
        df = ph.sb("df", [P, P + HEADS])
        pw = ph.sb("pw", [P, P + HEADS])
        minus = ph.sb("minus", [1, HEADS])
        pm = [ph.ps(f"pm{i}", [P, 512]) for i in range(QUAD)]
        pt = ph.ps("pt", [P, QUAD, P])
        pxr = ph.ps("pxr", [P, 3, P])
        px, pr = pxr[:, 0, :], pxr[0:1, 1:3, :]
        pma = ph.ps("pma", [P, 2, P])
        pmx, pa = pma[:, 0, :], pma[:, 1, :]
        pcf = ph.ps("pcf", [P, 2 + HEADS])
        pc, pf = pcf[:, 0:2], pcf[:, 2:2 + HEADS]
        gathered = [ph.sem(f"gathered{k}") for k in range(SECTS)]
        (idx_ready, taken, sel_ready, weighed, mm_done, added, turned, t_kept, a_done, a1_ready, x_turned, fl_loaded,
         th_loaded, local_done, row_done, row_kept, row_scanned, carry_kept, col_done, m_ready, m_turned, d_ready,
         p_ready, f_done, chain, passed, set_up, a2_kept) = (
            ph.sem(x) for x in (
                "idx_ready taken sel_ready weighed mm_done added turned t_kept a_done a1_ready x_turned fl_loaded "
                "th_loaded local_done row_done row_kept row_scanned carry_kept col_done m_ready m_turned d_ready "
                "p_ready f_done chain passed set_up a2_kept").split())
        block = ph.block()

        def blocks(eng, body):
            with eng.Fori(0, NB // PERIOD - 1) as turn:
                for i in range(PERIOD):
                    body(turn, i, True)
            for i in range(PERIOD):
                body(NB // PERIOD - 1, i, i < PERIOD - 1)

        last_but_one = lambda b: isinstance(b, int) and b == NB - 2
        block_of = lambda turn, i: turn * PERIOD + i
        following = lambda turn, i: (turn + (i + 1) // PERIOD, (i + 1) % PERIOD)
        slot = lambda i, s: (i * SEGS + s) % SLOTS
        place = lambda i, q: (i * NQ + q) % RINGQ * QUAD

        @block.sync
        def _(sp):
            def load(n):
                sp.dma_start(fl[:, :], K.fld[ds(n * SEGS, SEGS), :].unsqueeze(1).to_broadcast([SEGS, HEADS, P + 2])
                             ).then_inc(fl_loaded, 16)
                for d in range(2):
                    sp.dma_start(th[0:1, d, :, 1 - d:SLOT - d],
                                 K.thd[d:d + 1, ds(n * SEGS, SEGS)].unsqueeze(1).to_broadcast([1, HEADS, SEGS])
                                 ).then_inc(th_loaded, 16)
            sp.wait_ge(set_up, 1)
            load(0)

            def body(turn, i, more):
                if more:
                    sp.wait_ge(m_ready, block_of(turn, i) + 1)
                    load(block_of(turn, i) + 1)
            blocks(sp, body)

        @block.gpsimd
        def _(pool):
            with pool.Fori(0, STEPS // SLOTS) as turn:
                for j in range(SECTS):
                    pool.wait_ge(idx_ready, turn * SECTS + j + 1)
                    pool.sem_inc(taken, 1)
                    for k in range(j * SECT, (j + 1) * SECT):
                        pool.indirect_dma_start(out=rows[:, k, :], out_offset=None, in_=K.ftd,
                                                in_offset=bass.IndirectOffsetOnAxis(ap=idx[:, k:k + 1], axis=0)
                                                ).then_inc(gathered[j], 16)

        @block.scalar
        def _(act):
            def take(section, j):
                act.activation(idx[:, j * SECT:(j + 1) * SECT], K.edges[:, 0, ds(section * SECT, SECT)], ACT.Copy
                               ).then_inc(idx_ready, 1)

            def attention_of(turn, i):
                for k in range(2):
                    r, j = divmod(2 * i + k, SECTS)
                    act.wait_ge(gathered[j], turn * (2 * SECT * 16) + (r + 1) * SECT * 16)
                    ins = act.activation(a1[:, k * SECT:(k + 1) * SECT, :],
                                         rows[:, j * SECT:(j + 1) * SECT, HEADS * H1:RW], ACT.Copy)
                ins.then_inc(a1_ready, 1)

            def columns(n, q):
                act.wait_ge(turned, n * NQ + q + 1)
                act.activation(sel_t[:, :, :], pt[:, :, :], ACT.Copy).then_inc(t_kept, 1)

            def ends(n):
                act.wait_ge(row_done, n + 1)
                for d in range(2):
                    ins = act.activation(
                        rv[0:1, d, 0:HEADS * SLOT].rearrange("a (h s) -> a s h", s=SLOT)[:, 1 - d:SLOT - d, :],
                        pr[:, d, :].rearrange("a (s h) -> a s h", h=HEADS), ACT.Copy)
                ins.then_inc(row_kept, 1)

            def carries(n):
                act.wait_ge(row_scanned, n + 1)
                act.activation(rc[:, :, :, :],
                               ro[0:1, :, 1:HEADS * SLOT + 1].rearrange("a d (h s) -> a d s h", s=SLOT)[:, :, 0:SEGS, :],
                               ACT.Copy).then_inc(carry_kept, 1)

            def weights(n):
                act.wait_ge(a_done, n + 1)
                act.activation(a2[:, :], pa, ACT.Copy).then_inc(a2_kept, 1)
                act.wait_ge(d_ready, n + 1)
                act.activation(pw[:, :], df[:, :], ACT.Exp).then_inc(p_ready, 1)

            act.sem_inc(a2_kept, 1)
            for j in range(SECTS):
                take(j, j)
            attention_of(0, 0)
            columns(0, 0)
            ends(0)
            carries(0)
            for q in range(1, NQ):
                columns(0, q)
            weights(0)

            def body(turn, i, more):
                b = block_of(turn, i)
                n = b + 1

                def refill(k):
                    act.wait_ge(mm_done, b * SEGS + (k + 1) * SECT)
                    if not isinstance(turn, int) or 2 * b + k + SECTS < STEPS // SECT:
                        take(b * 2 + (k + SECTS), (2 * i + k) % SECTS)

                if more:
                    attention_of(*following(turn, i))
                    columns(n, 0)
                    ends(n)
                refill(0)
                if more:
                    carries(n)
                    columns(n, 1)
                    columns(n, 2)
                    columns(n, 3)
                refill(1)
                if more:
                    weights(n)
            blocks(act, body)

        @block.tensor
        def _(pe):
            mm, turn_ = nc.tensor.matmul, nc.tensor.transpose

            def heads_turned(n):
                pe.wait_ge(a1_ready, n + 1)
                turn_(px, a1[:, :, :].rearrange("p s h -> p (s h)"), K.ident[:, :]).then_inc(x_turned, 1)

            def turn_quad(n, i, q):
                pe.wait_ge(sel_ready, n * NQ + q + 1)
                for k in range(QUAD):
                    ins = turn_(pt[:, k, :], sel[:, place(i, q) + k, :], K.ident[:, :])
                ins.then_inc(turned, 1)

            def own_places(n, q):
                at = [K.a2[:, ds(w, 1), :].rearrange("p a c -> p (a c)") for w in quad_windows(pe, K, n * NQ + q)]
                for a in at:
                    pe.lower_ap(a)
                return at

            def own_attention(n, q, at):
                pe.wait_ge(t_kept, n * NQ + q + 1)
                if q == 0:
                    gate(pe, passed)
                    pe.wait_ge(a2_kept, n + 1)
                for k in range(QUAD):
                    s = q * QUAD + k
                    ins = mm(pa[:, s * HEADS:(s + 1) * HEADS], sel_t[:, k, :], at[k], start=True, stop=True)
                if q == NQ - 1:
                    ins.then_inc(a_done, 1)

            def ends_turned(n):
                pe.wait_ge(local_done, n + 1)
                mm(pr[:, 0, :], mx[:, P - 1:P], K.ident[:, :], start=True, stop=True)
                mm(pr[:, 1, :], mx[:, 0:1], K.ident[:, :], start=True, stop=True).then_inc(row_done, 1)

            def carries_turned(n):
                pe.wait_ge(carry_kept, n + 1)
                for d in range(2):
                    ins = mm(pc[:, d:d + 1], rc[0:1, d, :, :].rearrange("a s h -> a (s h)"), K.ones[0:1, 0:1],
                             start=True, stop=True)
                ins.then_inc(col_done, 1)

            def maxima_turned(n):
                pe.wait_ge(m_ready, n + 1)
                turn_(pmx, mx[:, :], K.ident[:, :]).then_inc(m_turned, 1)

            def factor(n, i):
                first = sel[0:1, place(i, 0), :]
                pe.wait_ge(p_ready, n + 1)
                mm(pf, K.ones[0:1, :], K.ones[0:1, 0:HEADS], start=True, stop=False)
                mm(pf, first, minus[:, :], start=False, stop=False)
                mm(pf, first, pw[0:1, P:P + HEADS], start=False, stop=True).then_inc(f_done, 1)

            def sums(b, i, q):
                pe.wait_ge(weighed, b * NQ + q + 1)
                for k in range(QUAD):
                    pe.wait_ge(added, b * SEGS + (q * QUAD + k + 1))
                    mm(pm[k][:, 0:HEADS * H1], sel[:, place(i, q) + k, :], rows[:, slot(i, q * QUAD + k), 0:HEADS * H1],
                       start=True, stop=True).then_inc(mm_done, 1)

            heads_turned(0)
            turn_quad(0, 0, 0)
            ends_turned(0)
            own_attention(0, 0, own_places(0, 0))
            carries_turned(0)
            maxima_turned(0)
            for q in range(1, NQ):
                turn_quad(0, 0, q)
                own_attention(0, q, own_places(0, q))

            def body(turn, i, more):
                b = block_of(turn, i)
                n, ni = b + 1, (i + 1) % PERIOD
                if more:
                    heads_turned(n)
                factor(b, i)
                sums(b, i, 0)
                if more:
                    turn_quad(n, ni, 0)
                    ends_turned(n)
                sums(b, i, 1)
                if more:
                    own_attention(n, 0, own_places(n, 0))
                    carries_turned(n)
                    turn_quad(n, ni, 1)
                sums(b, i, 2)
                if more:
                    own_attention(n, 1, own_places(n, 1))
                    maxima_turned(n)
                    turn_quad(n, ni, 2)
                sums(b, i, 3)
                if more:
                    own_attention(n, 2, own_places(n, 2))
                    turn_quad(n, ni, 3)
                    own_attention(n, 3, own_places(n, 3))
            blocks(pe, body)

        @block.vector
        def _(dve):
            own = Own(dve, chain)
            tt, scan = dve.tensor_tensor, dve.tensor_tensor_scan
            own.did(dve.memset(th[:, :, :, :], NEG))
            own.did(dve.memset(rv[:, :, :], NEG))
            own.did(dve.memset(minus[:, :], -1.0))
            own.then(dve.memset(uv[:, :, P:P + HEADS], 0.0))
            dve.sem_inc(set_up, 1)
            dve.sem_inc(added, QUAD)
            own.then(dve.memset(K.acc[:, :, :, :], 0.0))

            def hots(n, i, q):
                s, at = n * SEGS + q * QUAD, place(i, q)
                tt(sel[:, at:at + QUAD, :], K.iota[:, :].unsqueeze(1).to_broadcast([P, QUAD, P]),
                   K.edges[:, 1, ds(s, QUAD)].unsqueeze(2).to_broadcast([P, QUAD, P]), ALU.is_equal
                   ).then_inc(sel_ready, 1)

            def local(n):
                dve.wait_ge(fl_loaded, n * 16 + 16)
                own.wait()
                dve.wait_ge(x_turned, n + 1)
                own.then(scan(my[:, :], fl[:, 0:P], px, NEG, ALU.add, ALU.max))
                scan(mx[:, ::-1], fl[:, P:0:-1], my[:, ::-1], NEG, ALU.add, ALU.max).then_inc(local_done, 1)

            def along(n):
                dve.wait_ge(th_loaded, n * 32 + 32)
                own.wait()
                dve.wait_ge(row_kept, n + 1)
                width = HEADS * SLOT
                flat = lambda d: th[0:1, d, :, :].rearrange("a h s -> a (h s)")
                own.did(scan(ro[0:1, 0, 1:width + 1], flat(0), rv[0:1, 0, 0:width], NEG, ALU.add, ALU.max))
                own.then(scan(ro[0:1, 1, 0:width][:, ::-1], flat(1)[:, ::-1], rv[0:1, 1, 0:width][:, ::-1], NEG,
                              ALU.add, ALU.max))
                dve.sem_inc(row_scanned, 1)
                by_head = lambda t: t.rearrange("a (h s) -> a h s", s=SLOT)
                own.did(dve.tensor_copy(by_head(rv[0:1, 0, 0:width])[:, :, 0], by_head(ro[0:1, 0, 1:width + 1])[:, :, SEGS]))

            def whole(n):
                dve.wait_ge(col_done, n + 1)
                own.then(dve.tensor_copy(cc[:, :], pc))
                own.then(scan(my[:, :], fl[:, 0:P], mx[:, :], cc[:, 0:1], ALU.add, ALU.max))
                scan(mx[:, ::-1], fl[:, P:0:-1], my[:, ::-1], cc[:, 1:2], ALU.add, ALU.max).then_inc(m_ready, 1)

            def exponents(n):
                dve.wait_ge(m_turned, n + 1)
                own.wait()
                dve.wait_ge(a2_kept, n + 2)
                flat = a1[:, :, :].rearrange("p s h -> p (s h)")
                first, e = slice(0, HEADS), slice(P, P + HEADS)
                own.did(tt(uv[0:1, 0, e], rc[0:1, 0, 0, :], pmx[0:1, first], ALU.min))
                own.did(tt(uv[:, 0, 0:P], flat, a2[:, :], ALU.add))
                own.did(tt(uv[:, 1, 0:P], pmx, a2[:, :], ALU.add))
                own.did(tt(uv[0:1, 1, e], pmx[0:1, first], a2[0:1, first], ALU.add))
                own.wait(back=3)
                own.then(tt(uv[0:1, 0, e], uv[0:1, 0, e], a2[0:1, first], ALU.add))
                own.then(dve.scalar_tensor_tensor(out=uv[:, :, :], in0=uv[:, :, :], scalar=0.2, in1=uv[:, :, :],
                                                  op0=ALU.mult, op1=ALU.max))
                tt(df[:, :], uv[:, 0, :], uv[:, 1, :], ALU.subtract).then_inc(d_ready, 1)

            def weigh(b, i, q):
                if q == 0:
                    dve.wait_ge(p_ready, b + 1)
                s0 = slot(i, q * QUAD)
                r = rows[:, s0:s0 + QUAD, 0:HEADS * H1].rearrange("p s (h d) -> p s h d", d=H1)
                p = pw[:, q * QUAD * HEADS:(q + 1) * QUAD * HEADS].rearrange("p (s h) -> p s h", h=HEADS)
                tt(r, r, p.unsqueeze(3).to_broadcast([P, QUAD, HEADS, H1]), ALU.mult).then_inc(weighed, 1)

            flat_acc = K.acc[:, :, :, :].rearrange("p w h d -> p (w h d)")
            WIDTH = HEADS * H1

            def places(b, q):
                ws = quad_windows(dve, K, b * NQ + q)
                at = [flat_acc[:, ds(w * WIDTH, WIDTH)] for w in ws]
                counts = [b * SEGS + (q * QUAD + QUAD + k) for k in range(QUAD)]
                for a in at:
                    dve.lower_ap(a)
                for c in counts:
                    dve.compute_val(c)
                return at, counts

            def rescale(b, where):
                at, order = where
                a = at[0].rearrange("p (h d) -> p h d", d=H1)
                dve.wait_ge(f_done, b + 1)
                dve.wait_ge(added, order[0])
                own.then(tt(a, a, pf.unsqueeze(2).to_broadcast([P, HEADS, H1]), ALU.mult))

            def made(where):
                dve.wait_ge(mm_done, where[1][0])

            def add(b, q, where):
                at, order = where
                made(where)
                for k in range(QUAD):
                    dve.wait_ge(added, order[k])
                    tt(at[k], at[k], pm[k][:, 0:WIDTH], ALU.add).then_inc(added, 1)

            PER = 1 + 3 + 2 + 6 + 1
            first = own.k
            hots(0, 0, 0)
            local(0)
            for q in range(1, NQ):
                hots(0, 0, q)
            along(0)
            whole(0)
            hots(1, 1, 0)
            exponents(0)
            assert own.k - first == PER - 1
            start = own.start()

            def body(turn, i, more):
                b = block_of(turn, i)
                n, ni = b + 1, (i + 1) % PERIOD
                own.turn(start, b, PER)
                weigh(b, i, 0)
                if more:
                    local(n)
                weigh(b, i, 1)
                where = places(b, 0)
                rescale(b, where)
                add(b, 0, where)
                if more:
                    along(n)
                    hots(n, ni, 1)
                weigh(b, i, 2)
                where = places(b, 1)
                add(b, 1, where)
                if more:
                    whole(n)
                    hots(n, ni, 2)
                weigh(b, i, 3)
                where = places(b, 2)
                made(where)
                if more:
                    hots(n, ni, 3)
                add(b, 2, where)
                where = places(b, 3)
                add(b, 3, where)
                if more:
                    if not last_but_one(b):
                        hots(b + 2, (i + 2) % PERIOD, 0)
                    exponents(n)
                    assert own.k == PER
            blocks(dve, body)


def attended(nc, K):
    K.x = K.acc[:, :, :, :].rearrange("p w h d -> p w (h d)")[:, :, 0:D]
    with Phase(nc, "elu") as ph:
        xg = [ph.sb(f"xg{i}", [P, GW, D]) for i in range(2)]
        o = ph.sb("o", [P, GW, D])
        m = ph.sb("m", [P, GW, D])
        e = ph.sb("e", [P, GW, D])
        den = ph.sb("den", [P, GW, HEADS])
        st = ph.sb("st", [P, GW, 8])
        loaded = [ph.sem(f"loaded{i}") for i in range(2)]
        chain, low_ready, exped, used, passed = (ph.sem(x) for x in ("chain", "low_ready", "exped", "used", "passed"))
        block = ph.block()

        @block.sync
        def _(sp):
            sp.sem_inc(used, 2)

            def body(g, h):
                sp.wait_ge(used, g + 1)
                sp.dma_start(xg[h][:, :, :], K.xd[slice_rows(g), :].rearrange("(w p) c -> p w c", p=P)
                             ).then_inc(loaded[h], 16)
            over_groups(sp, body)

        @block.vector
        def _(dve):
            own = Own(dve, chain)

            def body(g, h):
                own.turn(0, g, 5 + 2 * GW + 1)
                a = K.acc[:, ds(g * GW, GW), :, :]
                heads = o[:, :, :].rearrange("p w (h d) -> p w h d", d=HD)
                x = K.x[:, ds(g * GW, GW), :]
                own.then(dve.tensor_scalar(den[:, :, :], a[:, :, :, HD], 0.5, None, ALU.max))
                own.then(dve.reciprocal(den[:, :, :], den[:, :, :]))
                own.then(dve.tensor_tensor(heads, a[:, :, :, 0:HD], den[:, :, :].unsqueeze(3).to_broadcast([P, GW, HEADS, HD]),
                                           ALU.mult))
                dve.tensor_scalar(m[:, :, :], o[:, :, :], 0.0, None, ALU.min).then_inc(low_ready, 1)
                dve.wait_ge(exped, g + 1)
                own.then(dve.scalar_tensor_tensor(out=o[:, :, :], in0=o[:, :, :], scalar=0.0, in1=e[:, :, :], op0=ALU.max, op1=ALU.add))
                dve.wait_ge(loaded[h], (g - h) * 8 + 16)
                own.then(dve.scalar_tensor_tensor(out=x, in0=o[:, :, :], scalar=-1.0, in1=xg[h][:, :, :], op0=ALU.add,
                                                  op1=ALU.add))
                dve.sem_inc(used, 1)
                stats_of(dve, own, K, st, x, g * GW, GW, passed)
            over_groups(dve, body)

        @block.scalar
        def _(act):
            def body(g, h):
                act.wait_ge(low_ready, g + 1)
                act.activation(e[:, :, :], m[:, :, :], ACT.Exp).then_inc(exped, 1)
            over_groups(act, body)
    rstd_of(nc, K)


def choose(nc, K, wr, br):
    BITS = 16
    with Phase(nc, "top") as ph:
        xn = [ph.sb(f"xn{i}", [P, GW, D]) for i in range(2)]
        junk = ph.sb("junk", [P, GW, D])
        wrt, brt = ph.sb("wrt", [P, D]), ph.sb("brt", [P, 1])
        dots = ph.sb("dots", [P, GW])
        wv = ph.sb("wv", [P, W])
        kb, sg, half = (ph.sb(x, [P, W], I32) for x in ("kb", "sg", "half"))
        up, low = ph.sb("up", [P, W]), ph.sb("low", [P, W])
        hit, sure, tie, rank, ones = (ph.sb(x, [P, W]) for x in ("hit", "sure", "tie", "rank", "ones"))
        cur, cand, cnt, step, left = (ph.sb(x, [P, 1]) for x in ("cur", "cand", "cnt", "step", "left"))
        lower = ph.sb("lower", [P, P])
        ptot, ptie = ph.ps("ptot", [P, 1]), ph.ps("ptie", [P, 2, W])
        loaded, normed, read, chain, counted, total, lower_ready = (
            ph.sem(x) for x in ("loaded", "normed", "read", "chain", "counted", "total", "lower_ready"))
        block = ph.block()
        COUNTS = 2 * BITS + 2

        @block.sync
        def _(sp):
            sp.dma_start(wrt[:, :], wr.rearrange("c a -> a c").to_broadcast([P, D])).then_inc(loaded, 16)
            sp.dma_start(brt[:, :], br.unsqueeze(0).to_broadcast([P, 1])).then_inc(loaded, 16)

        @block.gpsimd
        def _(pool):
            pool.memset(lower[:, :], 1.0).then_inc(lower_ready, 1)
            pool.wait_ge(lower_ready, 1)
            pool.affine_select(out=lower[:, :], in_=lower[:, :], compare_op=ALU.is_gt, fill=0.0, base=0,
                               pattern=[[1, P]], channel_multiplier=-1).then_inc(lower_ready, 1)

        @block.scalar
        def _(act):
            act.sem_inc(read, 2)

            def body(g, h):
                act.wait_ge(read, g + 1)
                normal(act, K, xn[h], g, normed)
            over_groups(act, body)

        @block.tensor
        def _(pe):
            for r in range(COUNTS):
                pe.wait_ge(counted, r + 1)
                nc.tensor.matmul(ptot[:, :], K.ones[:, :], cnt[:, :], start=True, stop=True).then_inc(total, 1)
            pe.wait_ge(counted, COUNTS + 1)
            pe.wait_ge(lower_ready, 2)
            nc.tensor.matmul(ptie[:, 0, :], lower[:, :], tie[:, :], start=True, stop=True)
            nc.tensor.matmul(ptie[:, 1, :], K.ones[:, :], tie[:, :], start=True, stop=True).then_inc(total, 1)

        @block.vector
        def _(dve):
            own = Own(dve, chain)
            ts, tt = dve.tensor_scalar, dve.tensor_tensor
            dve.wait_ge(loaded, 32)
            start = own.start()

            def body(g, h):
                own.turn(start, g, GW + 1)
                dve.wait_ge(normed, g + 1)
                for i in range(GW):
                    own.did(dve.scalar_tensor_tensor(out=junk[:, i, :], in0=xn[h][:, i, :], scalar=1.0, in1=wrt[:, :],
                                                     op0=ALU.mult, op1=ALU.mult, accum_out=dots[:, i:i + 1]))
                own.wait()
                dve.sem_inc(read, 1)
                own.then(ts(wv[:, ds(g * GW, GW)], dots[:, :], brt[:, 0:1], None, ALU.add))
            over_groups(dve, body)
            own.finish(start + (GROUPS - 1) * (GW + 1), 1, GW + 1)
            bits = wv[:, :].bitcast(I32)
            own.then(ts(sg[:, :], bits, 31, -(1 << 31), ALU.arith_shift_right, ALU.bitwise_or))
            own.then(tt(kb[:, :], bits, sg[:, :], ALU.bitwise_xor))
            own.then(ts(half[:, :], kb[:, :], BITS, None, ALU.logical_shift_right))
            own.then(ts(up[:, :], half[:, :], 1.0, None, ALU.add))
            own.then(ts(half[:, :], kb[:, :], (1 << BITS) - 1, None, ALU.bitwise_and))
            own.then(ts(low[:, :], half[:, :], 1.0, None, ALU.add))
            own.then(tt(up[:, :], up[:, :], K.real[:, :], ALU.mult))
            own.then(ts(up[:, :], up[:, :], -1.0, None, ALU.add))
            own.then(dve.memset(ones[:, :], 1.0))

            def ask(r):
                dve.sem_inc(counted, 1)
                dve.wait_ge(total, r + 1)

            def search(r, of, wanted):
                own.then(dve.memset(cur[:, :], 0.0))
                for b in reversed(range(BITS)):
                    own.then(ts(cand[:, :], cur[:, :], float(1 << b), None, ALU.add))
                    own.then(ts(hit[:, :], of[:, :], cand[:, 0:1], 0.0, ALU.is_ge, ALU.add, accum_out=cnt[:, 0:1]))
                    ask(r)
                    r += 1
                    own.then(ts(step[:, :], ptot[:, :], wanted, float(1 << b), ALU.is_ge, ALU.mult))
                    own.then(tt(cur[:, :], cur[:, :], step[:, :], ALU.add))
                return r

            def left_over(r):
                own.then(dve.tensor_reduce(cnt[:, :], sure[:, :], AX.X, ALU.add))
                ask(r)
                own.then(ts(left[:, :], ptot[:, :], -1.0, float(TOP), ALU.mult, ALU.add))
                return r + 1

            r = search(0, up, float(TOP))
            own.then(ts(sure[:, :], up[:, :], cur[:, 0:1], None, ALU.is_gt))
            r = left_over(r)
            own.then(ts(tie[:, :], up[:, :], cur[:, 0:1], None, ALU.is_equal))
            own.then(tt(low[:, :], low[:, :], tie[:, :], ALU.mult))
            own.then(ts(low[:, :], low[:, :], -1.0, None, ALU.add))
            r = search(r, low, left[:, 0:1])
            own.then(ts(hit[:, :], low[:, :], cur[:, 0:1], None, ALU.is_gt))
            own.then(tt(sure[:, :], sure[:, :], hit[:, :], ALU.add))
            r = left_over(r)
            assert r == COUNTS
            own.then(ts(tie[:, :], low[:, :], cur[:, 0:1], None, ALU.is_equal))
            ask(r)
            own.then(dve.tensor_copy(hit[:, :], ptie[:, 1, :]))
            own.then(dve.tensor_tensor_scan(rank[:, :], ones[:, :], hit[:, :], 0.0, ALU.mult, ALU.add))
            own.then(tt(rank[:, :], rank[:, :], hit[:, :], ALU.subtract))
            own.then(tt(rank[:, :], rank[:, :], ptie[:, 0, :], ALU.add))
            own.then(ts(rank[:, :], rank[:, :], left[:, 0:1], None, ALU.is_lt))
            own.then(tt(tie[:, :], tie[:, :], rank[:, :], ALU.mult))
            own.then(tt(sure[:, :], sure[:, :], tie[:, :], ALU.add))
            dve.tensor_tensor(K.sw[:, :], wv[:, :], sure[:, :], ALU.mult)


def feed_forward(nc, K, w1, b1, w2, b2, out):
    M = HID // P
    RING = 4
    last = lambda g: isinstance(g, int) and g == GROUPS - 1
    with Phase(nc, "ffn") as ph:
        w1t, b1t = ph.sb("w1t", [P, 2, HID]), ph.sb("b1t", [P, M])
        w2t, b2t = ph.sb("w2t", [P, M, D]), ph.sb("b2t", [1, D])
        xn = [ph.sb(f"xn{i}", [P, GW, D]) for i in range(2)]
        xt = [ph.sb(f"xt{i}", [P, 2, GW * P]) for i in range(2)]
        h1 = ph.sb("h1", [P, M, GW * P])
        y = [ph.sb(f"y{i}", [P, GW, D]) for i in range(2)]
        ring = [ph.ps(f"ring{i}", [P, GW * P]) for i in range(RING)]
        px = ph.ps("px", [P, 2, GW * P])
        py = ph.ps("py", [P, GW, D])
        loaded, normed, turned, xt_kept, h_done, h_kept, y_done, y_used, y_ready, chain = (
            ph.sem(x) for x in ("loaded", "normed", "turned", "xt_kept", "h_done", "h_kept", "y_done", "y_used",
                                "y_ready", "chain"))
        stored = [ph.sem(f"stored{i}") for i in range(2)]
        block = ph.block()

        @block.sync
        def _(sp):
            sp.dma_start(w1t[:, :, :], w1.rearrange("(k p) c -> p k c", p=P)).then_inc(loaded, 16)
            sp.dma_start(b1t[:, :], b1.rearrange("(m p) -> p m", p=P)).then_inc(loaded, 16)
            sp.dma_start(w2t[:, :, :], w2.rearrange("(k p) c -> p k c", p=P)).then_inc(loaded, 16)
            sp.dma_start(b2t[:, :], b2.unsqueeze(0)).then_inc(loaded, 16)
            for s in stored:
                sp.sem_inc(s, 16)
            with sp.Fori(0, GROUPS // 2) as gg:
                for h in range(2):
                    g = gg * 2 + h
                    sp.wait_ge(y_ready, g + 1)
                    sp.dma_start(out[slice_rows(g), :].rearrange("(w p) c -> p w c", p=P), y[h][:, :, :]
                                 ).then_inc(stored[h], 16)
            sp.wait_ge(y_ready, GROUPS)
            first = (GROUPS - 1) * GW * P
            whole = (N - first) // P
            sp.dma_start(out[first:first + whole * P, :].rearrange("(w p) c -> p w c", p=P), y[0][:, 0:whole, :]
                         ).then_inc(stored[0], 16)
            rest = N - first - whole * P
            sp.dma_start(out[N - rest:N, :], y[0][0:rest, whole, :]).then_inc(stored[0], 16)
            sp.wait_ge(stored[0], 16 * (GROUPS // 2 + 3))
            sp.wait_ge(stored[1], 16 * (GROUPS // 2 + 1))

        @block.scalar
        def _(act):
            act.sem_inc(h_kept, RING)
            act.wait_ge(loaded, 64)
            normal(act, K, xn[0], 0, normed)

            def body(g, h):
                if not last(g):
                    act.wait_ge(y_used, g + 1)
                    normal(act, K, xn[1 - h], g + 1, normed)
                for m in range(M):
                    act.wait_ge(h_done, g * M + m + 1)
                    act.activation(h1[:, m, :], ring[m % RING][:, :], ACT.Gelu_apprx_tanh, bias=b1t[:, m:m + 1]
                                   ).then_inc(h_kept, 1)
            over_groups(act, body)

        @block.tensor
        def _(pe):
            pe.wait_ge(loaded, 64)
            pe.wait_ge(normed, 1)
            turn_rows(nc, K, xn[0], px, turned)

            def body(g, h):
                pe.wait_ge(xt_kept, g + 1)
                for m in range(M):
                    pe.wait_ge(h_kept, g * M + m + 1)
                    for k in range(2):
                        ins = nc.tensor.matmul(ring[m % RING][:, :], w1t[:, k, m * P:(m + 1) * P], xt[h][:, k, :],
                                               start=(k == 0), stop=(k == 1))
                    ins.then_inc(h_done, 1)
                if not last(g):
                    pe.wait_ge(normed, g + 2)
                    turn_rows(nc, K, xn[1 - h], px, turned)
                pe.wait_ge(y_used, g + 1)
                pe.wait_ge(h_kept, g * M + RING + M)
                for i in range(GW):
                    nc.tensor.matmul(py[:, i, :], K.ones[0:1, :], b2t[:, :], start=True, stop=False)
                    for m in range(M):
                        ins = nc.tensor.matmul(py[:, i, :], h1[:, m, i * P:(i + 1) * P], w2t[:, m, :],
                                               start=False, stop=(m == M - 1))
                ins.then_inc(y_done, 1)
            over_groups(pe, body)

        @block.vector
        def _(dve):
            own = Own(dve, chain)

            def columns(g, h):
                dve.wait_ge(turned, g + 1)
                dve.tensor_copy(xt[h][:, :, :], px[:, :, :]).then_inc(xt_kept, 1)

            dve.sem_inc(y_used, 1)
            columns(0, 0)

            def body(g, h):
                own.turn(0, g, GW)
                if not last(g):
                    columns(g + 1, 1 - h)
                dve.wait_ge(y_done, g + 1)
                dve.wait_ge(stored[h], (g - h) * 8 + 16)
                for i in range(GW):
                    own.did(dve.scalar_tensor_tensor(out=y[h][:, i, :], in0=py[:, i, :],
                                                     scalar=K.sw[:, ds(g * GW + i, 1)], in1=xn[h][:, i, :],
                                                     op0=ALU.mult, op1=ALU.add))
                own.wait()
                dve.sem_inc(y_used, 1)
                dve.tensor_tensor(y[h][:, :, :], y[h][:, :, :], K.x[:, ds(g * GW, GW), :], ALU.add
                                  ).then_inc(y_ready, 1)
            over_groups(dve, body)


class Kept:
    pass


def build(nc, a, out, until=None, dump=None):
    K = Kept()
    with ExitStack() as stack:
        stack.enter_context(nc.allow_non_contiguous_dma(reason="biases over partitions, a few hundred elements"))

        def sb(name, shape, dt=F32):
            return stack.enter_context(nc.sbuf_tensor(name, shape, dt))

        def dram(name, shape, dt=F32):
            return nc.dram_tensor(name, shape, dt, kind="Internal").ap()

        K.etd = dram("edge_tiles", [TB * P, 3 * P])
        K.keyd = dram("keys", [P + SP * P + P])
        K.t1 = dram("table1", [NP, CH1])
        K.t2 = dram("table2", [NP, CH2])
        K.xd = dram("x_spilled", [NP, D])
        K.ftd = dram("ft_rows", [NP, RW])
        K.fld = dram("flags", [SP, P + 2], BF16)
        K.thd = dram("crossings", [2, SP])
        K.ident, K.ones, K.iota = sb("ident", [P, P]), sb("ones", [P, P]), sb("iota", [P, P])
        K.onesb, K.iotab = sb("onesb", [P, P], BF16), sb("iotab", [P, P], BF16)
        K.real = sb("real", [P, W])
        K.sw = sb("sw", [P, W])
        K.iotaw = K.iota[:, 0:W]
        K.edges = sb("edges", [P, 2, SP])
        K.wpack = sb("wpack", [1, SP // QUAD], I32)
        K.wcol = sb("wcol", [P, SB])
        K.dis = sb("dis", [P, W])
        K.a2 = sb("a2", [P, W, HEADS])
        K.mv, K.rs, K.nmr = sb("mv", [P, W, 2]), sb("rs", [P, W]), sb("nmr", [P, W])
        constants(nc, K)
        with ExitStack() as stack2:
            K.ew = stack2.enter_context(nc.sbuf_tensor("edge_w", [P, SP], F32))
            schedule(nc, K, a["src"], a["dst"], a["edge_weight"])
            segment_flags(nc, K)
            degrees(nc, K)
            K.x = stack2.enter_context(nc.sbuf_tensor("x_rows", [P, W, D], F32))
            load_x(nc, K, a["x"])
            K.acc2 = stack2.enter_context(nc.sbuf_tensor("acc2", [P, W, CH2], F32))
            with nc.sbuf_tensor("acc1", [P, W, CH1], F32) as acc1:
                K.acc1 = acc1
                first_table(nc, K, a["L0_gnn_W1"])
                graph_sum(nc, K, "conv1", K.t1, K.acc1, CH1)
                if until == "conv1":
                    return dump(nc, K)
                second_table(nc, K, a["L0_gnn_b1"], a["L0_gnn_W2"])
            graph_sum(nc, K, "conv2", K.t2, K.acc2, CH2)
            if until == "conv2":
                return dump(nc, K)
            decode(nc, K, a["L0_gnn_b2"], a["L0_gnn_Wd1"], a["L0_gnn_bd1"], a["L0_gnn_Wd2"], a["L0_gnn_bd2"])
            if until == "x1":
                return dump(nc, K)
            mixture(nc, K, a)
            if until == "x2":
                return dump(nc, K)
            project(nc, K, a["L1_gnn_W"], a["L1_gnn_attn_l"], a["L1_gnn_attn_r"])
            if until == "proj":
                return dump(nc, K)
        with nc.sbuf_tensor("sums", [P, W, HEADS, HD + 1], F32) as acc:
            K.acc = acc
            attention(nc, K)
            if until == "att":
                return dump(nc, K)
            attended(nc, K)
            if until == "x3":
                return dump(nc, K)
            choose(nc, K, a["L1_ffn_wr"], a["L1_ffn_br"])
            if until == "sw":
                return dump(nc, K)
            feed_forward(nc, K, a["L1_ffn_w1"], a["L1_ffn_b1"], a["L1_ffn_w2"], a["L1_ffn_b2"], out)


def kernel(**inputs):
    import concourse.bacc as bacc
    from concourse.bass_utils import run_bass_kernel_spmd

    nc = bacc.Bacc("TRN2", target_bir_lowering=False, num_devices=1)
    arrays = {name: np.ascontiguousarray(inputs[name]) for name in inputs if name != "L1_ffn_attention_mask"}
    aps = {name: nc.dram_tensor(name, v.shape, mybir.dt.from_np(v.dtype), kind="ExternalInput").ap()
           for name, v in arrays.items()}
    out = nc.dram_tensor("out", (N, D), F32, kind="ExternalOutput").ap()
    build(nc, aps, out)
    return run_bass_kernel_spmd(nc, [arrays], core_ids=[0]).results[0]["out"]
```
